# Optimizing a Trainium2 kernel written in Bass

```python
import numpy as np
import jax
import jax.numpy as jnp

def _softmax(x, axis=-1):
    return jax.nn.softmax(x, axis=axis)

def _gelu(x):
    return jax.nn.gelu(x, approximate=True)

def _silu(x):
    return jax.nn.silu(x)

def _sigmoid(x):
    return jax.nn.sigmoid(x)

def _layernorm(x, axis=-1, eps=1e-05):
    m = jnp.mean(x, axis=axis, keepdims=True)
    v = jnp.var(x, axis=axis, keepdims=True)
    return (x - m) / jnp.sqrt(v + eps)

def _scatter_add(tgt, idx, src, axis=0):
    return tgt.at[idx].add(src)

def _segment_sum(src, seg, n):
    return jax.ops.segment_sum(src, seg, n)
kernel_name = 'mk_early_fusion_d1_tok_img1024_r4_2d6fa3'

def setup_inputs(seed: int=0):
    np.random.seed(seed)
    _w = jnp.asarray

    def _rec_inputs():
        import jax
        import jax.numpy as jnp
        _rk = jax.random.key(seed)
        x = -0.00016672 + 0.999947 * jax.random.normal(jax.random.fold_in(_rk, 1), (16, 3, 96, 96), jnp.float32)
        txt = 0.00140885 + 1.4139 * jax.random.normal(jax.random.fold_in(_rk, 2), (16, 77, 256), jnp.float32)
        return (x, txt)
    x, txt = _rec_inputs()

    def _L0_tok_setup():
        import jax, jax.numpy as jnp
        import numpy as np
        B, C, H, W = (64, 3, 96, 96)
        P = 16
        NP = H // P * (W // P)
        PD = C * P * P
        ED = 256
        NCLS = 1

        def _layernorm(x, g, b, eps=1e-05):
            mu = jnp.mean(x, axis=-1, keepdims=True)
            var = jnp.mean(jnp.square(x - mu), axis=-1, keepdims=True)
            return (x - mu) * jax.lax.rsqrt(var + eps) * g + b
        key = jax.random.key(seed)
        ks = jax.random.split(key, 8)
        x = jax.random.normal(ks[0], (B, C, H, W), dtype=jnp.float32)
        ln1_g = jnp.ones((PD,), jnp.float32)
        ln1_b = jnp.zeros((PD,), jnp.float32)
        W_proj = jax.random.normal(ks[1], (PD, ED), jnp.float32) / np.sqrt(PD)
        b_proj = jnp.zeros((ED,), jnp.float32)
        ln2_g = jnp.ones((ED,), jnp.float32)
        ln2_b = jnp.zeros((ED,), jnp.float32)
        cls_token = jax.random.normal(ks[2], (1, NCLS, ED), jnp.float32)
        pos_emb = jax.random.normal(ks[3], (1, NP + NCLS, ED), jnp.float32)
        return {'x': x, 'ln1_g': ln1_g, 'ln1_b': ln1_b, 'W_proj': W_proj, 'b_proj': b_proj, 'ln2_g': ln2_g, 'ln2_b': ln2_b, 'cls_token': cls_token, 'pos_emb': pos_emb}
    _L0_tok_all = _L0_tok_setup()
    _L0_tok_in = {k: v for k, v in _L0_tok_all.items() if k in ('ln1_g', 'ln1_b', 'W_proj', 'b_proj', 'ln2_g', 'ln2_b', 'cls_token', 'pos_emb')}
    del _L0_tok_all

    def _L0_attn_setup():
        import jax, jax.numpy as jnp
        import numpy as np
        from math import sqrt
        N_HEAD = 16
        W_SCALE = 0.02

        def _reference_tuple_inner(x, W_dq, W_uq, W_dkv, W_uk, W_uv, W_o):
            B, T, C = x.shape
            nh = N_HEAD
            hs = C // nh
            n_kvl = W_dkv.shape[0]
            k_eff = (W_dq.T @ W_uq.T @ W_uk).reshape(nh, hs, n_kvl)
            v_eff = jnp.transpose((W_uv.T @ W_o.T).reshape(n_kvl, nh, hs), (1, 0, 2))
            c_kv = x @ W_dkv.T
            q = x @ W_dq.T @ W_uq.T
            q = q.reshape(B, T, nh, hs)
            q_lat = jnp.einsum('bqhd,hdl->bhql', q, k_eff)
            attn = jnp.einsum('bhql,bkl->bhqk', q_lat, c_kv) / sqrt(hs)
            causal = jnp.tril(jnp.ones((T, T), dtype=bool))
            attn = jnp.where(causal[None, None], attn, -jnp.inf)
            attn = jax.nn.softmax(attn, axis=-1)
            y_lat = jnp.einsum('bhqk,bkl->bhql', attn, c_kv)
            y = jnp.einsum('bhql,hld->bqhd', y_lat, v_eff).reshape(B, T, C)
            return (y, c_kv)
        key = jax.random.key(seed)
        ks = jax.random.split(key, 7)
        B, T, C = (2, 512, 256)
        QL, KVL = (128, 128)
        return {'x': jax.random.normal(ks[0], (B, T, C), dtype=jnp.float32), 'W_dq': jax.random.normal(ks[1], (QL, C), dtype=jnp.float32) * W_SCALE, 'W_uq': jax.random.normal(ks[2], (C, QL), dtype=jnp.float32) * W_SCALE, 'W_dkv': jax.random.normal(ks[3], (KVL, C), dtype=jnp.float32) * W_SCALE, 'W_uk': jax.random.normal(ks[4], (C, KVL), dtype=jnp.float32) * W_SCALE, 'W_uv': jax.random.normal(ks[5], (C, KVL), dtype=jnp.float32) * W_SCALE, 'W_o': jax.random.normal(ks[6], (C, C), dtype=jnp.float32) * W_SCALE}
    _L0_attn_all = _L0_attn_setup()
    _L0_attn_in = {k: v for k, v in _L0_attn_all.items() if k in ('W_dq', 'W_uq', 'W_dkv', 'W_uk', 'W_uv', 'W_o')}
    del _L0_attn_all

    def _L0_ffn_setup():
        import jax, jax.numpy as jnp
        import numpy as np
        import math
        GOLDEN_CENTER = 1.0 / math.e
        GOLDEN_LOWER = 0.5 - math.log(4.0 / 3.0)
        GOLDEN_UPPER = 0.5
        B, T, D = (4, 512, 256)
        E = 8
        I = 1024 // (E // 2)

        def _routing_weights(x, Wr, temperature):
            inh = jax.nn.sigmoid(x @ Wr / temperature)
            in_zone = (inh >= GOLDEN_LOWER) & (inh <= GOLDEN_UPPER)
            dist = jnp.abs(inh - GOLDEN_CENTER)
            w = jnp.exp(-dist / 0.1) * in_zone.astype(x.dtype)
            wsum = w.sum(axis=-1, keepdims=True)
            no_expert = wsum < 1e-08
            fb = jnp.exp(-dist / 0.3)
            _, top2 = jax.lax.top_k(fb, 2)
            fb_mask = jax.nn.one_hot(top2, E, dtype=x.dtype).sum(axis=-2)
            fb_w = fb * fb_mask
            fb_w = fb_w / jnp.clip(fb_w.sum(axis=-1, keepdims=True), 1e-08)
            w = jnp.where(no_expert, fb_w, w)
            wsum = w.sum(axis=-1, keepdims=True)
            return w / jnp.clip(wsum, 1e-08)
        key = jax.random.key(seed)
        k = jax.random.split(key, 6)
        s_d = 1.0 / math.sqrt(D)
        s_i = 1.0 / math.sqrt(I)
        return {'x': jax.random.normal(k[0], (B, T, D), jnp.float32), 'Wg': jax.random.normal(k[1], (E, D, I), jnp.float32) * s_d, 'Wu': jax.random.normal(k[2], (E, D, I), jnp.float32) * s_d, 'Wd': jax.random.normal(k[3], (E, I, D), jnp.float32) * s_i, 'Wr': jax.random.normal(k[4], (D, E), jnp.float32) * s_d, 'temperature': jnp.ones((1,), jnp.float32)}
    _L0_ffn_all = _L0_ffn_setup()
    _L0_ffn_in = {k: v for k, v in _L0_ffn_all.items() if k in ('Wg', 'Wu', 'Wd', 'Wr', 'temperature')}
    del _L0_ffn_all
    return {'x': x, 'txt': txt, 'L0_tok_ln1_g': _L0_tok_in['ln1_g'], 'L0_tok_ln1_b': _L0_tok_in['ln1_b'], 'L0_tok_W_proj': _L0_tok_in['W_proj'], 'L0_tok_b_proj': _L0_tok_in['b_proj'], 'L0_tok_ln2_g': _L0_tok_in['ln2_g'], 'L0_tok_ln2_b': _L0_tok_in['ln2_b'], 'L0_tok_cls_token': _L0_tok_in['cls_token'], 'L0_tok_pos_emb': _L0_tok_in['pos_emb'], 'L0_attn_W_dq': _L0_attn_in['W_dq'], 'L0_attn_W_uq': _L0_attn_in['W_uq'], 'L0_attn_W_dkv': _L0_attn_in['W_dkv'], 'L0_attn_W_uk': _L0_attn_in['W_uk'], 'L0_attn_W_uv': _L0_attn_in['W_uv'], 'L0_attn_W_o': _L0_attn_in['W_o'], 'L0_ffn_Wg': _L0_ffn_in['Wg'], 'L0_ffn_Wu': _L0_ffn_in['Wu'], 'L0_ffn_Wd': _L0_ffn_in['Wd'], 'L0_ffn_Wr': _L0_ffn_in['Wr'], 'L0_ffn_temperature': _L0_ffn_in['temperature']}

def reference(x, txt, L0_tok_ln1_g, L0_tok_ln1_b, L0_tok_W_proj, L0_tok_b_proj, L0_tok_ln2_g, L0_tok_ln2_b, L0_tok_cls_token, L0_tok_pos_emb, L0_attn_W_dq, L0_attn_W_uq, L0_attn_W_dkv, L0_attn_W_uk, L0_attn_W_uv, L0_attn_W_o, L0_ffn_Wg, L0_ffn_Wu, L0_ffn_Wd, L0_ffn_Wr, L0_ffn_temperature):
    import jax
    import jax.numpy as jnp

    def _L0_tok_ref(x, ln1_g, ln1_b, W_proj, b_proj, ln2_g, ln2_b, cls_token, pos_emb):
        import jax, jax.numpy as jnp
        import numpy as np
        B, C, H, W = (64, 3, 96, 96)
        P = 16
        NP = H // P * (W // P)
        PD = C * P * P
        ED = 256
        NCLS = 1

        def _layernorm(x, g, b, eps=1e-05):
            mu = jnp.mean(x, axis=-1, keepdims=True)
            var = jnp.mean(jnp.square(x - mu), axis=-1, keepdims=True)
            return (x - mu) * jax.lax.rsqrt(var + eps) * g + b
        b = x.shape[0]
        h, w = (H // P, W // P)
        patches = x.reshape(b, C, h, P, w, P)
        patches = patches.transpose(0, 2, 4, 3, 5, 1).reshape(b, h * w, P * P * C)
        z = _layernorm(patches, ln1_g, ln1_b)
        z = jnp.einsum('bnp,pe->bne', z, W_proj) + b_proj
        z = _layernorm(z, ln2_g, ln2_b)
        cls = jnp.broadcast_to(cls_token, (b, NCLS, ED))
        z = jnp.concatenate([cls, z], axis=1)
        z = z + pos_emb
        return z

    def _L0_attn_ref(x, W_dq, W_uq, W_dkv, W_uk, W_uv, W_o):
        import jax, jax.numpy as jnp
        import numpy as np
        from math import sqrt
        N_HEAD = 16
        W_SCALE = 0.02

        def _reference_tuple_inner(x, W_dq, W_uq, W_dkv, W_uk, W_uv, W_o):
            B, T, C = x.shape
            nh = N_HEAD
            hs = C // nh
            n_kvl = W_dkv.shape[0]
            k_eff = (W_dq.T @ W_uq.T @ W_uk).reshape(nh, hs, n_kvl)
            v_eff = jnp.transpose((W_uv.T @ W_o.T).reshape(n_kvl, nh, hs), (1, 0, 2))
            c_kv = x @ W_dkv.T
            q = x @ W_dq.T @ W_uq.T
            q = q.reshape(B, T, nh, hs)
            q_lat = jnp.einsum('bqhd,hdl->bhql', q, k_eff)
            attn = jnp.einsum('bhql,bkl->bhqk', q_lat, c_kv) / sqrt(hs)
            causal = jnp.tril(jnp.ones((T, T), dtype=bool))
            attn = jnp.where(causal[None, None], attn, -jnp.inf)
            attn = jax.nn.softmax(attn, axis=-1)
            y_lat = jnp.einsum('bhqk,bkl->bhql', attn, c_kv)
            y = jnp.einsum('bhql,hld->bqhd', y_lat, v_eff).reshape(B, T, C)
            return (y, c_kv)
        return _reference_tuple_inner(x, W_dq, W_uq, W_dkv, W_uk, W_uv, W_o)[0]

    def _L0_ffn_ref(x, Wg, Wu, Wd, Wr, temperature):
        import jax, jax.numpy as jnp
        import numpy as np
        import math
        GOLDEN_CENTER = 1.0 / math.e
        GOLDEN_LOWER = 0.5 - math.log(4.0 / 3.0)
        GOLDEN_UPPER = 0.5
        B, T, D = (4, 512, 256)
        E = 8
        I = 1024 // (E // 2)

        def _routing_weights(x, Wr, temperature):
            inh = jax.nn.sigmoid(x @ Wr / temperature)
            in_zone = (inh >= GOLDEN_LOWER) & (inh <= GOLDEN_UPPER)
            dist = jnp.abs(inh - GOLDEN_CENTER)
            w = jnp.exp(-dist / 0.1) * in_zone.astype(x.dtype)
            wsum = w.sum(axis=-1, keepdims=True)
            no_expert = wsum < 1e-08
            fb = jnp.exp(-dist / 0.3)
            _, top2 = jax.lax.top_k(fb, 2)
            fb_mask = jax.nn.one_hot(top2, E, dtype=x.dtype).sum(axis=-2)
            fb_w = fb * fb_mask
            fb_w = fb_w / jnp.clip(fb_w.sum(axis=-1, keepdims=True), 1e-08)
            w = jnp.where(no_expert, fb_w, w)
            wsum = w.sum(axis=-1, keepdims=True)
            return w / jnp.clip(wsum, 1e-08)
        weights = _routing_weights(x, Wr, temperature)
        gate = jnp.einsum('btd,edi->beti', x, Wg)
        up = jnp.einsum('btd,edi->beti', x, Wu)
        h = jax.nn.silu(gate) * up
        e_out = jnp.einsum('beti,eid->betd', h, Wd)
        out = jnp.einsum('bte,betd->btd', weights, e_out)
        return out
    h = _L0_tok_ref(x, L0_tok_ln1_g, L0_tok_ln1_b, L0_tok_W_proj, L0_tok_b_proj, L0_tok_ln2_g, L0_tok_ln2_b, L0_tok_cls_token, L0_tok_pos_emb)
    h = jnp.concatenate([h, txt], axis=1)
    h = h + _L0_attn_ref(_layernorm(h, axis=-1), L0_attn_W_dq, L0_attn_W_uq, L0_attn_W_dkv, L0_attn_W_uk, L0_attn_W_uv, L0_attn_W_o)
    h = h + _L0_ffn_ref(_layernorm(h, axis=-1), L0_ffn_Wg, L0_ffn_Wu, L0_ffn_Wd, L0_ffn_Wr, L0_ffn_temperature)
    return h

_drawn_inputs = setup_inputs


def setup_inputs(seed=0):
    import zlib

    import numpy as np

    out = dict(_drawn_inputs(seed))
    spreads = {'L0_tok_ln1_g': (1.0, 0.2),
     'L0_tok_ln1_b': (0.0, 0.1),
     'L0_tok_b_proj': (0.0, 0.1),
     'L0_tok_ln2_g': (1.0, 0.2),
     'L0_tok_ln2_b': (0.0, 0.1)}
    factors = {'L0_attn_W_dq': 8.0,
     'L0_attn_W_uq': 8.0,
     'L0_attn_W_dkv': 4.199,
     'L0_attn_W_uk': 8.0,
     'L0_attn_W_uv': 3.808,
     'L0_attn_W_o': 4.744}
    for name, (base, spread) in spreads.items():
        noise = np.random.default_rng([zlib.crc32(name.encode()), seed]).standard_normal(out[name].shape)
        drawn = base * np.exp(spread * noise) if base else spread * noise
        out[name] = jnp.asarray(drawn.astype(out[name].dtype))
    for name, factor in factors.items():
        out[name] = (out[name] * factor).astype(out[name].dtype)
    return out
```

```python
from contextlib import ExitStack

import concourse.bass as bass
from concourse import mybir

F32 = mybir.dt.float32
F32R = mybir.dt.float32r
BF16 = mybir.dt.bfloat16
I32 = mybir.dt.int32
ALU = mybir.AluOpType
ACT = mybir.ActivationFunctionType
AX = mybir.AxisListType

NI = 16
NPATCH = 36
NTXT = 77
T = 1 + NPATCH + NTXT
C = 256
KT = C // 128
PD = 768
PT = PD // 128
G = NI // 2
GP = 2 * NPATCH
TG = 2 * T
NC = NI // 4
TC = 4 * T
NH = 16
HS = C // NH
L = 128
NPAIR = NH // 2
NE = 8
EW = 6 * C
EPS = 1e-5
MASKED = -3.0e38
RSQRT_SEED = float(0x5F3759DF)
STACK_DMAS = 48
ROW_DMAS = 8
GOLDEN_CENTER = 0.36787944117144233
GOLDEN_LOWER = 0.5 - 0.28768207245178085
GOLDEN_UPPER = 0.5


def wait(eng, sem, value):
    if isinstance(value, int) and value <= 0:
        return
    eng.wait_ge(sem, value)


def settle(eng, past):
    eng.sem_inc(past, 1)


class Steps:

    def __init__(self, eng, sem, start=0):
        self.eng, self.sem, self.start, self.n = eng, sem, start, 0

    def __call__(self, instruction):
        instruction.then_inc(self.sem, 1)
        self.n += 1

    def join(self):
        self.eng.wait_ge(self.sem, self.start + self.n)

    def then(self, instruction):
        self(instruction)
        self.join()


def three_pass(pe, out, whi, wlo, xhi, xlo, first, last):
    pe.matmul(out, whi, xhi, start=first, stop=False)
    pe.matmul(out, wlo, xhi, start=False, stop=False)
    return pe.matmul(out, whi, xlo, start=False, stop=last)


def build(nc, patches, txt, ln1_g, ln1_b, W_proj, b_proj, ln2_g, ln2_b, cls_token, pos_emb,
          W_dq, W_dqT, W_uqT, W_dkvT, W_uk, W_uv, W_oT, Wg, Wu, Wd, Wr, temperature, out):
    wscratch = nc.dram_tensor("routing_rows", (NI, NE, T), F32, kind="Internal").ap()

    with ExitStack() as ctx:
        def sb(where, name, shape, dt=F32):
            return where.enter_context(nc.sbuf_tensor(name, shape, dt))

        def sem(name):
            return ctx.enter_context(nc.semaphore(name))

        def psum(name, width):
            return ctx.enter_context(nc.psum_tensor(name, [128, width], F32))

        ring = [psum(f"ring{i}", 1024) for i in range(2)]
        trans = psum("trans", 512)
        proj_a = psum("proj_a", 512)
        proj_b = psum("proj_b", 512)
        psY = psum("psY", 512)

        h = sb(ctx, "h", [T, NI, C])
        wh = sb(ctx, "expert_w_hi", [128, NE * EW], F32R)
        ident = sb(ctx, "ident", [128, 128])
        ident_b = sb(ctx, "ident_b", [128, 128], BF16)
        stats = sb(ctx, "stats", [128, 4, 12])
        mv = sb(ctx, "mv", [128, NI, 2])
        rstd = sb(ctx, "rstd", [128, NI])
        offset = sb(ctx, "offset", [128, NI])
        nt = sb(ctx, "newton", [128, 2, NI])

        early = ExitStack()
        praw = sb(early, "praw", [GP, G, PD])
        z = sb(early, "z", [GP, G, C])
        raw3 = sb(early, "raw3", [128, 3 * C])
        raw_dq = sb(early, "raw_dq", [128, C])
        raw_uk = sb(early, "raw_uk", [128, KT, L])
        raw_uv = sb(early, "raw_uv", [128, KT, L])
        raw_o = sb(early, "raw_o", [128, KT, C])
        aT = sb(early, "aT", [128, KT, C])
        early.close()
        wl = sb(ctx, "expert_w_lo", [128, NE * EW], F32R)

        upto_attention = ExitStack()
        stage = [sb(upto_attention, f"stage{b}", [128, EW]) for b in range(2)]
        attw_h = sb(upto_attention, "attw_h", [128, 5 * C], F32R)
        attw_l = sb(upto_attention, "attw_l", [128, 5 * C], F32R)
        causal = sb(upto_attention, "causal", [T, 4, T], BF16)
        causal_t = sb(upto_attention, "causal_t", [T, 4, T], BF16)

        embedding = ExitStack()
        pn = [sb(embedding, f"pn{b}", [GP, PD]) for b in range(2)]
        zs = [sb(embedding, f"zs{b}", [128, PT, GP]) for b in range(2)]
        zT = [sb(embedding, f"zT{b}", [128, PT, GP]) for b in range(2)]
        emb = [sb(embedding, f"emb{b}", [GP, C]) for b in range(2)]
        zn = [sb(embedding, f"zn{b}", [GP, C]) for b in range(2)]
        zg = [sb(embedding, f"zg{b}", [GP, C]) for b in range(2)]
        wproj = sb(embedding, "wproj", [128, PT, C])
        g1 = sb(embedding, "g1", [128, PT])
        b1 = sb(embedding, "b1", [128, PT])
        bproj = sb(embedding, "bproj", [GP, C])
        g2 = sb(embedding, "g2", [GP, C])
        b2 = sb(embedding, "b2", [GP, C])
        pos = sb(embedding, "pos", [GP, C])
        posb = sb(embedding, "posb", [GP, C])
        cls = sb(embedding, "cls", [1, 3, C])
        embedding.close()

        attention = ExitStack()
        xn = sb(attention, "xn", [T, 2, C])
        xh = sb(attention, "xh", [128, KT, TG], F32R)
        xl = sb(attention, "xl", [128, KT, TG], F32R)
        cdh = sb(attention, "cdh", [128, 2, TG], F32R)
        cdl = sb(attention, "cdl", [128, 2, TG], F32R)
        qk = sb(attention, "qk", [128, 8, TG], F32R)
        stacks = [sb(attention, f"stacks{b}", [128, 2, NPAIR, TG], F32R) for b in range(2)]
        vals = [sb(attention, f"vals{b}", [T, 2, NH, HS + 1]) for b in range(2)]
        probs = [sb(attention, f"probs{b}", [T, 2, 4, T]) for b in range(2)]
        mx = sb(attention, "mx", [T, 128])
        mrow = sb(attention, "mrow", [32, 2, T], F32R)
        rden = sb(attention, "rden", [T, 2, NH])
        y = sb(attention, "y", [T, 2, C])
        attention.close()
        upto_attention.close()

        x2n = [sb(ctx, f"x2n{b}", [T, 2, C]) for b in range(2)]
        x2h = sb(ctx, "x2h", [128, KT, NI * T], F32R)
        x2l = sb(ctx, "x2l", [128, KT, NI * T], F32R)
        wr_raw = sb(ctx, "wr_raw", [128, KT, NE])
        wrh = sb(ctx, "wrh", [128, KT, 128], F32R)
        wrl = sb(ctx, "wrl", [128, KT, 128], F32R)
        temp = sb(ctx, "temp", [128, 2])
        lgT = sb(ctx, "lgT", [NE, TC])
        rt = sb(ctx, "rt", [T, 10, NI * NE])
        rs = sb(ctx, "rs", [T, 4, NI])
        descend = sb(ctx, "descend", [T, NI, NE])
        wT = sb(ctx, "wT", [128, T])
        wrow = [sb(ctx, f"wrow{b}", [1, TC]) for b in range(2)]
        wb = [sb(ctx, f"wb{b}", [128, TC]) for b in range(2)]
        sg = [sb(ctx, f"sg{m}", [128, TC]) for m in range(2)]
        wu = [sb(ctx, f"wu{m}", [128, TC]) for m in range(2)]
        hf = [sb(ctx, f"hf{m}", [128, TC]) for m in range(2)]
        hh = [sb(ctx, f"hh{b}", [128, 2, TC], F32R) for b in range(2)]
        hl = [sb(ctx, f"hl{b}", [128, 2, TC], F32R) for b in range(2)]
        oT = sb(ctx, "oT", [128, 2, TC])
        res = sb(ctx, "res", [T, 4, C])

        ones_set = sem("ones_set")
        ident_ready = sem("ident_ready")
        attw_in = sem("attw_in")
        emb_w_in = sem("emb_w_in")
        cls_in = sem("cls_in")
        cls_made = sem("cls_made")
        patch_in = [sem(f"patch_in{i}") for i in range(2)]
        text_in = sem("text_in")
        cls_put = sem("cls_put")
        attw3_hi = sem("attw3_hi")
        aT_ps = sem("aT_ps")
        aT_ready = sem("aT_ready")
        kv_ps = sem("kv_ps")
        attw_hi = sem("attw_hi")
        attw_ready = sem("attw_ready")
        dve_step = sem("dve_step")
        pn_ready = sem("pn_ready")
        pnT_ps = sem("pnT_ps")
        ln1_ready = sem("ln1_ready")
        descend_set = sem("descend_set")
        zs_ready = sem("zs_ready")
        zT_ready = sem("zT_ready")
        emb_ps = sem("emb_ps")
        z_ready = sem("z_ready")
        zn_ready = sem("zn_ready")
        posb_ready = sem("posb_ready")
        zg_ready = sem("zg_ready")
        emb_ready = sem("emb_ready")
        emb_put = [sem(f"emb_put{b}") for b in range(2)]
        h_stat = sem("h_stat")
        ln_ready = sem("ln_ready")
        sp_past = sem("sp_past")
        pool_past = sem("pool_past")
        act_past = sem("act_past")
        tiles_set = sem("tiles_set")
        xn_ready = sem("xn_ready")
        xt_ps = sem("xt_ps")
        xh_ready = sem("xh_ready")
        xl_ready = sem("xl_ready")
        cd_ps = sem("cd_ps")
        cdh_ready = sem("cdh_ready")
        cdl_ready = sem("cdl_ready")
        q_ps = sem("q_ps")
        k_ps = sem("k_ps")
        v_ps = sem("v_ps")
        qkh_ready = sem("qkh_ready")
        qkl_ready = sem("qkl_ready")
        v_ready = sem("v_ready")
        stack_loaded = [sem(f"stack_loaded{b}") for b in range(2)]
        s_ps = sem("s_ps")
        max_done = sem("max_done")
        m_ps = sem("m_ps")
        mh_ready = sem("mh_ready")
        ml_ready = sem("ml_ready")
        rows_loaded = sem("rows_loaded")
        st_ps = sem("st_ps")
        exp_done = sem("exp_done")
        pv_done = sem("pv_done")
        rden_ready = sem("rden_ready")
        y_done = sem("y_done")
        y_added = sem("y_added")
        stage_in = [sem(f"stage_in{b}") for b in range(2)]
        wh_ready = sem("wh_ready")
        wl_ready = sem("wl_ready")
        wr_in = sem("wr_in")
        wr_cleared = sem("wr_cleared")
        wrh_ready = sem("wrh_ready")
        wr_ready = sem("wr_ready")
        ln3_stat = sem("ln3_stat")
        ln3_ready = sem("ln3_ready")
        x2n_ready = sem("x2n_ready")
        x2t_ps = sem("x2t_ps")
        x2h_ready = sem("x2h_ready")
        x2l_ready = sem("x2l_ready")
        lgT_ps = sem("lgT_ps")
        lgT_ready = sem("lgT_ready")
        lg_ps = sem("lg_ps")
        lg_ready = sem("lg_ready")
        route_exp = sem("route_exp")
        dist_ready = sem("dist_ready")
        route_done = sem("route_done")
        wT_ps = sem("wT_ps")
        wT_ready = sem("wT_ready")
        wT_out = sem("wT_out")
        wrow_in = [sem(f"wrow_in{b}") for b in range(2)]
        wb_ready = sem("wb_ready")
        gu_ps = sem("gu_ps")
        sg_ready = sem("sg_ready")
        wu_ready = sem("wu_ready")
        hf_ready = sem("hf_ready")
        hh_ready = sem("hh_ready")
        hl_ready = sem("hl_ready")
        down_done = sem("down_done")
        oT_ready0 = sem("oT_ready0")
        oT_ready1 = sem("oT_ready1")
        o_ps = sem("o_ps")
        res_ready = sem("res_ready")
        out_sent = sem("out_sent")

        def dkv(w, k):
            return w[:, k * L:(k + 1) * L]

        def dq(w, k):
            return w[:, C + k * L:C + (k + 1) * L]

        def uq(w, m):
            return w[:, 2 * C + m * 128:2 * C + (m + 1) * 128]

        def keff(w, m):
            return w[:, 3 * C + m * 128:3 * C + (m + 1) * 128]

        def veff(w):
            return w[:, 4 * C:5 * C]

        def expert_w(w, e, part, k, m):
            at = e * EW + part * KT * C + k * C + m * 128
            return w[:, at:at + 128]

        block = ctx.enter_context(nc.Block())

        def pipeline(eng, proj_a, maxrows, proj_b, scores, values):
            def body(i, last):
                scores(i, 0)
                proj_a(i, 1)
                maxrows(i, 0, False)
                proj_b(i, 1)
                values(i, 0)
                scores(i, 1)
                if not last:
                    proj_a(i + 1, 0)
                maxrows(i, 1, last)
                if not last:
                    proj_b(i + 1, 0)
                values(i, 1)

            proj_a(0, 0)
            proj_b(0, 0)
            with eng.Fori(0, G // 2 - 1) as i:
                body(i, False)
            body(G // 2 - 1, True)

        def nothing(*_):
            return None

        @block.sync
        def _(sp):
            for i in range(2):
                sp.dma_start(praw[:, 4 * i:4 * i + 4, :],
                             patches[4 * i:4 * i + 4].rearrange("g p d -> p g d")).then_inc(patch_in[i], 16)
            for dst, src in ((wproj[:, :, :], W_proj.rearrange("(k p) n -> p k n", p=128)),
                             (g1[:, :], ln1_g),
                             (b1[:, :], ln1_b),
                             (bproj[:, :], b_proj.partition_broadcast(GP)),
                             (g2[:, :], ln2_g.partition_broadcast(GP)),
                             (b2[:, :], ln2_b.partition_broadcast(GP)),
                             (pos[0:NPATCH, :], pos_emb[0, 1:, :]),
                             (pos[NPATCH:GP, :], pos_emb[0, 1:, :])):
                sp.dma_start(dst, src).then_inc(emb_w_in, 16)
            for dst, src in ((raw_dq[:, :], W_dq),
                             (raw_uk[:, :, :], W_uk.rearrange("(k p) n -> p k n", p=128)),
                             (raw_uv[:, :, :], W_uv.rearrange("(k p) n -> p k n", p=128)),
                             (raw_o[:, :, :], W_oT.rearrange("(k p) n -> p k n", p=128)),
                             (raw3[:, 0:C].rearrange("p (k n) -> p k n", k=KT), W_dkvT.rearrange("(k p) n -> p k n", p=128)),
                             (raw3[:, C:2 * C].rearrange("p (k n) -> p k n", k=KT), W_dqT.rearrange("(k p) n -> p k n", p=128)),
                             (raw3[:, 2 * C:3 * C], W_uqT)):
                sp.dma_start(dst, src).then_inc(attw_in, 16)
            sp.dma_start(cls[0:1, 0, :], cls_token[0]).then_inc(cls_in, 16)
            sp.dma_start(cls[0:1, 1, :], pos_emb[0, 0:1, :]).then_inc(cls_in, 16)
            for i in range(4):
                sp.dma_start(h[1 + NPATCH:T, 4 * i:4 * i + 4, :],
                             txt[4 * i:4 * i + 4].rearrange("b t c -> t b c")).then_inc(text_in, 16)
            sp.wait_ge(cls_made, 1)
            sp.dma_start(h[0:1, :, :], cls[0:1, 2:3, :].to_broadcast([1, NI, C])).then_inc(cls_put, 16)

            with sp.Fori(0, G // 2) as i:
                for b in range(2):
                    sp.wait_ge(emb_ready, 2 * i + b + 1)
                    settle(sp, sp_past)
                    for m in range(2):
                        sp.dma_start(h[1:1 + NPATCH, bass.ds(4 * i + 2 * b + m, 1), :],
                                     emb[b][m * NPATCH:(m + 1) * NPATCH, :].unsqueeze(1)
                                     ).then_inc(emb_put[b], 16)

            def load_expert(i, b):
                g = 2 * i + b
                wait(sp, wh_ready, g - 1)
                settle(sp, sp_past)
                wait(sp, wl_ready, g - 1)
                settle(sp, sp_past)
                for part, w in enumerate((Wg, Wu, Wd)):
                    src = w.rearrange("e (k p) n -> p e k n", p=128)[:, bass.ds(g, 1) if not isinstance(g, int) else slice(g, g + 1), :, :]
                    dst = stage[b][:, part * KT * C:(part + 1) * KT * C].rearrange("p (e k n) -> p e k n", e=1, k=KT)
                    sp.dma_start(dst, src).then_inc(stage_in[b], 16)

            def stack(i, b):
                g = 2 * i + b
                sp.wait_ge(qkh_ready, 2 * g + 2)
                settle(sp, sp_past)
                sp.wait_ge(qkl_ready, 2 * g + 2)
                settle(sp, sp_past)
                wait(sp, st_ps, 4 * (g - 1))
                settle(sp, sp_past)
                slots = qk[:, :, :].bitcast(F32).rearrange("p (s m) t -> p s m t", m=2)
                to = stacks[b][:, :, :, :].bitcast(F32).rearrange("p q (m j) t -> p q m j t", j=4)
                for blk in range(8):
                    par, j = blk % 2, blk // 2
                    at = 64 * par
                    source = slots[16 * blk:16 * blk + 16]
                    for copy, which, s in ((0, 0, 0), (0, 1, 2), (1, 0, 0), (1, 1, 3), (2, 0, 1), (2, 1, 2)):
                        sp.dma_start(to[at + 16 * copy:at + 16 * copy + 16, which, :, j, :],
                                     source[:, s, :, :]).then_inc(stack_loaded[b], 16)

            def rows(i, b, last):
                g = 2 * i + b
                sp.wait_ge(mh_ready, g + 1)
                settle(sp, sp_past)
                sp.wait_ge(ml_ready, g + 1)
                settle(sp, sp_past)
                for half in range(2):
                    for par in range(2):
                        for m in range(2):
                            at = 64 * par + 48 + half
                            sp.dma_start(stacks[b][at:at + 1, 0, :, m * T:(m + 1) * T].bitcast(F32),
                                         mrow[m * 16 + par * 8:m * 16 + par * 8 + 8, half, :].bitcast(F32)
                                         ).then_inc(rows_loaded, 16)

            pipeline(sp, load_expert, rows, stack, nothing, nothing)

            sp.wait_ge(y_added, NI)
            sp.wait_ge(wl_ready, NE)
            sp.wait_ge(wh_ready, NE)
            sp.dma_start(wr_raw[:, :, :], Wr.rearrange("(k p) n -> p k n", p=128)).then_inc(wr_in, 16)
            sp.dma_start(temp[:, 0:1], temperature.partition_broadcast(128)).then_inc(wr_in, 16)
            sp.wait_ge(wT_ready, 1)
            sp.dma_start(wscratch.rearrange("i e t -> (i e) t"), wT[:, :]).then_inc(wT_out, 16)
            sp.wait_ge(wT_out, 16)

            with sp.Fori(0, NC) as c:
                for e in range(NE):
                    if e >= 2:
                        sp.wait_ge(wb_ready, NE * c + e - 1)
                        settle(sp, sp_past)
                    else:
                        sp.wait_ge(wb_ready, NE * c)
                        settle(sp, sp_past)
                    sp.dma_start(wrow[e % 2][0:1, :].rearrange("p (i t) -> p i t", t=T),
                                 wscratch.rearrange("(c i) e t -> e c i t", i=4)[e, bass.ds(c, 1), :, :]
                                 ).then_inc(wrow_in[e % 2], 16)
                sp.wait_ge(res_ready, 2 * c + 2)
                settle(sp, sp_past)
                sp.dma_start(out.rearrange("(c i) t n -> t c i n", i=4)[:, bass.ds(c, 1), :, :],
                             res[:, :, :].unsqueeze(1)).then_inc(out_sent, 16)
            sp.wait_ge(out_sent, 16 * NC)

        @block.gpsimd
        def _(pool):
            pool.memset(ident[:, :], 1.0).then_inc(ones_set, 1)
            pool.memset(ident_b[:, :], 1.0).then_inc(ones_set, 1)
            pool.memset(causal[:, :, :], 0.0).then_inc(ones_set, 1)
            pool.memset(causal_t[:, :, :], 0.0).then_inc(ones_set, 1)
            pool.wait_ge(ones_set, 4)
            for t in (ident, ident_b):
                pool.affine_select(out=t[:, :], in_=t[:, :], compare_op=ALU.is_equal, fill=0.0, base=0,
                                   pattern=[[-1, 128]], channel_multiplier=1).then_inc(ident_ready, 1)
            pool.affine_select(out=causal[:, :, :], in_=causal[:, :, :], compare_op=ALU.is_ge, fill=MASKED,
                               base=0, pattern=[[0, 4], [-1, T]], channel_multiplier=1).then_inc(ident_ready, 1)
            pool.affine_select(out=causal_t[:, :, :], in_=causal_t[:, :, :], compare_op=ALU.is_ge, fill=MASKED,
                               base=0, pattern=[[0, 4], [1, T]], channel_multiplier=-1).then_inc(ident_ready, 1)
            pool.wait_ge(attw3_hi, 1)
            pool.tensor_tensor(attw_l[:, 0:3 * C], raw3[:, :], attw_h[:, 0:3 * C].bitcast(F32),
                               ALU.subtract).then_inc(attw_ready, 1)
            pool.wait_ge(emb_w_in, 16 * 8)
            pool.tensor_tensor(posb[:, :], pos[:, :], b2[:, :], ALU.add).then_inc(posb_ready, 1)
            pool.wait_ge(posb_ready, 1)
            with pool.Fori(0, G // 2) as i:
                for b in range(2):
                    pool.wait_ge(zg_ready, 2 * i + b + 1)
                    pool.wait_ge(emb_put[b], 32 * i)
                    pool.tensor_tensor(emb[b][:, :], zg[b][:, :], posb[:, :], ALU.add).then_inc(emb_ready, 1)

            def values(i, b):
                g = 2 * i + b
                pool.wait_ge(wh_ready, g + 1)
                settle(pool, pool_past)
                pool.tensor_tensor(wl[:, bass.ds(g * EW, EW)], stage[b][:, :],
                                   wh[:, bass.ds(g * EW, EW)].bitcast(F32), ALU.subtract).then_inc(wl_ready, 1)
                for m in range(2):
                    pool.wait_ge(y_done, 2 * g + m + 1)
                    settle(pool, pool_past)
                    row = h[:, bass.ds(2 * g + m, 1), :].rearrange("p a c -> p (a c)")
                    pool.tensor_tensor(row, row, y[:, m, :], ALU.add).then_inc(y_added, 1)

            pipeline(pool, nothing, nothing, nothing, nothing, values)

            for e in range(NE):
                pool.memset(descend[:, :, e:e + 1], float(NE - e)).then_inc(descend_set, 1)
            with pool.Fori(0, NC) as c:
                for e in range(NE):
                    n = NE * c + e
                    pool.wait_ge(wrow_in[e % 2], 16 * (4 * c + e // 2 + 1))
                    if e >= 2:
                        pool.wait_ge(wu_ready, 2 * n - 2)
                    else:
                        pool.wait_ge(wu_ready, 2 * NE * c)
                    settle(pool, pool_past)
                    pool.partition_broadcast(wb[e % 2][:, :], wrow[e % 2][0:1, :]).then_inc(wb_ready, 1)
                    for m in range(2):
                        pool.wait_ge(sg_ready, 2 * n + m + 1)
                        pool.wait_ge(wu_ready, 2 * n + m + 1)
                        if e >= 1:
                            pool.wait_ge(hl_ready, 2 * n + m - 1)
                        else:
                            pool.wait_ge(hl_ready, 2 * n)
                        pool.tensor_tensor(hf[m][:, :], sg[m][:, :], wu[m][:, :], ALU.mult).then_inc(hf_ready, 1)

        @block.scalar
        def _(act):
            def norm(dst, src, at):
                w = src.shape[0]
                at = bass.ds(at, 1)
                return act.activation(dst, src[:, at, :].rearrange("p a c -> p (a c)"), ACT.Identity,
                                      scale=rstd[0:w, at], bias=offset[0:w, at])

            act.wait_ge(attw_in, 16 * 7)
            act.copy(attw_h[:, 0:3 * C], raw3[:, :]).then_inc(attw3_hi, 1)
            act.wait_ge(aT_ps, 1)
            act.copy(aT[:, :, :].rearrange("p k n -> p (k n)"), ring[0][:, 0:512]).then_inc(aT_ready, 1)
            act.wait_ge(kv_ps, 1)
            act.copy(attw_h[:, 3 * C:5 * C], ring[0][:, 512:1024]).then_inc(attw_hi, 1)

            act.wait_ge(ln1_ready, 1)
            with act.Fori(0, G // 2) as i:
                for b in range(2):
                    act.wait_ge(pnT_ps, 2 * i)
                    settle(act, act_past)
                    norm(pn[b][:, :], praw, 2 * i + b).then_inc(pn_ready, 1)
            act.wait_ge(ln_ready, 1)

            def hi_x(i, b):
                g = 2 * i + b
                wait(act, xt_ps, g)
                settle(act, act_past)
                for m in range(2):
                    norm(xn[:, m, :], h, 2 * g + m).then_inc(xn_ready, 1)
                act.wait_ge(xt_ps, g + 1)
                wait(act, cd_ps, g)
                act.copy(xh[:, :, :], trans[:, 0:2 * TG].rearrange("p (k t) -> p k t", k=KT)).then_inc(xh_ready, 1)
                act.wait_ge(cd_ps, g + 1)
                wait(act, v_ps, g)
                act.copy(cdh[:, :, :], proj_a[:, 0:2 * TG].rearrange("p (k t) -> p k t", k=2)).then_inc(cdh_ready, 1)

            def hi_rows(i, b, last):
                g = 2 * i + b
                act.wait_ge(m_ps, g + 1)
                wait(act, rows_loaded, 16 * ROW_DMAS * g)
                act.mul(mrow[:, 0, :], trans[0:32, 0:T], -1.0).then_inc(mh_ready, 1)

            def hi_qkv(i, b):
                g = 2 * i + b
                act.wait_ge(q_ps, g + 1)
                wait(act, stack_loaded[1 - b], 16 * STACK_DMAS * (i + b))
                act.mul(qk[:, 0:2, :], proj_b[:, 0:2 * TG].rearrange("p (k t) -> p k t", k=2), HS ** -0.5).then_inc(qkh_ready, 1)
                act.wait_ge(k_ps, g + 1)
                act.copy(qk[:, 4:6, :], proj_a[:, 0:2 * TG].rearrange("p (k t) -> p k t", k=2)).then_inc(qkh_ready, 1)
                act.wait_ge(v_ps, g + 1)
                wait(act, pv_done, 4 * (g - 1))
                act.copy(vals[b][:, :, :, 0:HS], proj_b[0:T, 0:2 * C].rearrange("p (m h d) -> p m h d", m=2, h=NH)).then_inc(v_ready, 1)

            def exps(i, b):
                g = 2 * i + b
                for u in range(4):
                    act.wait_ge(st_ps, 4 * g + u + 1)
                    act.wait_ge(pv_done, 4 * g + max(u - 1, 0))
                    act.activation(probs[u % 2][:, :, :, :].rearrange("k a j q -> k a (j q)"),
                                   ring[u % 2][0:T, :].rearrange("p (a x) -> p a x", a=2)[:, :, 0:4 * T],
                                   ACT.Exp).then_inc(exp_done, 1)
                act.wait_ge(stage_in[b], 48 * (i + 1))
                settle(act, act_past)
                act.copy(wh[:, bass.ds(g * EW, EW)], stage[b][:, :]).then_inc(wh_ready, 1)

            pipeline(act, hi_x, hi_rows, hi_qkv, nothing, exps)

            act.wait_ge(wr_in, 32)
            act.wait_ge(wr_cleared, 2)
            act.copy(wrh[:, :, 0:NE], wr_raw[:, :, :]).then_inc(wrh_ready, 1)
            act.wait_ge(ln3_ready, 1)

            def x2_norm(g, b):
                wait(act, x2t_ps, g - 1)
                settle(act, act_past)
                for m in range(2):
                    norm(x2n[b][:, m, :], h, 2 * g + m).then_inc(x2n_ready, 1)

            def x2_high(g, b):
                act.wait_ge(x2t_ps, g + 1)
                settle(act, act_past)
                act.copy(x2h[:, :, bass.ds(g * TG, TG)],
                         (trans, proj_a)[b][:, 0:2 * TG].rearrange("p (k t) -> p k t", k=KT)).then_inc(x2h_ready, 1)

            x2_norm(0, 0)
            with act.Fori(0, G // 2 - 1) as i:
                x2_norm(2 * i + 1, 1)
                x2_high(2 * i, 0)
                x2_norm(2 * i + 2, 0)
                x2_high(2 * i + 1, 1)
            x2_norm(G - 1, 1)
            x2_high(G - 2, 0)
            x2_high(G - 1, 1)
            for c in range(NC):
                act.wait_ge(lgT_ps, c + 1)
                if c:
                    act.wait_ge(lg_ps, c)
                act.copy(lgT[:, :], proj_b[0:NE, 0:TC]).then_inc(lgT_ready, 1)
            act.wait_ge(lg_ready, 1)
            act.activation(rt[:, 1, :], rt[:, 0, :], ACT.Exp, scale=-1.0).then_inc(route_exp, 1)
            act.wait_ge(dist_ready, 1)
            act.activation(rt[:, 4, :], rt[:, 3, :], ACT.Exp, scale=-1.0 / 0.1).then_inc(route_exp, 1)
            act.activation(rt[:, 5, :], rt[:, 3, :], ACT.Exp, scale=-1.0 / 0.3).then_inc(route_exp, 1)
            act.wait_ge(wT_ps, 1)
            act.copy(wT[:, :], psY[:, 256:256 + T]).then_inc(wT_ready, 1)

            with act.Fori(0, NC) as c:
                for e in range(NE):
                    n = NE * c + e
                    act.wait_ge(hf_ready, 2 * n)
                    for m in range(2):
                        act.wait_ge(gu_ps, 2 * n + m + 1)
                        act.activation(sg[m][:, :], ring[m][:, 0:TC], ACT.Silu).then_inc(sg_ready, 1)
                    act.wait_ge(down_done, n - 1 if e else n)
                    for m in range(2):
                        act.wait_ge(hf_ready, 2 * n + m + 1)
                        act.copy(hh[e % 2][:, m, :], hf[m][:, :]).then_inc(hh_ready, 1)
                act.wait_ge(down_done, NE * c + NE)
                act.wait_ge(o_ps, c)
                act.copy(oT[:, 0, :], trans[:, 0:TC]).then_inc(oT_ready0, 1)

        @block.vector
        def _(dve):
            step = Steps(dve, dve_step)
            dve.sem_inc(z_ready, 1)

            def moments(images, src, width, parts):
                for j, at in enumerate(images):
                    for q in range(parts):
                        step(dve.bn_stats(stats[0:width, j, 6 * q:6 * q + 6], src(j, q)))
                step.join()
                for j, at in enumerate(images):
                    step(dve.bn_aggr(mv[0:width, at, :].rearrange("p a c -> p (a c)") if not isinstance(at, int) else mv[0:width, at, :],
                                     stats[0:width, j, 0:6 * parts]))

            def rsqrt(width, n):
                v, yy, t = nt[0:width, 0, 0:n], rstd[0:width, 0:n], nt[0:width, 1, 0:n]
                step.join()
                step.then(dve.tensor_scalar(v, mv[0:width, 0:n, 1:2].rearrange("p a c -> p (a c)"), EPS, None, ALU.add))
                step.then(dve.tensor_scalar(yy.bitcast(I32), v.bitcast(I32), -0.5, RSQRT_SEED, ALU.mult, ALU.add))
                for _ in range(3):
                    step.then(dve.tensor_tensor(t, yy, yy, ALU.mult))
                    step.then(dve.scalar_tensor_tensor(t, t, -0.5, v, ALU.mult, ALU.mult))
                    step.then(dve.scalar_tensor_tensor(yy, t, 1.5, yy, ALU.add, ALU.mult))
                step.then(dve.scalar_tensor_tensor(offset[0:width, 0:n], mv[0:width, 0:n, 0:1].rearrange("p a c -> p (a c)"),
                                                   -1.0, yy, ALU.mult, ALU.mult))

            dve.wait_ge(cls_in, 32)
            dve.tensor_tensor(cls[0:1, 2, :], cls[0:1, 0, :], cls[0:1, 1, :], ALU.add).then_inc(cls_made, 1)
            for i in range(2):
                dve.wait_ge(patch_in[i], 16)
                if i:
                    step.join()
                moments(range(4 * i, 4 * i + 4),
                        lambda j, q: praw[:, 4 * i + j, q * (PD // 2):(q + 1) * (PD // 2)], GP, 2)
            rsqrt(GP, G)
            dve.sem_inc(ln1_ready, 1)
            dve.wait_ge(attw_hi, 1)
            dve.tensor_tensor(attw_l[:, 3 * C:5 * C], ring[0][:, 512:1024], attw_h[:, 3 * C:5 * C].bitcast(F32),
                              ALU.subtract).then_inc(attw_ready, 1)
            dve.wait_ge(emb_w_in, 16 * 8)

            def patch_affine(g, b):
                dve.wait_ge(pnT_ps, g + 1)
                wait(dve, emb_ps, g - 1)
                dve.tensor_tensor(zs[b][:, :, :], (trans, proj_a)[b][:, 0:PT * GP].rearrange("p (k t) -> p k t", k=PT),
                                  g1[:, :].unsqueeze(2).to_broadcast([128, PT, GP]), ALU.mult).then_inc(zs_ready, 1)
                dve.wait_ge(zs_ready, g + 1)
                dve.tensor_tensor(zT[b][:, :, :], zs[b][:, :, :],
                                  b1[:, :].unsqueeze(2).to_broadcast([128, PT, GP]), ALU.add).then_inc(zT_ready, 1)

            def embedded(g, b):
                dve.wait_ge(emb_ps, g + 1)
                at = slice(g, g + 1) if isinstance(g, int) else bass.ds(g, 1)
                dve.tensor_tensor(z[:, at, :].rearrange("p a c -> p (a c)"), (proj_b, psY)[b][0:GP, 0:C], bproj[:, :],
                                  ALU.add).then_inc(z_ready, 1)

            patch_affine(0, 0)
            with dve.Fori(0, G // 2 - 1) as i:
                patch_affine(2 * i + 1, 1)
                embedded(2 * i, 0)
                patch_affine(2 * i + 2, 0)
                embedded(2 * i + 1, 1)
            patch_affine(G - 1, 1)
            embedded(G - 2, 0)
            embedded(G - 1, 1)
            dve.wait_ge(z_ready, 1 + G)
            for i in range(2):
                step.join()
                moments(range(4 * i, 4 * i + 4), lambda j, q: z[:, 4 * i + j, :], GP, 1)
            rsqrt(GP, G)
            with dve.Fori(0, G // 2) as i:
                for b in range(2):
                    at = bass.ds(2 * i + b, 1)
                    dve.tensor_scalar(zn[b][:, :], z[:, at, :].rearrange("p a c -> p (a c)"),
                                      mv[0:GP, at, 0:1].rearrange("p a c -> p (a c)"), rstd[0:GP, at],
                                      ALU.subtract, ALU.mult).then_inc(zn_ready, 1)
                    dve.wait_ge(zn_ready, 2 * i + b + 1)
                    dve.wait_ge(emb_ready, 2 * i)
                    dve.tensor_tensor(zg[b][:, :], zn[b][:, :], g2[:, :], ALU.mult).then_inc(zg_ready, 1)
            for b in range(2):
                dve.wait_ge(emb_put[b], 32 * (G // 2))
            dve.wait_ge(text_in, 64)
            dve.wait_ge(cls_put, 16)
            for i in range(4):
                step.join()
                moments(range(4 * i, 4 * i + 4), lambda j, q: h[:, 4 * i + j, :], T, 1)
            rsqrt(T, NI)
            for b in range(2):
                for at in (32, 96):
                    dve.memset(stacks[b][at:at + 32, :, :, :].bitcast(F32), 1.0).then_inc(tiles_set, 1)
                dve.memset(vals[b][:, :, :, HS:HS + 1], 1.0).then_inc(tiles_set, 1)
            dve.memset(mx[:, :], 0.0).then_inc(tiles_set, 1)
            dve.wait_ge(tiles_set, 7)
            dve.sem_inc(ln_ready, 1)

            def lo_x(i, b):
                g = 2 * i + b
                dve.wait_ge(xh_ready, g + 1)
                dve.tensor_tensor(xl[:, :, :], trans[:, 0:2 * TG].rearrange("p (k t) -> p k t", k=KT),
                                  xh[:, :, :].bitcast(F32), ALU.subtract).then_inc(xl_ready, 1)
                dve.wait_ge(cdh_ready, g + 1)
                dve.tensor_tensor(cdl[:, :, :], proj_a[:, 0:2 * TG].rearrange("p (k t) -> p k t", k=2),
                                  cdh[:, :, :].bitcast(F32), ALU.subtract).then_inc(cdl_ready, 1)

            def lo_rows(i, b, last):
                g = 2 * i + b
                dve.wait_ge(mh_ready, g + 1)
                dve.scalar_tensor_tensor(mrow[:, 1, :], trans[0:32, 0:T], -1.0, mrow[:, 0, :].bitcast(F32),
                                         ALU.mult, ALU.subtract).then_inc(ml_ready, 1)

            def lo_qk(i, b):
                g = 2 * i + b
                dve.wait_ge(qkh_ready, 2 * g + 1)
                dve.scalar_tensor_tensor(qk[:, 2:4, :], proj_b[:, 0:2 * TG].rearrange("p (k t) -> p k t", k=2), HS ** -0.5,
                                         qk[:, 0:2, :].bitcast(F32), ALU.mult, ALU.subtract).then_inc(qkl_ready, 1)
                dve.wait_ge(qkh_ready, 2 * g + 2)
                dve.tensor_tensor(qk[:, 6:8, :], proj_a[:, 0:2 * TG].rearrange("p (k t) -> p k t", k=2),
                                  qk[:, 4:6, :].bitcast(F32), ALU.subtract).then_inc(qkl_ready, 1)

            def maxima(i, b):
                g = 2 * i + b
                wait(dve, m_ps, g)
                for u in range(4):
                    m, half = u // 2, u % 2
                    dve.wait_ge(s_ps, 4 * g + u + 1)
                    dve.tensor_reduce(
                        mx[:, 16 * m:16 * m + 16].rearrange("p (a j) -> p a j", a=2)[:, :, 4 * half:4 * half + 4],
                        ring[u % 2][0:T, :].rearrange("p (a x) -> p a x", a=2)[:, :, 0:4 * T]
                        .rearrange("p a (j k) -> p a j k", j=4), AX.X, ALU.max).then_inc(max_done, 1)

            def divide(i, b):
                g = 2 * i + b
                dve.wait_ge(y_added, 2 * g)
                for m in range(2):
                    dve.wait_ge(pv_done, 4 * g + 2 * m + 2)
                    heads = psY[0:T, 0:NH * (HS + 1)].rearrange("p (h d) -> p h d", h=NH)
                    dve.reciprocal(rden[:, m, :], heads[:, :, HS:HS + 1].rearrange("p h d -> p (h d)")).then_inc(rden_ready, 1)
                    dve.wait_ge(rden_ready, 2 * g + m + 1)
                    dve.tensor_tensor(y[:, m, :].rearrange("p (h d) -> p h d", h=NH), heads[:, :, 0:HS],
                                      rden[:, m, :].unsqueeze(2).to_broadcast([T, NH, HS]), ALU.mult).then_inc(y_done, 1)

            pipeline(dve, lo_x, lo_rows, lo_qk, maxima, divide)

            dve.wait_ge(y_added, NI)
            for i in range(4):
                step.join()
                moments(range(4 * i, 4 * i + 4), lambda j, q: h[:, 4 * i + j, :], T, 1)
            rsqrt(T, NI)
            dve.sem_inc(ln3_ready, 1)
            dve.memset(wrh[:, :, :].bitcast(F32), 0.0).then_inc(wr_cleared, 1)
            dve.memset(wrl[:, :, :].bitcast(F32), 0.0).then_inc(wr_cleared, 1)
            dve.wait_ge(wr_cleared, 2)
            dve.wait_ge(wrh_ready, 1)
            dve.tensor_tensor(wrl[:, :, 0:NE], wr_raw[:, :, :], wrh[:, :, 0:NE].bitcast(F32), ALU.subtract).then_inc(wr_ready, 1)
            with dve.Fori(0, G // 2) as i:
                for b in range(2):
                    dve.wait_ge(x2h_ready, 2 * i + b + 1)
                    at = bass.ds((2 * i + b) * TG, TG)
                    dve.tensor_tensor(x2l[:, :, at], (trans, proj_a)[b][:, 0:2 * TG].rearrange("p (k t) -> p k t", k=KT),
                                      x2h[:, :, at].bitcast(F32), ALU.subtract).then_inc(x2l_ready, 1)
            step.then(dve.reciprocal(temp[:, 1:2], temp[:, 0:1]))

            def grid(k):
                return rt[:, k, :]

            def by_image(k):
                return rt[:, k, :].rearrange("p (i e) -> p i e", e=NE)

            def spread(k):
                return rs[:, k, :].unsqueeze(2).to_broadcast([T, NI, NE])

            dve.wait_ge(lg_ps, NC)
            dve.tensor_scalar(grid(0), psY[0:T, 0:NI * NE], temp[0:T, 1:2], None, ALU.mult).then_inc(lg_ready, 1)
            dve.wait_ge(route_exp, 1)
            step.then(dve.tensor_scalar(grid(1), grid(1), 1.0, None, ALU.add))
            step.then(dve.reciprocal(grid(2), grid(1)))
            step.then(dve.tensor_scalar(grid(7), grid(2), -GOLDEN_CENTER, None, ALU.add))
            dve.scalar_tensor_tensor(grid(3), grid(7), -1.0, grid(7), ALU.mult, ALU.max).then_inc(dist_ready, 1)
            step.then(dve.tensor_scalar(grid(6), grid(2), GOLDEN_LOWER, None, ALU.is_ge))
            step.then(dve.scalar_tensor_tensor(grid(6), grid(2), GOLDEN_UPPER, grid(6), ALU.is_le, ALU.mult))
            dve.wait_ge(route_exp, 3)
            step.then(dve.tensor_tensor(grid(4), grid(4), grid(6), ALU.mult))
            step.then(dve.tensor_reduce(rs[:, 0, :], by_image(4), AX.X, ALU.add))
            step(dve.tensor_scalar(rs[:, 1, :], rs[:, 0, :], 1e-8, None, ALU.is_lt))
            step(dve.tensor_scalar(rs[:, 2, :], rs[:, 0, :], 1e-8, None, ALU.is_ge))
            dve.wait_ge(descend_set, NE)
            step.then(dve.tensor_copy(grid(7), grid(5)))
            for k in (8, 9):
                step.then(dve.tensor_reduce(rs[:, 3, :], by_image(7), AX.X, ALU.max))
                step.then(dve.tensor_tensor(by_image(k), by_image(7), spread(3), ALU.is_equal))
                step.then(dve.tensor_tensor(by_image(k), by_image(k), descend[:, :, :], ALU.mult))
                step.then(dve.tensor_reduce(rs[:, 3, :], by_image(k), AX.X, ALU.max))
                step.then(dve.tensor_tensor(by_image(k), by_image(k), spread(3), ALU.is_equal))
                step.then(dve.scalar_tensor_tensor(grid(7), grid(k), -4.0, grid(7), ALU.mult, ALU.add))
            step.then(dve.tensor_tensor(grid(8), grid(8), grid(9), ALU.add))
            step.then(dve.tensor_tensor(grid(5), grid(5), grid(8), ALU.mult))

            def normalise(k):
                step.then(dve.tensor_reduce(rs[:, 3, :], by_image(k), AX.X, ALU.add))
                step.then(dve.tensor_scalar(rs[:, 3, :], rs[:, 3, :], 1e-8, None, ALU.max))
                step.then(dve.reciprocal(rs[:, 3, :], rs[:, 3, :]))
                return dve.tensor_tensor(by_image(k), by_image(k), spread(3), ALU.mult)

            step.then(normalise(5))
            step.then(dve.tensor_tensor(by_image(5), by_image(5), spread(1), ALU.mult))
            step.then(dve.tensor_tensor(by_image(4), by_image(4), spread(2), ALU.mult))
            step.then(dve.tensor_tensor(grid(4), grid(4), grid(5), ALU.add))
            normalise(4).then_inc(route_done, 1)

            with dve.Fori(0, NC) as c:
                for e in range(NE):
                    n = NE * c + e
                    dve.wait_ge(wb_ready, n + 1)
                    for m in range(2):
                        dve.wait_ge(gu_ps, 2 * n + m + 1)
                        dve.tensor_tensor(wu[m][:, :], ring[m][:, 512:512 + TC], wb[e % 2][:, :], ALU.mult).then_inc(wu_ready, 1)
                    for m in range(2):
                        dve.wait_ge(hh_ready, 2 * n + m + 1)
                        dve.tensor_tensor(hl[e % 2][:, m, :], hf[m][:, :], hh[e % 2][:, m, :].bitcast(F32),
                                          ALU.subtract).then_inc(hl_ready, 1)
                dve.wait_ge(down_done, NE * c + NE)
                dve.wait_ge(o_ps, c)
                dve.tensor_copy(oT[:, 1, :], proj_a[:, 0:TC]).then_inc(oT_ready1, 1)
                dve.wait_ge(o_ps, c + 1)
                dve.wait_ge(out_sent, 16 * c)
                for half, ps in enumerate((proj_b, psY)):
                    dve.tensor_tensor(res[:, 2 * half:2 * half + 2, :], h[:, bass.ds(4 * c + 2 * half, 2), :],
                                      ps[0:T, :].rearrange("p (i n) -> p i n", i=2), ALU.add).then_inc(res_ready, 1)

        @block.tensor
        def _(pe):
            pe.wait_ge(attw_in, 16 * 7)
            for m in range(KT):
                last = pe.matmul(ring[0][:, m * C:(m + 1) * C], raw3[:, 2 * C + m * 128:2 * C + (m + 1) * 128],
                                 raw_dq[:, :], start=True, stop=True)
            last.then_inc(aT_ps, 1)
            pe.wait_ge(aT_ready, 1)
            for at, w, x in ((512, raw_uk, aT), (512 + C, raw_uv, raw_o)):
                for k in range(KT):
                    last = pe.matmul(ring[0][:, at:at + C], w[:, k, :], x[:, k, :], start=(k == 0), stop=(k == KT - 1))
            last.then_inc(kv_ps, 1)

            pe.wait_ge(ident_ready, 4)
            pe.wait_ge(emb_w_in, 16 * 8)

            def patch_transposes(g, b):
                pe.wait_ge(pn_ready, g + 1)
                wait(pe, zs_ready, g - 1)
                for k in range(PT):
                    last = pe.transpose((trans, proj_a)[b][:, k * GP:(k + 1) * GP], pn[b][:, k * 128:(k + 1) * 128],
                                        ident[0:GP, 0:GP])
                last.then_inc(pnT_ps, 1)

            def embed(g, b):
                pe.wait_ge(zT_ready, g + 1)
                wait(pe, z_ready, g)
                for k in range(PT):
                    last = pe.matmul((proj_b, psY)[b][0:GP, 0:C], zT[b][:, k, :], wproj[:, k, :],
                                     start=(k == 0), stop=(k == PT - 1))
                last.then_inc(emb_ps, 1)

            patch_transposes(0, 0)
            with pe.Fori(0, G // 2 - 1) as i:
                patch_transposes(2 * i + 1, 1)
                embed(2 * i, 0)
                patch_transposes(2 * i + 2, 0)
                embed(2 * i + 1, 1)
            patch_transposes(G - 1, 1)
            embed(G - 2, 0)
            embed(G - 1, 1)

            pe.wait_ge(attw_ready, 2)

            def latents(i, b):
                g = 2 * i + b
                pe.wait_ge(xn_ready, 2 * g + 2)
                wait(pe, ml_ready, g - 1)
                for m in range(2):
                    for k in range(KT):
                        last = pe.transpose(trans[:, k * TG + m * T:k * TG + (m + 1) * T],
                                            xn[:, m, k * 128:(k + 1) * 128], ident[0:T, 0:T])
                last.then_inc(xt_ps, 1)
                pe.wait_ge(xh_ready, g + 1)
                pe.wait_ge(xl_ready, g + 1)
                wait(pe, qkl_ready, 2 * g)
                for j, w in enumerate((dkv, dq)):
                    for k in range(KT):
                        last = three_pass(pe, proj_a[:, j * TG:(j + 1) * TG], w(attw_h, k), w(attw_l, k),
                                          xh[:, k, :], xl[:, k, :], k == 0, k == KT - 1)
                last.then_inc(cd_ps, 1)

            def maximum_rows(i, b, last_group):
                g = 2 * i + b
                pe.wait_ge(max_done, 4 * g + 4)
                if not last_group:
                    pe.wait_ge(xl_ready, g + 2)
                pe.transpose(trans[:, 0:T], mx[:, :], ident[0:T, 0:T]).then_inc(m_ps, 1)

            def heads(i, b):
                g = 2 * i + b
                pe.wait_ge(cdh_ready, g + 1)
                pe.wait_ge(cdl_ready, g + 1)
                wait(pe, v_ready, g)
                for m in range(2):
                    last = three_pass(pe, proj_b[:, m * TG:(m + 1) * TG], uq(attw_h, m), uq(attw_l, m),
                                      cdh[:, 1, :], cdl[:, 1, :], True, True)
                last.then_inc(q_ps, 1)
                for m in range(2):
                    last = three_pass(pe, proj_a[:, m * TG:(m + 1) * TG], keff(attw_h, m), keff(attw_l, m),
                                      cdh[:, 0, :], cdl[:, 0, :], True, True)
                last.then_inc(k_ps, 1)
                pe.wait_ge(qkl_ready, 2 * g + 1)
                for m in range(2):
                    ch, cl = cdh[:, 0, m * T:(m + 1) * T], cdl[:, 0, m * T:(m + 1) * T]
                    o = proj_b[0:T, m * C:(m + 1) * C]
                    pe.matmul(o, ch, veff(attw_h), start=True, stop=False)
                    pe.matmul(o, ch, veff(attw_l), start=False, stop=False)
                    last = pe.matmul(o, cl, veff(attw_h), start=False, stop=True)
                last.then_inc(v_ps, 1)

            def score(u, b, q_first):
                m, half = u // 2, u % 2
                rows = 48 if q_first else 50
                for par in range(2):
                    pe.matmul(ring[u % 2][0:T, par * 512:par * 512 + 4 * T], ident_b[0:T, 0:T],
                              (causal if q_first else causal_t)[:, :, :].rearrange("p j k -> p (j k)"),
                              start=True, stop=False, skip_group_check=True)
                for j in range(4):
                    for par in range(2):
                        q, k = (stacks[b][64 * par:64 * par + rows, s, 4 * half + j, m * T:(m + 1) * T] for s in range(2))
                        o = ring[u % 2][0:T, par * 512 + j * T:par * 512 + (j + 1) * T]
                        w, x = (q, k) if q_first else (k, q)
                        last = pe.matmul(o, w, x, start=False, stop=(j == 3), skip_group_check=True)
                return last

            def scores(i, b):
                g = 2 * i + b
                pe.wait_ge(stack_loaded[b], 16 * STACK_DMAS * (i + 1))
                wait(pe, exp_done, 4 * g)
                for u in range(4):
                    if u >= 2:
                        pe.wait_ge(max_done, 4 * g + u - 1)
                    score(u, b, True).then_inc(s_ps, 1)

            def values(i, b):
                g = 2 * i + b
                pe.wait_ge(rows_loaded, 16 * ROW_DMAS * (g + 1))

                def transposed_scores(u):
                    if u >= 2:
                        pe.wait_ge(exp_done, 4 * g + u - 1)
                    score(u, b, False).then_inc(st_ps, 1)

                def weighted(u):
                    m, half = u // 2, u % 2
                    pe.wait_ge(exp_done, 4 * g + u + 1)
                    if half == 0:
                        pe.wait_ge(y_done, 2 * g + m)
                    for j in range(4):
                        for par in range(2):
                            head = 2 * (4 * half + j) + par
                            last = pe.matmul(psY[0:T, head * (HS + 1):(head + 1) * (HS + 1)], probs[u % 2][:, par, j, :],
                                             vals[b][:, m, head, :], start=True, stop=True)
                    last.then_inc(pv_done, 1)

                pe.wait_ge(v_ready, g + 1)
                transposed_scores(0)
                transposed_scores(1)
                weighted(0)
                transposed_scores(2)
                weighted(1)
                transposed_scores(3)
                weighted(2)
                weighted(3)

            pipeline(pe, latents, maximum_rows, heads, scores, values)

            with pe.Fori(0, G // 2) as i:
                for b in range(2):
                    pe.wait_ge(x2n_ready, 4 * i + 2 * b + 2)
                    pe.wait_ge(x2l_ready, 2 * i)
                    for m in range(2):
                        for k in range(KT):
                            last = pe.transpose((trans, proj_a)[b][:, k * TG + m * T:k * TG + (m + 1) * T],
                                                x2n[b][:, m, k * 128:(k + 1) * 128], ident[0:T, 0:T])
                    last.then_inc(x2t_ps, 1)
            pe.wait_ge(wr_ready, 1)
            pe.wait_ge(x2l_ready, G)
            for c in range(NC):
                if c:
                    pe.wait_ge(lgT_ready, c)
                at = slice(c * TC, (c + 1) * TC)
                for k in range(KT):
                    last = three_pass(pe, proj_b[:, 0:TC], wrh[:, k, :], wrl[:, k, :], x2h[:, k, at], x2l[:, k, at],
                                      k == 0, k == KT - 1)
                last.then_inc(lgT_ps, 1)
                pe.wait_ge(lgT_ready, c + 1)
                for m in range(4):
                    at = (4 * c + m) * NE
                    last = pe.transpose(psY[0:T, at:at + NE], lgT[:, m * T:(m + 1) * T], ident[0:NE, 0:NE])
                last.then_inc(lg_ps, 1)

            def gate_up(c, e):
                n = NE * c + e
                at = slice(c * TC, (c + 1) * TC) if isinstance(c, int) else bass.ds(c * TC, TC)
                for m in range(2):
                    wait(pe, sg_ready, 2 * n + m - 1 if e else 2 * n)
                    wait(pe, wu_ready, 2 * n + m - 1 if e else 2 * n)
                    for part in range(2):
                        for k in range(KT):
                            last = three_pass(pe, ring[m][:, part * 512:part * 512 + TC], expert_w(wh, e, part, k, m),
                                              expert_w(wl, e, part, k, m), x2h[:, k, at], x2l[:, k, at],
                                              k == 0, k == KT - 1)
                    last.then_inc(gu_ps, 1)

            def down(c, e):
                n = NE * c + e
                if e == 0:
                    wait(pe, oT_ready0, c)
                    wait(pe, oT_ready1, c)
                pe.wait_ge(hh_ready, 2 * n + 2)
                pe.wait_ge(hl_ready, 2 * n + 2)
                for m in range(2):
                    for k in range(2):
                        last = three_pass(pe, (trans, proj_a)[m][:, 0:TC], expert_w(wh, e, 2, k, m),
                                          expert_w(wl, e, 2, k, m), hh[e % 2][:, k, :], hl[e % 2][:, k, :],
                                          e == 0 and k == 0, e == NE - 1 and k == 1)
                last.then_inc(down_done, 1)

            def chunk(c, last_chunk):
                for e in range(NE):
                    if e < NE - 1:
                        gate_up(c, e + 1)
                    elif not last_chunk:
                        gate_up(c + 1, 0)
                    down(c, e)
                pe.wait_ge(oT_ready0, c + 1)
                pe.wait_ge(oT_ready1, c + 1)
                wait(pe, res_ready, 2 * c)
                for m in range(4):
                    for k in range(2):
                        last = pe.transpose((proj_b, psY)[m // 2][0:T, (m % 2) * C + k * 128:(m % 2) * C + (k + 1) * 128],
                                            oT[:, k, m * T:(m + 1) * T], ident[:, :])
                last.then_inc(o_ps, 1)

            gate_up(0, 0)
            pe.wait_ge(route_done, 1)
            pe.transpose(psY[:, 256:256 + T], rt[:, 4, :], ident[0:T, 0:T]).then_inc(wT_ps, 1)
            pe.wait_ge(wT_ready, 1)
            with pe.Fori(0, NC - 1) as c:
                chunk(c, False)
            chunk(NC - 1, True)


def kernel(x, txt, L0_tok_ln1_g, L0_tok_ln1_b, L0_tok_W_proj, L0_tok_b_proj, L0_tok_ln2_g, L0_tok_ln2_b,
           L0_tok_cls_token, L0_tok_pos_emb, L0_attn_W_dq, L0_attn_W_uq, L0_attn_W_dkv, L0_attn_W_uk,
           L0_attn_W_uv, L0_attn_W_o, L0_ffn_Wg, L0_ffn_Wu, L0_ffn_Wd, L0_ffn_Wr, L0_ffn_temperature):
    import numpy as np
    import concourse.bacc as bacc
    from concourse.bass_utils import run_bass_kernel_spmd

    patches = np.asarray(x).reshape(NI, 3, 6, 16, 6, 16).transpose(0, 2, 4, 3, 5, 1).reshape(G, GP, PD)
    laid_out = {
        "patches": patches, "txt": txt, "ln1_g": np.asarray(L0_tok_ln1_g).reshape(PT, 128).T, "ln1_b": np.asarray(L0_tok_ln1_b).reshape(PT, 128).T, "W_proj": L0_tok_W_proj,
        "b_proj": L0_tok_b_proj, "ln2_g": L0_tok_ln2_g, "ln2_b": L0_tok_ln2_b, "cls_token": L0_tok_cls_token,
        "pos_emb": L0_tok_pos_emb, "W_dq": L0_attn_W_dq, "W_dqT": np.asarray(L0_attn_W_dq).T,
        "W_uqT": np.asarray(L0_attn_W_uq).T, "W_dkvT": np.asarray(L0_attn_W_dkv).T, "W_uk": L0_attn_W_uk,
        "W_uv": L0_attn_W_uv, "W_oT": np.asarray(L0_attn_W_o).T, "Wg": L0_ffn_Wg, "Wu": L0_ffn_Wu, "Wd": L0_ffn_Wd,
        "Wr": L0_ffn_Wr, "temperature": L0_ffn_temperature,
    }
    nc = bacc.Bacc("TRN2", target_bir_lowering=False, num_devices=1)
    arrays, args = {}, []
    for name, a in laid_out.items():
        a = np.ascontiguousarray(a)
        arrays[f"in_{name}"] = a
        args.append(nc.dram_tensor(f"in_{name}", a.shape, mybir.dt.from_np(a.dtype), kind="ExternalInput").ap())
    out = nc.dram_tensor("out_tokens", (NI, T, C), F32, kind="ExternalOutput").ap()
    build(nc, *args, out)
    ran = run_bass_kernel_spmd(nc, [arrays], core_ids=[0])
    return ran.results[0]["out_tokens"]
```

```python
from contextlib import ExitStack

import concourse.bass as bass
from concourse import mybir

F32 = mybir.dt.float32
F32R = mybir.dt.float32r
BF16 = mybir.dt.bfloat16
I32 = mybir.dt.int32
ALU = mybir.AluOpType
ACT = mybir.ActivationFunctionType
AX = mybir.AxisListType

NI = 16
NPATCH = 36
NTXT = 77
T = 1 + NPATCH + NTXT
C = 256
KT = C // 128
PD = 768
PT = PD // 128
G = NI // 2
GP = 2 * NPATCH
TG = 2 * T
NC = NI // 4
TC = 4 * T
NH = 16
HS = C // NH
L = 128
NPAIR = NH // 2
NE = 8
EW = 6 * C
EPS = 1e-5
MASKED = -3.0e38
RSQRT_SEED = float(0x5F3759DF)
REP = 4
AW = 3 * C + 2 * NPAIR * 128
LEAD = 8
GOLDEN_CENTER = 0.36787944117144233
GOLDEN_LOWER = 0.5 - 0.28768207245178085
GOLDEN_UPPER = 0.5


def settle(eng, past):
    eng.sem_inc(past, 1)


class Steps:

    def __init__(self, eng, sem, start=0):
        self.eng, self.sem, self.start, self.n = eng, sem, start, 0

    def __call__(self, instruction):
        instruction.then_inc(self.sem, 1)
        self.n += 1

    def join(self):
        self.eng.wait_ge(self.sem, self.start + self.n)

    def then(self, instruction):
        self(instruction)
        self.join()


def three_pass(pe, out, whi, wlo, xhi, xlo, first, last):
    pe.matmul(out, whi, xhi, start=first, stop=False)
    pe.matmul(out, wlo, xhi, start=False, stop=False)
    return pe.matmul(out, whi, xlo, start=False, stop=last)


def build(nc, patches, txt, by_column, W_proj, by_row, pos_emb, first_token, attn_weights, expert_weights,
          Wr, temperature, out):
    wscratch = nc.dram_tensor("routing_rows", (NI, NE, T), F32, kind="Internal").ap()

    with ExitStack() as ctx:
        def sb(where, name, shape, dt=F32):
            return where.enter_context(nc.sbuf_tensor(name, shape, dt))

        def sem(name):
            return ctx.enter_context(nc.semaphore(name))

        def psum(name, width):
            return ctx.enter_context(nc.psum_tensor(name, [128, width], F32))

        ring = [psum(f"ring{i}", 1024) for i in range(2)]
        trans = psum("trans", 512)
        proj_a = psum("proj_a", 512)
        proj_b = psum("proj_b", 512)
        psY = psum("psY", 512)

        h = sb(ctx, "h", [T, NI, C])
        wh = sb(ctx, "expert_w_hi", [128, NE * EW], F32R)
        ident = sb(ctx, "ident", [128, 128])
        ident_b = sb(ctx, "ident_b", [128, 128], BF16)
        stats = sb(ctx, "stats", [128, 4, 12])
        stats3 = sb(ctx, "stats3", [T, NI, 6])
        mv = sb(ctx, "mv", [128, NI + G, 2])
        rstd = sb(ctx, "rstd", [128, NI + G])
        offset = sb(ctx, "offset", [128, NI + G])
        nt = sb(ctx, "newton", [128, 2, NI + G])

        early = ExitStack()
        praw = sb(early, "praw", [GP, G, PD])
        z = sb(early, "z", [GP, G, C])
        raw = sb(early, "raw", [128, 8 * C])
        aT = sb(early, "aT", [128, KT, C])
        early.close()
        wl = sb(ctx, "expert_w_lo", [128, NE * EW], F32R)

        upto_attention = ExitStack()
        stage = sb(upto_attention, "stage", [128, EW])
        attw_h = sb(upto_attention, "attw_h", [128, AW], F32R)
        attw_l = sb(upto_attention, "attw_l", [128, AW], F32R)
        causal = sb(upto_attention, "causal", [T, 1, T], BF16)
        causal_t = sb(upto_attention, "causal_t", [T, 1, T], BF16)
        column = sb(upto_attention, "column", [128, 2 * PT + 6])
        pick = sb(upto_attention, "pick", [128, 4, T], F32R)

        embedding = ExitStack()
        pn = [sb(embedding, f"pn{b}", [GP, PD]) for b in range(4)]
        zs = [sb(embedding, f"zs{b}", [128, PT, GP]) for b in range(2)]
        zT = [sb(embedding, f"zT{b}", [128, PT, GP]) for b in range(2)]
        wproj = sb(embedding, "wproj", [128, PT, C])
        cls = sb(embedding, "cls", [1, 3, C])
        pos = sb(embedding, "pos", [GP, C])
        emb = [sb(embedding, f"emb{b}", [GP, C]) for b in range(2)]
        zn = [sb(embedding, f"zn{b}", [GP, C]) for b in range(2)]
        zg = [sb(embedding, f"zg{b}", [GP, C]) for b in range(2)]
        rows = sb(embedding, "rows", [GP, 3, C])
        posb = sb(embedding, "posb", [GP, C])
        embedding.close()

        attention = ExitStack()
        xn = sb(attention, "xn", [T, 2, C])
        xh = sb(attention, "xh", [128, KT, TG], F32R)
        xl = sb(attention, "xl", [128, KT, TG], F32R)
        cdh = sb(attention, "cdh", [128, 2, TG], F32R)
        cdl = sb(attention, "cdl", [128, 2, TG], F32R)
        stacks = [sb(attention, f"stacks{b}", [128, 2, NPAIR, TG], F32R) for b in range(2)]
        probs = [sb(attention, f"probs{b}", [T, 2, 4, T]) for b in range(2)]
        vals = [sb(attention, f"vals{b}", [T, 2, NH, HS + 1]) for b in range(2)]
        mx = sb(attention, "mx", [T, 128])
        mrow = sb(attention, "mrow", [128, T], F32R)
        mdiag = sb(attention, "mdiag", [128, 4, T], F32R)
        rden = sb(attention, "rden", [T, 2, NH])
        y = sb(attention, "y", [T, 2, C])
        attention.close()
        upto_attention.close()

        x2n = [sb(ctx, f"x2n{b}", [T, 2, C]) for b in range(2)]
        x2h = sb(ctx, "x2h", [128, KT, NI * T], F32R)
        x2l = sb(ctx, "x2l", [128, KT, NI * T], F32R)
        wr_raw = sb(ctx, "wr_raw", [128, KT, NE])
        wrh = sb(ctx, "wrh", [128, KT, 128], F32R)
        wrl = sb(ctx, "wrl", [128, KT, 128], F32R)
        temp = sb(ctx, "temp", [128, 2])
        lgT = sb(ctx, "lgT", [NE, TC])
        rt = sb(ctx, "rt", [T, 10, NI * NE])
        rs = sb(ctx, "rs", [T, 4, NI])
        descend = sb(ctx, "descend", [T, NI, NE])
        wT = sb(ctx, "wT", [128, T])
        wrow = [sb(ctx, f"wrow{b}", [1, TC]) for b in range(2)]
        wb = [sb(ctx, f"wb{b}", [128, TC]) for b in range(2)]
        sg = [sb(ctx, f"sg{m}", [128, TC]) for m in range(2)]
        wu = [sb(ctx, f"wu{m}", [128, TC]) for m in range(2)]
        hf = [sb(ctx, f"hf{m}", [128, TC]) for m in range(2)]
        hh = [sb(ctx, f"hh{b}", [128, 2, TC], F32R) for b in range(2)]
        hl = [sb(ctx, f"hl{b}", [128, 2, TC], F32R) for b in range(2)]
        oT = sb(ctx, "oT", [128, 2, TC])
        res = sb(ctx, "res", [T, 4, C])

        ones_set = sem("ones_set")
        ident_ready = sem("ident_ready")
        attw_in = sem("attw_in")
        emb_w_in = sem("emb_w_in")
        cls_in = sem("cls_in")
        cls_made = sem("cls_made")
        patch_in = [sem(f"patch_in{i}") for i in range(2)]
        text_in = sem("text_in")
        cls_put = sem("cls_put")
        attw3_hi = sem("attw3_hi")
        aT_ps = sem("aT_ps")
        aT_ready = sem("aT_ready")
        kv_ps = sem("kv_ps")
        attw_hi = sem("attw_hi")
        attw_ready = sem("attw_ready")
        dve_step = sem("dve_step")
        pn_ready = sem("pn_ready")
        pnT_ps = sem("pnT_ps")
        ln1_ready = sem("ln1_ready")
        ln2_ready = sem("ln2_ready")
        descend_set = sem("descend_set")
        zs_ready = sem("zs_ready")
        zT_ready = sem("zT_ready")
        emb_ps = sem("emb_ps")
        z_ready = sem("z_ready")
        zn_ready = sem("zn_ready")
        posb_ready = sem("posb_ready")
        zg_ready = sem("zg_ready")
        emb_ready = sem("emb_ready")
        emb_put = [sem(f"emb_put{b}") for b in range(2)]
        h_stat = sem("h_stat")
        ln_ready = sem("ln_ready")
        sp_past = sem("sp_past")
        pool_past = sem("pool_past")
        act_past = sem("act_past")
        tiles_set = sem("tiles_set")
        xn_ready = sem("xn_ready")
        xt_ps = sem("xt_ps")
        xh_ready = sem("xh_ready")
        xl_ready = sem("xl_ready")
        cd_ps = sem("cd_ps")
        cdh_ready = sem("cdh_ready")
        cdl_ready = sem("cdl_ready")
        qk_ps = sem("qk_ps")
        v_ps = sem("v_ps")
        qkh_ready = sem("qkh_ready")
        qkl_ready = sem("qkl_ready")
        v_ready = sem("v_ready")
        pick_ready = sem("pick_ready")
        s_ps = sem("s_ps")
        max_done = sem("max_done")
        m_ps = sem("m_ps")
        mh_ready = sem("mh_ready")
        ml_ready = sem("ml_ready")
        mdiag_ready = sem("mdiag_ready")
        st_ps = sem("st_ps")
        exp_done = sem("exp_done")
        pv_done = sem("pv_done")
        rden_ready = sem("rden_ready")
        y_done = sem("y_done")
        y_added = sem("y_added")
        stage_in = sem("stage_in")
        wh_ready = sem("wh_ready")
        wl_ready = sem("wl_ready")
        wr_in = sem("wr_in")
        wr_cleared = sem("wr_cleared")
        wrh_ready = sem("wrh_ready")
        wr_ready = sem("wr_ready")
        stat3_ready = sem("stat3_ready")
        ln3_ready = sem("ln3_ready")
        x2n_ready = [sem(f"x2n_ready{m}") for m in range(2)]
        x2t_ps = sem("x2t_ps")
        x2h_ready = sem("x2h_ready")
        x2l_ready = sem("x2l_ready")
        lgT_ps = sem("lgT_ps")
        lgT_ready = sem("lgT_ready")
        lg_ps = sem("lg_ps")
        lg_ready = sem("lg_ready")
        route_exp = sem("route_exp")
        dist_ready = sem("dist_ready")
        route_done = sem("route_done")
        wT_ps = sem("wT_ps")
        wT_ready = sem("wT_ready")
        wT_out = sem("wT_out")
        wrow_in = [sem(f"wrow_in{b}") for b in range(2)]
        wb_ready = sem("wb_ready")
        gu_ps = sem("gu_ps")
        sg_ready = sem("sg_ready")
        wu_ready = sem("wu_ready")
        hf_ready = sem("hf_ready")
        hh_ready = sem("hh_ready")
        hl_ready = sem("hl_ready")
        down_done = sem("down_done")
        oT_ready0 = sem("oT_ready0")
        oT_ready1 = sem("oT_ready1")
        o_ps = sem("o_ps")
        res_ready = sem("res_ready")
        out_sent = sem("out_sent")

        def dkv(w, k):
            return w[:, k * L:(k + 1) * L]

        def dq(w, k):
            return w[:, C + k * L:C + (k + 1) * L]

        def veff(w):
            return w[:, 2 * C:3 * C]

        def repeated(w, which):
            at = 3 * C + which * NPAIR * 128
            return w[:, at:at + NPAIR * 128].rearrange("p (h r d) -> p h r d", r=REP, d=HS)

        def pair_w(w, which, pair):
            at = 3 * C + (which * NPAIR + pair) * 128
            return w[:, at:at + 128]

        def heads_of(x):
            return x.rearrange("p (h d) -> p h d", d=HS).unsqueeze(2).to_broadcast([128, NH, REP, HS])

        raw_dkvT, raw_dqT, raw_uqT, raw_dq, raw_uk, raw_uv = (raw[:, j * C:(j + 1) * C] for j in range(6))
        raw_o = raw[:, 6 * C:8 * C]

        def expert_w(w, e, part, k, m):
            at = e * EW + part * KT * C + k * C + m * 128
            return w[:, at:at + 128]

        leading = [zs_ready, zg_ready, emb_ps, z_ready, emb_ready, pnT_ps, *emb_put, xt_ps, cd_ps, v_ps, st_ps, pv_done,
                      ml_ready, mdiag_ready, qkl_ready, v_ready, exp_done, y_done, m_ps, y_added, wl_ready, lg_ps, lgT_ready, x2t_ps, x2l_ready,
                      wb_ready, wu_ready, hl_ready, sg_ready, hf_ready, down_done, o_ps, out_sent, oT_ready0,
                      oT_ready1, res_ready]

        block = ctx.enter_context(nc.Block())

        def over_groups(eng, body):
            with eng.Fori(0, G // 2 - 1) as i:
                for b in range(2):
                    body(2 * i + b, b, True, True)
            body(G - 2, 0, True, False)
            body(G - 1, 1, False, False)

        def proj_bank(s):
            return (proj_b, proj_a)[s % 2]

        def stacked(b, s):
            return stacks[b][:, s // 4, 2 * (s % 4):2 * (s % 4) + 2, :]

        @block.sync
        def _(sp):
            for led in leading:
                sp.sem_inc(led, LEAD)
            def patches_in(i):
                sp.dma_start(praw[:, 4 * i:4 * i + 4, :],
                             patches[4 * i:4 * i + 4].rearrange("g p d -> p g d")).then_inc(patch_in[i], 16)

            patches_in(0)
            sp.dma_start(raw[:, :], attn_weights).then_inc(attw_in, 16)
            sp.dma_start(column[:, :], by_column).then_inc(emb_w_in, 16)
            sp.dma_start(wproj[:, :, :], W_proj.rearrange("(k p) n -> p k n", p=128)).then_inc(emb_w_in, 16)
            patches_in(1)
            sp.dma_start(rows[:, :, :].rearrange("p a c -> p (a c)"), by_row.partition_broadcast(GP)).then_inc(emb_w_in, 16)
            sp.dma_start(pos[0:NPATCH, :], pos_emb[0, 1:, :]).then_inc(emb_w_in, 16)
            sp.dma_start(pos[NPATCH:GP, :], pos_emb[0, 1:, :]).then_inc(emb_w_in, 16)
            sp.dma_start(cls[0:1, 0:2, :].rearrange("p a c -> p (a c)"), first_token).then_inc(cls_in, 16)
            for i in range(2):
                sp.dma_start(h[1 + NPATCH:T, 8 * i:8 * i + 8, :],
                             txt[8 * i:8 * i + 8].rearrange("b t c -> t b c")).then_inc(text_in, 16)
            sp.wait_ge(cls_made, 1)
            sp.dma_start(h[0:1, :, :], cls[0:1, 2:3, :].to_broadcast([1, NI, C])).then_inc(cls_put, 16)

            with sp.Fori(0, G // 2) as i:
                for b in range(2):
                    sp.wait_ge(emb_ready, LEAD + 2 * i + b + 1)
                    settle(sp, sp_past)
                    for m in range(2):
                        sp.dma_start(h[1:1 + NPATCH, bass.ds(4 * i + 2 * b + m, 1), :],
                                     emb[b][m * NPATCH:(m + 1) * NPATCH, :].unsqueeze(1)
                                     ).then_inc(emb_put[b], 16)

            with sp.Fori(0, NE) as e:
                sp.wait_ge(wl_ready, LEAD + e)
                settle(sp, sp_past)
                sp.dma_start(stage[:, :].unsqueeze(1), expert_weights[:, bass.ds(e, 1), :]).then_inc(stage_in, 16)

            sp.wait_ge(y_added, LEAD + NI)
            sp.wait_ge(wl_ready, LEAD + NE)
            sp.dma_start(wr_raw[:, :, :], Wr.rearrange("(k p) n -> p k n", p=128)).then_inc(wr_in, 16)
            sp.dma_start(temp[:, 0:1], temperature.partition_broadcast(128)).then_inc(wr_in, 16)
            sp.wait_ge(wT_ready, 1)
            sp.dma_start(wscratch.rearrange("i e t -> (i e) t"), wT[:, :]).then_inc(wT_out, 16)
            sp.wait_ge(wT_out, 16)

            def row_in(c, e):
                sp.wait_ge(wb_ready, LEAD + NE * c + e - 1)
                settle(sp, sp_past)
                at = slice(c, c + 1) if isinstance(c, int) else bass.ds(c, 1)
                sp.dma_start(wrow[e % 2][0:1, :].rearrange("p (i t) -> p i t", t=T),
                             wscratch.rearrange("(c i) e t -> e c i t", i=4)[e, at, :, :]
                             ).then_inc(wrow_in[e % 2], 16)

            def rows_and_results(c, last):
                for e in range(2, NE):
                    row_in(c, e)
                if not last:
                    row_in(c + 1, 0)
                    row_in(c + 1, 1)
                sp.wait_ge(res_ready, LEAD + 2 * c + 2)
                settle(sp, sp_past)
                at = slice(c, c + 1) if isinstance(c, int) else bass.ds(c, 1)
                sp.dma_start(out.rearrange("(c i) t n -> t c i n", i=4)[:, at, :, :],
                             res[:, :, :].unsqueeze(1)).then_inc(out_sent, 16)

            row_in(0, 0)
            row_in(0, 1)
            with sp.Fori(0, NC - 1) as c:
                rows_and_results(c, False)
            rows_and_results(NC - 1, True)
            sp.wait_ge(out_sent, LEAD + 16 * NC)

        @block.gpsimd
        def _(pool):
            pool.memset(ident[:, :], 1.0).then_inc(ones_set, 1)
            pool.memset(ident_b[:, :], 1.0).then_inc(ones_set, 1)
            pool.memset(causal[:, :, :], 0.0).then_inc(ones_set, 1)
            pool.memset(causal_t[:, :, :], 0.0).then_inc(ones_set, 1)
            pool.memset(pick[:, :, :].bitcast(F32), 1.0).then_inc(ones_set, 1)
            pool.wait_ge(ones_set, 5)
            for t in (ident, ident_b):
                pool.affine_select(out=t[:, :], in_=t[:, :], compare_op=ALU.is_equal, fill=0.0, base=0,
                                   pattern=[[-1, 128]], channel_multiplier=1).then_inc(ident_ready, 1)
            pool.affine_select(out=causal[:, :, :], in_=causal[:, :, :], compare_op=ALU.is_ge, fill=MASKED,
                               base=0, pattern=[[0, 1], [-1, T]], channel_multiplier=1).then_inc(ident_ready, 1)
            pool.affine_select(out=causal_t[:, :, :], in_=causal_t[:, :, :], compare_op=ALU.is_ge, fill=MASKED,
                               base=0, pattern=[[0, 1], [1, T]], channel_multiplier=-1).then_inc(ident_ready, 1)
            pool.wait_ge(ident_ready, 4)
            for at in range(0, 128, 32):
                if at:
                    pool.wait_ge(pick_ready, at // 16)
                pool.affine_select(out=pick[at:at + 32, :, :], in_=pick[at:at + 32, :, :], compare_op=ALU.is_ge, fill=0.0, base=0,
                                   pattern=[[-4, 4], [0, T]], channel_multiplier=1).then_inc(pick_ready, 1)
                pool.wait_ge(pick_ready, at // 16 + 1)
                pool.affine_select(out=pick[at:at + 32, :, :], in_=pick[at:at + 32, :, :], compare_op=ALU.is_ge, fill=0.0, base=3,
                                   pattern=[[4, 4], [0, T]], channel_multiplier=-1).then_inc(pick_ready, 1)
            pool.wait_ge(pick_ready, 8)
            pool.wait_ge(attw3_hi, 2)
            pool.tensor_tensor(attw_l[:, 0:2 * C], raw[:, 0:2 * C], attw_h[:, 0:2 * C].bitcast(F32),
                               ALU.subtract).then_inc(attw_ready, 1)
            pool.tensor_tensor(repeated(attw_l, 0), heads_of(raw_uqT), repeated(attw_h, 0).bitcast(F32),
                               ALU.subtract).then_inc(attw_ready, 1)
            pool.wait_ge(emb_w_in, 16 * 5)
            pool.tensor_tensor(posb[:, :], pos[:, :], rows[:, 2, :], ALU.add).then_inc(posb_ready, 1)
            pool.wait_ge(posb_ready, 1)
            with pool.Fori(0, G // 2) as i:
                for b in range(2):
                    g = 2 * i + b
                    pool.wait_ge(zn_ready, g + 1)
                    pool.wait_ge(emb_ready, LEAD + g - 1)
                    pool.tensor_tensor(zg[b][:, :], zn[b][:, :], rows[:, 1, :], ALU.mult).then_inc(zg_ready, 1)
                    pool.wait_ge(zg_ready, LEAD + g + 1)
                    pool.wait_ge(emb_put[b], LEAD + 32 * i)
                    pool.tensor_tensor(emb[b][:, :], zg[b][:, :], posb[:, :], ALU.add).then_inc(emb_ready, 1)

            def group(g, b, ahead, further):
                for m in range(2):
                    pool.wait_ge(y_done, LEAD + 2 * g + m + 1)
                    settle(pool, pool_past)
                    row = h[:, bass.ds(2 * g + m, 1), :].rearrange("p a c -> p (a c)")
                    pool.tensor_tensor(row, row, y[:, m, :], ALU.add).then_inc(y_added, 1)
                pool.wait_ge(wh_ready, g + 1)
                settle(pool, pool_past)
                pool.tensor_tensor(wl[:, bass.ds(g * EW, EW)], stage[:, :],
                                   wh[:, bass.ds(g * EW, EW)].bitcast(F32), ALU.subtract).then_inc(wl_ready, 1)

            over_groups(pool, group)

            pool.wait_ge(y_added, LEAD + NI)
            pool.wait_ge(ln3_ready, 1)
            pool.memset(wrh[:, :, :].bitcast(F32), 0.0).then_inc(wr_cleared, 1)
            pool.memset(wrl[:, :, :].bitcast(F32), 0.0).then_inc(wr_cleared, 1)
            for e in range(NE):
                pool.memset(descend[:, :, e:e + 1], float(NE - e)).then_inc(descend_set, 1)
            with pool.Fori(0, NC) as c:
                for e in range(NE):
                    n = NE * c + e
                    pool.wait_ge(wrow_in[e % 2], 16 * (4 * c + e // 2 + 1))
                    if e >= 2:
                        pool.wait_ge(wu_ready, LEAD + 2 * n - 2)
                    else:
                        pool.wait_ge(wu_ready, LEAD + 2 * NE * c)
                    settle(pool, pool_past)
                    pool.partition_broadcast(wb[e % 2][:, :], wrow[e % 2][0:1, :]).then_inc(wb_ready, 1)
                    for m in range(2):
                        pool.wait_ge(sg_ready, LEAD + 2 * n + m + 1)
                        pool.wait_ge(wu_ready, LEAD + 2 * n + m + 1)
                        if e >= 1:
                            pool.wait_ge(hl_ready, LEAD + 2 * n + m - 1)
                        else:
                            pool.wait_ge(hl_ready, LEAD + 2 * n)
                        pool.tensor_tensor(hf[m][:, :], sg[m][:, :], wu[m][:, :], ALU.mult).then_inc(hf_ready, 1)

        @block.scalar
        def _(act):
            def norm(dst, src, at):
                w = src.shape[0]
                at = bass.ds(at, 1)
                return act.activation(dst, src[:, at, :].rearrange("p a c -> p (a c)"), ACT.Identity,
                                      scale=rstd[0:w, at], bias=offset[0:w, at])

            act.wait_ge(attw_in, 16)
            act.copy(attw_h[:, 0:2 * C], raw[:, 0:2 * C]).then_inc(attw3_hi, 1)
            act.copy(repeated(attw_h, 0), heads_of(raw_uqT)).then_inc(attw3_hi, 1)
            act.wait_ge(aT_ps, 1)
            act.mul(aT[:, :, :].rearrange("p k n -> p (k n)"), ring[0][:, 0:512], HS ** -0.5).then_inc(aT_ready, 1)
            act.wait_ge(kv_ps, 1)
            act.copy(repeated(attw_h, 1), heads_of(ring[0][:, 512:512 + C])).then_inc(attw_hi, 1)
            act.copy(veff(attw_h), ring[0][:, 512 + C:1024]).then_inc(attw_hi, 1)

            for half in range(2):
                act.wait_ge(ln1_ready, half + 1)
                for b in range(4):
                    act.wait_ge(pnT_ps, LEAD + 4 * half + b - 3)
                    norm(pn[b][:, :], praw, 4 * half + b).then_inc(pn_ready, 1)
            for half in range(2):
                act.wait_ge(ln2_ready, half + 1)
                for g in range(4 * half, 4 * half + 4):
                    act.wait_ge(zg_ready, LEAD + g - 1)
                    act.activation(zn[g % 2][:, :], z[:, g, :], ACT.Identity, scale=rstd[0:GP, NI + g:NI + g + 1],
                                   bias=offset[0:GP, NI + g:NI + g + 1]).then_inc(zn_ready, 1)
            act.wait_ge(ln_ready, 1)
            act.wait_ge(pnT_ps, LEAD + G)
            act.wait_ge(emb_ps, LEAD + G)

            def normalised(g):
                act.wait_ge(xt_ps, LEAD + g)
                settle(act, act_past)
                for m in range(2):
                    norm(xn[:, m, :], h, 2 * g + m).then_inc(xn_ready, 1)

            def high_x(g):
                act.wait_ge(xt_ps, LEAD + g + 1)
                act.wait_ge(cd_ps, LEAD + g)
                act.copy(xh[:, :, :], trans[:, 0:2 * TG].rearrange("p (k t) -> p k t", k=KT)).then_inc(xh_ready, 1)

            def high_latents(g):
                act.wait_ge(cd_ps, LEAD + g + 1)
                act.wait_ge(v_ps, LEAD + g)
                act.copy(cdh[:, :, :], proj_a[:, 0:2 * TG].rearrange("p (k t) -> p k t", k=2)).then_inc(cdh_ready, 1)

            def high_qk(g, b, s):
                act.wait_ge(qk_ps, 8 * g + s + 1)
                if s == 0:
                    act.wait_ge(st_ps, LEAD + 4 * (g - 1))
                act.copy(stacked(b, s), proj_bank(s)[:, 0:2 * TG].rearrange("p (k t) -> p k t", k=2)).then_inc(qkh_ready, 1)

            def values_out(g, b):
                act.wait_ge(v_ps, LEAD + g + 1)
                act.wait_ge(pv_done, LEAD + 4 * (g - 1))
                act.copy(vals[b][:, :, :, 0:HS], proj_b[0:T, 0:2 * C].rearrange("p (m h d) -> p m h d", m=2, h=NH)).then_inc(v_ready, 1)

            def high_maxima(g):
                act.wait_ge(m_ps, LEAD + g + 1)
                act.wait_ge(mdiag_ready, LEAD + g)
                act.copy(mrow[:, :], trans[:, 0:T]).then_inc(mh_ready, 1)

            def exponentials(g, u):
                act.wait_ge(st_ps, LEAD + 4 * g + u + 1)
                act.wait_ge(pv_done, LEAD + 4 * g + u - 1)
                act.activation(probs[u % 2][:, :, :, :].rearrange("k a j q -> k a (j q)"),
                               ring[u % 2][0:T, :].rearrange("p (a x) -> p a x", a=2)[:, :, 0:4 * T],
                               ACT.Exp).then_inc(exp_done, 1)

            def group(g, b, ahead, further):
                if ahead:
                    for s in range(1, 5):
                        high_qk(g + 1, 1 - b, s)
                high_maxima(g)
                if ahead:
                    high_qk(g + 1, 1 - b, 5)
                exponentials(g, 0)
                if ahead:
                    high_qk(g + 1, 1 - b, 6)
                exponentials(g, 1)
                if further:
                    normalised(g + 2)
                if ahead:
                    high_qk(g + 1, 1 - b, 7)
                exponentials(g, 2)
                if ahead:
                    values_out(g + 1, 1 - b)
                if further:
                    high_x(g + 2)
                exponentials(g, 3)
                if further:
                    high_latents(g + 2)
                    high_qk(g + 2, b, 0)
                act.wait_ge(stage_in, 16 * (g + 1))
                settle(act, act_past)
                act.copy(wh[:, bass.ds(g * EW, EW)], stage[:, :]).then_inc(wh_ready, 1)

            normalised(0)
            high_x(0)
            high_latents(0)
            normalised(1)
            for s in range(8):
                high_qk(0, 0, s)
            values_out(0, 0)
            high_x(1)
            high_latents(1)
            act.wait_ge(ln_ready, 2)
            high_qk(1, 1, 0)
            over_groups(act, group)

            act.wait_ge(wr_in, 32)
            act.wait_ge(wr_cleared, 2)
            act.copy(wrh[:, :, 0:NE], wr_raw[:, :, :]).then_inc(wrh_ready, 1)
            act.wait_ge(ln3_ready, 1)

            def x2_norm(g, b):
                act.wait_ge(x2t_ps, LEAD + g - 1)
                settle(act, act_past)
                norm(x2n[b][:, 0, :], h, 2 * g).then_inc(x2n_ready[0], 1)

            def x2_high(g, b):
                act.wait_ge(x2t_ps, LEAD + g + 1)
                settle(act, act_past)
                act.copy(x2h[:, :, bass.ds(g * TG, TG)],
                         (trans, proj_a)[b][:, 0:2 * TG].rearrange("p (k t) -> p k t", k=KT)).then_inc(x2h_ready, 1)

            def logits_out(c):
                act.wait_ge(lgT_ps, c + 1)
                act.wait_ge(lg_ps, LEAD + c)
                act.copy(lgT[:, :], proj_b[0:NE, 0:TC]).then_inc(lgT_ready, 1)

            x2_norm(0, 0)
            x2_norm(1, 1)
            with act.Fori(0, NC - 1) as c:
                x2_high(2 * c, 0)
                x2_norm(2 * c + 2, 0)
                x2_high(2 * c + 1, 1)
                x2_norm(2 * c + 3, 1)
                logits_out(c)
            x2_high(G - 2, 0)
            x2_high(G - 1, 1)
            logits_out(NC - 1)
            act.wait_ge(lg_ready, 1)
            act.activation(rt[:, 1, :], rt[:, 0, :], ACT.Exp, scale=-1.0).then_inc(route_exp, 1)
            act.wait_ge(dist_ready, 1)
            act.activation(rt[:, 4, :], rt[:, 3, :], ACT.Exp, scale=-1.0 / 0.1).then_inc(route_exp, 1)
            act.activation(rt[:, 5, :], rt[:, 3, :], ACT.Exp, scale=-1.0 / 0.3).then_inc(route_exp, 1)
            act.wait_ge(wT_ps, 1)
            act.copy(wT[:, :], psY[:, 256:256 + T]).then_inc(wT_ready, 1)

            def gate(c, e):
                n = NE * c + e
                act.wait_ge(hf_ready, LEAD + 2 * n)
                for m in range(2):
                    act.wait_ge(gu_ps, 2 * n + m + 1)
                    act.activation(sg[m][:, :], ring[m][:, 0:TC], ACT.Silu).then_inc(sg_ready, 1)

            def hidden_high(c, e):
                n = NE * c + e
                act.wait_ge(down_done, LEAD + n - 1)
                for m in range(2):
                    act.wait_ge(hf_ready, LEAD + 2 * n + m + 1)
                    act.copy(hh[e % 2][:, m, :], hf[m][:, :]).then_inc(hh_ready, 1)

            def chunk(c, last):
                for e in range(1, NE):
                    gate(c, e)
                    hidden_high(c, e)
                if not last:
                    gate(c + 1, 0)
                act.wait_ge(down_done, LEAD + NE * c + NE)
                act.wait_ge(o_ps, LEAD + c)
                act.copy(oT[:, 0, :], trans[:, 0:TC]).then_inc(oT_ready0, 1)
                if not last:
                    hidden_high(c + 1, 0)

            gate(0, 0)
            hidden_high(0, 0)
            with act.Fori(0, NC - 1) as c:
                chunk(c, False)
            chunk(NC - 1, True)

        @block.vector
        def _(dve):
            step = Steps(dve, dve_step)

            def moments(images, src, width, parts):
                for j, at in enumerate(images):
                    for q in range(parts):
                        step(dve.bn_stats(stats[0:width, j, 6 * q:6 * q + 6], src(j, q)))
                step.join()
                for j, at in enumerate(images):
                    step(dve.bn_aggr(mv[0:width, at, :].rearrange("p a c -> p (a c)") if not isinstance(at, int) else mv[0:width, at, :],
                                     stats[0:width, j, 0:6 * parts]))

            def rsqrt(width, first, n):
                at = slice(first, first + n)
                v, yy, t = nt[0:width, 0, at], rstd[0:width, at], nt[0:width, 1, at]
                step.join()
                step.then(dve.tensor_scalar(v, mv[0:width, at, 1:2].rearrange("p a c -> p (a c)"), EPS, None, ALU.add))
                step.then(dve.tensor_scalar(yy.bitcast(I32), v.bitcast(I32), -0.5, RSQRT_SEED, ALU.mult, ALU.add))
                for _ in range(3):
                    step.then(dve.tensor_tensor(t, yy, yy, ALU.mult))
                    step.then(dve.scalar_tensor_tensor(t, t, -0.5, v, ALU.mult, ALU.mult))
                    step.then(dve.scalar_tensor_tensor(yy, t, 1.5, yy, ALU.add, ALU.mult))
                step.then(dve.scalar_tensor_tensor(offset[0:width, at], mv[0:width, at, 0:1].rearrange("p a c -> p (a c)"),
                                                   -1.0, yy, ALU.mult, ALU.mult))

            def token_moments(first, n):
                for i in range(first, first + n, 4):
                    step.join()
                    moments(range(i, i + 4), lambda j, q: h[:, i + j, :], T, 1)

            for i in range(2):
                dve.wait_ge(patch_in[i], 16)
                if i:
                    step.join()
                moments(range(4 * i, 4 * i + 4),
                        lambda j, q: praw[:, 4 * i + j, q * (PD // 2):(q + 1) * (PD // 2)], GP, 2)
                rsqrt(GP, 4 * i, 4)
                dve.sem_inc(ln1_ready, 1)
            dve.wait_ge(attw_hi, 2)
            dve.tensor_tensor(repeated(attw_l, 1), heads_of(ring[0][:, 512:512 + C]), repeated(attw_h, 1).bitcast(F32),
                              ALU.subtract).then_inc(attw_ready, 1)
            dve.tensor_tensor(veff(attw_l), ring[0][:, 512 + C:1024], veff(attw_h).bitcast(F32),
                              ALU.subtract).then_inc(attw_ready, 1)
            dve.wait_ge(emb_w_in, 16 * 5)
            dve.wait_ge(cls_in, 16)
            dve.tensor_tensor(cls[0:1, 2, :], cls[0:1, 0, :], cls[0:1, 1, :], ALU.add).then_inc(cls_made, 1)

            def patch_affine(g, b):
                dve.wait_ge(pnT_ps, LEAD + g + 1)
                dve.wait_ge(emb_ps, LEAD + g - 1)
                dve.tensor_tensor(zs[b][:, :, :], (trans, proj_a)[b][:, 0:PT * GP].rearrange("p (k t) -> p k t", k=PT),
                                  column[:, 0:PT].unsqueeze(2).to_broadcast([128, PT, GP]), ALU.mult).then_inc(zs_ready, 1)
                dve.wait_ge(zs_ready, LEAD + g + 1)
                dve.tensor_tensor(zT[b][:, :, :], zs[b][:, :, :],
                                  column[:, PT:2 * PT].unsqueeze(2).to_broadcast([128, PT, GP]), ALU.add).then_inc(zT_ready, 1)

            def embedded(g, b):
                dve.wait_ge(emb_ps, LEAD + g + 1)
                at = slice(g, g + 1) if isinstance(g, int) else bass.ds(g, 1)
                dve.tensor_tensor(z[:, at, :].rearrange("p a c -> p (a c)"), (proj_b, psY)[b][0:GP, 0:C], rows[:, 0, :],
                                  ALU.add).then_inc(z_ready, 1)

            def second_norm(half):
                dve.wait_ge(z_ready, LEAD + 4 * half + 4)
                step.join()
                moments(range(NI + 4 * half, NI + 4 * half + 4), lambda j, q: z[:, 4 * half + j, :], GP, 1)
                rsqrt(GP, NI + 4 * half, 4)
                dve.sem_inc(ln2_ready, 1)

            for half in range(2):
                patch_affine(4 * half, 0)
                for g in range(4 * half + 1, 4 * half + 4):
                    patch_affine(g, g % 2)
                    if g == 5:
                        second_norm(0)
                    embedded(g - 1, (g - 1) % 2)
                if half == 0:
                    embedded(3, 1)
            embedded(G - 1, 1)
            second_norm(1)
            dve.wait_ge(text_in, 32)
            dve.wait_ge(cls_put, 16)
            dve.wait_ge(pn_ready, G)
            for b in range(2):
                dve.wait_ge(emb_put[b], LEAD + 32)
            token_moments(0, 4)
            rsqrt(T, 0, 4)
            dve.sem_inc(ln_ready, 1)
            dve.wait_ge(emb_ps, LEAD + G)
            def low_x(g):
                dve.wait_ge(xh_ready, g + 1)
                dve.tensor_tensor(xl[:, :, :], trans[:, 0:2 * TG].rearrange("p (k t) -> p k t", k=KT),
                                  xh[:, :, :].bitcast(F32), ALU.subtract).then_inc(xl_ready, 1)

            def low_latents(g):
                dve.wait_ge(cdh_ready, g + 1)
                dve.tensor_tensor(cdl[:, :, :], proj_a[:, 0:2 * TG].rearrange("p (k t) -> p k t", k=2),
                                  cdh[:, :, :].bitcast(F32), ALU.subtract).then_inc(cdl_ready, 1)

            def low_qk(g, b, s):
                dve.wait_ge(qkh_ready, 8 * g + s + 1)
                at = 2 * PT + s // 4
                dve.scalar_tensor_tensor(stacked(b, s), stacked(b, s).bitcast(F32), column[:, at:at + 1],
                                         proj_bank(s)[:, 0:2 * TG].rearrange("p (k t) -> p k t", k=2),
                                         ALU.mult, ALU.add).then_inc(qkl_ready, 1)

            def maximum(g, u):
                m, half = u // 2, u % 2
                if u == 0:
                    dve.wait_ge(m_ps, LEAD + g)
                dve.wait_ge(s_ps, 4 * g + u + 1)
                dve.tensor_reduce(
                    mx[:, :].rearrange("p (a x) -> p a x", a=2)[:, :, NPAIR * m + 4 * half:NPAIR * m + 4 * half + 4],
                    ring[u % 2][0:T, :].rearrange("p (a x) -> p a x", a=2)[:, :, 0:4 * T]
                    .rearrange("p a (j k) -> p a j k", j=4), AX.X, ALU.max).then_inc(max_done, 1)

            def low_maxima(g):
                dve.wait_ge(mh_ready, g + 1)
                for at in (0, 64):
                    dve.tensor_tensor(mrow[at + 32:at + 64, :], trans[at:at + 32, 0:T],
                                      mrow[at:at + 32, :].bitcast(F32), ALU.subtract).then_inc(ml_ready, 1)
                dve.wait_ge(ml_ready, LEAD + 2 * g + 2)
                dve.wait_ge(st_ps, LEAD + 4 * g)
                dve.tensor_tensor(mdiag[:, :, :], mrow[:, :].bitcast(F32).unsqueeze(1).to_broadcast([128, 4, T]),
                                  column[:, 2 * PT + 2:2 * PT + 6].unsqueeze(2).to_broadcast([128, 4, T]),
                                  ALU.mult).then_inc(mdiag_ready, 1)

            def divide(g, m):
                dve.wait_ge(pv_done, LEAD + 4 * g + 2 * m + 2)
                heads = psY[0:T, 0:NH * (HS + 1)].rearrange("p (h d) -> p h d", h=NH)
                dve.reciprocal(rden[:, m, :], heads[:, :, HS:HS + 1].rearrange("p h d -> p (h d)")).then_inc(rden_ready, 1)
                dve.wait_ge(rden_ready, 2 * g + m + 1)
                dve.wait_ge(y_added, LEAD + 2 * g + m - 1)
                dve.tensor_tensor(y[:, m, :].rearrange("p (h d) -> p h d", h=NH), heads[:, :, 0:HS],
                                  rden[:, m, :].unsqueeze(2).to_broadcast([T, NH, HS]), ALU.mult).then_inc(y_done, 1)

            def third_moments(n):
                at = slice(n, n + 1) if isinstance(n, int) else bass.ds(n, 1)
                dve.wait_ge(y_added, LEAD + n + 1)
                dve.bn_stats(stats3[:, at, :].rearrange("p a c -> p (a c)"),
                             h[:, at, :].rearrange("p a c -> p (a c)")).then_inc(stat3_ready, 1)

            def group(g, b, ahead, further):
                for u in range(1, 4):
                    maximum(g, u)
                    if ahead:
                        low_qk(g + 1, 1 - b, u)
                low_maxima(g)
                if ahead:
                    for s in range(4, 8):
                        low_qk(g + 1, 1 - b, s)
                divide(g, 0)
                if further:
                    low_x(g + 2)
                    low_latents(g + 2)
                third_moments(2 * g)
                if ahead:
                    maximum(g + 1, 0)
                if further:
                    low_qk(g + 2, b, 0)
                divide(g, 1)

            low_x(0)
            low_latents(0)
            for s in range(8):
                low_qk(0, 0, s)
                if s == 1:
                    for b in range(2):
                        dve.wait_ge(emb_put[b], LEAD + 128)
                if s in (1, 3, 5):
                    token_moments(4 + 2 * (s - 1), 4)
            low_x(1)
            rsqrt(T, 4, 12)
            dve.sem_inc(ln_ready, 1)
            low_latents(1)
            for b in range(2):
                dve.memset(vals[b][:, :, :, HS:HS + 1], 1.0).then_inc(tiles_set, 1)
            dve.memset(mx[:, :], 0.0).then_inc(tiles_set, 1)
            dve.wait_ge(tiles_set, 3)
            maximum(0, 0)
            low_qk(1, 1, 0)
            over_groups(dve, group)

            for n in range(1, NI, 2):
                third_moments(n)
            dve.wait_ge(stat3_ready, NI)
            for n in range(NI):
                step(dve.bn_aggr(mv[0:T, n, :], stats3[:, n, :]))
            dve.wait_ge(xn_ready, NI)
            rsqrt(T, 0, NI)
            dve.sem_inc(ln3_ready, 1)
            dve.wait_ge(wr_cleared, 2)
            dve.wait_ge(wrh_ready, 1)
            dve.tensor_tensor(wrl[:, :, 0:NE], wr_raw[:, :, :], wrh[:, :, 0:NE].bitcast(F32), ALU.subtract).then_inc(wr_ready, 1)

            def x2_norm(g, b):
                at = bass.ds(2 * g + 1, 1)
                dve.wait_ge(x2t_ps, LEAD + g - 1)
                dve.tensor_scalar(x2n[b][:, 1, :], h[:, at, :].rearrange("p a c -> p (a c)"), rstd[0:T, at], offset[0:T, at],
                                  ALU.mult, ALU.add).then_inc(x2n_ready[1], 1)

            def x2_low(g, b):
                dve.wait_ge(x2h_ready, g + 1)
                at = bass.ds(g * TG, TG)
                dve.tensor_tensor(x2l[:, :, at], (trans, proj_a)[b][:, 0:2 * TG].rearrange("p (k t) -> p k t", k=KT),
                                  x2h[:, :, at].bitcast(F32), ALU.subtract).then_inc(x2l_ready, 1)

            x2_norm(0, 0)
            x2_norm(1, 1)
            with dve.Fori(0, NC - 1) as c:
                x2_low(2 * c, 0)
                x2_norm(2 * c + 2, 0)
                x2_low(2 * c + 1, 1)
                x2_norm(2 * c + 3, 1)
            x2_low(G - 2, 0)
            x2_low(G - 1, 1)
            step.then(dve.reciprocal(temp[:, 1:2], temp[:, 0:1]))

            def grid(k):
                return rt[:, k, :]

            def by_image(k):
                return rt[:, k, :].rearrange("p (i e) -> p i e", e=NE)

            def spread(k):
                return rs[:, k, :].unsqueeze(2).to_broadcast([T, NI, NE])

            dve.wait_ge(lg_ps, LEAD + NC)
            dve.tensor_scalar(grid(0), psY[0:T, 0:NI * NE], temp[0:T, 1:2], None, ALU.mult).then_inc(lg_ready, 1)
            dve.wait_ge(route_exp, 1)
            step.then(dve.tensor_scalar(grid(1), grid(1), 1.0, None, ALU.add))
            step.then(dve.reciprocal(grid(2), grid(1)))
            step.then(dve.tensor_scalar(grid(7), grid(2), -GOLDEN_CENTER, None, ALU.add))
            dve.scalar_tensor_tensor(grid(3), grid(7), -1.0, grid(7), ALU.mult, ALU.max).then_inc(dist_ready, 1)
            step.then(dve.tensor_scalar(grid(6), grid(2), GOLDEN_LOWER, None, ALU.is_ge))
            step.then(dve.scalar_tensor_tensor(grid(6), grid(2), GOLDEN_UPPER, grid(6), ALU.is_le, ALU.mult))
            dve.wait_ge(route_exp, 3)
            step.then(dve.tensor_tensor(grid(4), grid(4), grid(6), ALU.mult))
            step.then(dve.tensor_reduce(rs[:, 0, :], by_image(4), AX.X, ALU.add))
            step(dve.tensor_scalar(rs[:, 1, :], rs[:, 0, :], 1e-8, None, ALU.is_lt))
            step(dve.tensor_scalar(rs[:, 2, :], rs[:, 0, :], 1e-8, None, ALU.is_ge))
            dve.wait_ge(descend_set, NE)
            step.then(dve.tensor_copy(grid(7), grid(5)))
            for k in (8, 9):
                step.then(dve.tensor_reduce(rs[:, 3, :], by_image(7), AX.X, ALU.max))
                step.then(dve.tensor_tensor(by_image(k), by_image(7), spread(3), ALU.is_equal))
                step.then(dve.tensor_tensor(by_image(k), by_image(k), descend[:, :, :], ALU.mult))
                step.then(dve.tensor_reduce(rs[:, 3, :], by_image(k), AX.X, ALU.max))
                step.then(dve.tensor_tensor(by_image(k), by_image(k), spread(3), ALU.is_equal))
                step.then(dve.scalar_tensor_tensor(grid(7), grid(k), -4.0, grid(7), ALU.mult, ALU.add))
            step.then(dve.tensor_tensor(grid(8), grid(8), grid(9), ALU.add))
            step.then(dve.tensor_tensor(grid(5), grid(5), grid(8), ALU.mult))

            def normalise(k):
                step.then(dve.tensor_reduce(rs[:, 3, :], by_image(k), AX.X, ALU.add))
                step.then(dve.tensor_scalar(rs[:, 3, :], rs[:, 3, :], 1e-8, None, ALU.max))
                step.then(dve.reciprocal(rs[:, 3, :], rs[:, 3, :]))
                return dve.tensor_tensor(by_image(k), by_image(k), spread(3), ALU.mult)

            step.then(normalise(5))
            step.then(dve.tensor_tensor(by_image(5), by_image(5), spread(1), ALU.mult))
            step.then(dve.tensor_tensor(by_image(4), by_image(4), spread(2), ALU.mult))
            step.then(dve.tensor_tensor(grid(4), grid(4), grid(5), ALU.add))
            normalise(4).then_inc(route_done, 1)

            def weighted_up(c, e):
                n = NE * c + e
                dve.wait_ge(wb_ready, LEAD + n + 1)
                for m in range(2):
                    dve.wait_ge(gu_ps, 2 * n + m + 1)
                    dve.wait_ge(hf_ready, LEAD + 2 * n + m - 1)
                    dve.tensor_tensor(wu[m][:, :], ring[m][:, 512:512 + TC], wb[e % 2][:, :], ALU.mult).then_inc(wu_ready, 1)

            def hidden_low(c, e):
                n = NE * c + e
                dve.wait_ge(down_done, LEAD + n - 1)
                for m in range(2):
                    dve.wait_ge(hh_ready, 2 * n + m + 1)
                    dve.tensor_tensor(hl[e % 2][:, m, :], hf[m][:, :], hh[e % 2][:, m, :].bitcast(F32),
                                      ALU.subtract).then_inc(hl_ready, 1)

            def chunk(c, last):
                for e in range(1, NE):
                    weighted_up(c, e)
                    hidden_low(c, e)
                if not last:
                    weighted_up(c + 1, 0)
                dve.wait_ge(down_done, LEAD + NE * c + NE)
                dve.wait_ge(o_ps, LEAD + c)
                dve.tensor_copy(oT[:, 1, :], proj_a[:, 0:TC]).then_inc(oT_ready1, 1)
                if not last:
                    hidden_low(c + 1, 0)
                dve.wait_ge(o_ps, LEAD + c + 1)
                dve.wait_ge(out_sent, LEAD + 16 * c)
                for half, ps in enumerate((proj_b, psY)):
                    dve.tensor_tensor(res[:, 2 * half:2 * half + 2, :],
                                      h[:, slice(4 * c + 2 * half, 4 * c + 2 * half + 2) if isinstance(c, int) else bass.ds(4 * c + 2 * half, 2), :],
                                      ps[0:T, :].rearrange("p (i n) -> p i n", i=2), ALU.add).then_inc(res_ready, 1)

            weighted_up(0, 0)
            hidden_low(0, 0)
            with dve.Fori(0, NC - 1) as c:
                chunk(c, False)
            chunk(NC - 1, True)

        @block.tensor
        def _(pe):
            pe.wait_ge(attw_in, 16)
            for m in range(KT):
                last = pe.matmul(ring[0][:, m * C:(m + 1) * C], raw_uqT[:, m * 128:(m + 1) * 128],
                                 raw_dq, start=True, stop=True)
            last.then_inc(aT_ps, 1)
            pe.wait_ge(aT_ready, 1)
            for at, w, x in ((512, raw_uk, aT[:, :, :].rearrange("p k n -> p (k n)")), (512 + C, raw_uv, raw_o)):
                for k in range(KT):
                    last = pe.matmul(ring[0][:, at:at + C], w[:, k * L:(k + 1) * L], x[:, k * C:(k + 1) * C], start=(k == 0), stop=(k == KT - 1))
            last.then_inc(kv_ps, 1)

            pe.wait_ge(ident_ready, 4)
            pe.wait_ge(emb_w_in, 16 * 5)

            def patch_transposes(g, k):
                pe.wait_ge(pn_ready, g + 1)
                pe.wait_ge(zs_ready, LEAD + g - 1)
                for n in range(PT):
                    last = pe.transpose((trans, proj_a)[k % 2][:, n * GP:(n + 1) * GP], pn[k][:, n * 128:(n + 1) * 128],
                                        ident[0:GP, 0:GP])
                last.then_inc(pnT_ps, 1)

            def embed(g, k):
                pe.wait_ge(zT_ready, g + 1)
                pe.wait_ge(z_ready, LEAD + g - 1)
                for n in range(PT):
                    last = pe.matmul((proj_b, psY)[k % 2][0:GP, 0:C], zT[k % 2][:, n, :], wproj[:, n, :],
                                     start=(n == 0), stop=(n == PT - 1))
                last.then_inc(emb_ps, 1)

            with pe.Fori(0, 2) as i:
                patch_transposes(4 * i, 0)
                for k in range(1, 4):
                    patch_transposes(4 * i + k, k)
                    embed(4 * i + k - 1, k - 1)
                embed(4 * i + 3, 3)

            pe.wait_ge(attw_ready, 4)
            pe.wait_ge(z_ready, LEAD + G)
            pe.wait_ge(pick_ready, 8)

            def tokens_transposed(g):
                pe.wait_ge(xn_ready, 2 * g + 2)
                pe.wait_ge(ml_ready, LEAD + 2 * (g - 1))
                for m in range(2):
                    for k in range(KT):
                        last = pe.transpose(trans[:, k * TG + m * T:k * TG + (m + 1) * T],
                                            xn[:, m, k * 128:(k + 1) * 128], ident[0:T, 0:T])
                last.then_inc(xt_ps, 1)

            def latents(g, j):
                if j == 0:
                    pe.wait_ge(xh_ready, g + 1)
                    pe.wait_ge(xl_ready, g + 1)
                    pe.wait_ge(qkl_ready, LEAD + 8 * g)
                w = (dkv, dq)[j]
                for k in range(KT):
                    last = three_pass(pe, proj_a[:, j * TG:(j + 1) * TG], w(attw_h, k), w(attw_l, k),
                                      xh[:, k, :], xl[:, k, :], k == 0, k == KT - 1)
                if j == 1:
                    last.then_inc(cd_ps, 1)

            def project_qk(g, s):
                if s == 0:
                    pe.wait_ge(cdh_ready, g + 1)
                    pe.wait_ge(cdl_ready, g + 1)
                    pe.wait_ge(v_ready, LEAD + g)
                elif s >= 2:
                    pe.wait_ge(qkl_ready, LEAD + 8 * g + s - 1)
                which = s // 4
                for k in range(2):
                    w = (attw_h, attw_l)
                    last = three_pass(pe, proj_bank(s)[:, k * TG:(k + 1) * TG],
                                      *(pair_w(x, which, 2 * (s % 4) + k) for x in w),
                                      cdh[:, 1 - which, :], cdl[:, 1 - which, :], True, True)
                last.then_inc(qk_ps, 1)

            def project_v(g):
                pe.wait_ge(qkl_ready, LEAD + 8 * g + 7)
                for m in range(2):
                    ch, cl = cdh[:, 0, m * T:(m + 1) * T], cdl[:, 0, m * T:(m + 1) * T]
                    o = proj_b[0:T, m * C:(m + 1) * C]
                    pe.matmul(o, ch, veff(attw_h), start=True, stop=False)
                    pe.matmul(o, ch, veff(attw_l), start=False, stop=False)
                    last = pe.matmul(o, cl, veff(attw_h), start=False, stop=True)
                last.then_inc(v_ps, 1)

            def score(g, b, u, q_first):
                m, half = u // 2, u % 2
                for par in range(2):
                    pe.matmul(ring[u % 2][0:T, par * 512:par * 512 + 4 * T], ident_b[0:T, 0:T],
                              (causal if q_first else causal_t)[:, :, :].to_broadcast([T, 4, T]),
                              start=True, stop=False, skip_group_check=True)
                for j in range(4):
                    for par in range(2):
                        pair = 4 * half + j
                        q, k = (stacks[b][64 * par:64 * par + 64, s, pair, m * T:(m + 1) * T] for s in range(2))
                        o = ring[u % 2][0:T, par * 512 + j * T:par * 512 + (j + 1) * T]
                        w, x = (q, k) if q_first else (k, q)
                        last = pe.matmul(o, w, x, start=False, stop=(q_first and j == 3), skip_group_check=True)
                if not q_first:
                    if u == 0:
                        pe.wait_ge(mdiag_ready, LEAD + g + 1)
                    for par in range(2):
                        last = pe.matmul(ring[u % 2][0:T, par * 512:par * 512 + 4 * T], pick[64 * par:64 * par + 64, u, :],
                                         mdiag[64 * par:64 * par + 64, :, :].rearrange("p j t -> p (j t)"),
                                         start=False, stop=True, skip_group_check=True)
                return last

            def scores(g, b, u):
                if u == 0:
                    pe.wait_ge(qkl_ready, LEAD + 8 * g + 8)
                if u < 2:
                    pe.wait_ge(exp_done, LEAD + 4 * g + u - 1)
                else:
                    pe.wait_ge(max_done, 4 * g + u - 1)
                score(g, b, u, True).then_inc(s_ps, 1)

            def maxima_transposed(g, ahead):
                pe.wait_ge(max_done, 4 * g + 4)
                if ahead:
                    pe.wait_ge(xl_ready, g + 2)
                pe.transpose(trans[:, 0:T], mx[:, :], ident[0:T, 0:T]).then_inc(m_ps, 1)

            def transposed_scores(g, b, u):
                if u >= 2:
                    pe.wait_ge(exp_done, LEAD + 4 * g + u - 1)
                score(g, b, u, False).then_inc(st_ps, 1)

            def weighted(g, b, u, part):
                m, half = u // 2, u % 2
                if part == 0:
                    pe.wait_ge(tiles_set, 3)
                    pe.wait_ge(exp_done, LEAD + 4 * g + u + 1)
                    if u == 0:
                        pe.wait_ge(v_ready, LEAD + g + 1)
                    if half == 0:
                        pe.wait_ge(y_done, LEAD + 2 * g + m)
                for j in range(2 * part, 2 * part + 2):
                    for par in range(2):
                        head = 2 * (4 * half + j) + par
                        last = pe.matmul(psY[0:T, head * (HS + 1):(head + 1) * (HS + 1)], probs[u % 2][:, par, j, :],
                                         vals[b][:, m, head, :], start=True, stop=True)
                if part == 1:
                    last.then_inc(pv_done, 1)

            def group(g, b, ahead, further):
                for u in range(1, 4):
                    scores(g, b, u)
                    if ahead:
                        project_qk(g + 1, u)
                if ahead:
                    project_qk(g + 1, 4)
                maxima_transposed(g, ahead)
                if ahead:
                    project_qk(g + 1, 5)
                transposed_scores(g, b, 0)
                if ahead:
                    project_qk(g + 1, 6)
                transposed_scores(g, b, 1)
                weighted(g, b, 0, 0)
                if ahead:
                    project_qk(g + 1, 7)
                weighted(g, b, 0, 1)
                transposed_scores(g, b, 2)
                weighted(g, b, 1, 0)
                if ahead:
                    project_v(g + 1)
                weighted(g, b, 1, 1)
                if further:
                    tokens_transposed(g + 2)
                transposed_scores(g, b, 3)
                weighted(g, b, 2, 0)
                if further:
                    latents(g + 2, 0)
                weighted(g, b, 2, 1)
                if further:
                    latents(g + 2, 1)
                if ahead:
                    scores(g + 1, 1 - b, 0)
                weighted(g, b, 3, 0)
                if further:
                    project_qk(g + 2, 0)
                weighted(g, b, 3, 1)

            tokens_transposed(0)
            latents(0, 0)
            latents(0, 1)
            for s in range(8):
                project_qk(0, s)
            project_v(0)
            tokens_transposed(1)
            latents(1, 0)
            latents(1, 1)
            scores(0, 0, 0)
            project_qk(1, 0)
            over_groups(pe, group)

            def gate_up(c, e):
                n = NE * c + e
                at = slice(c * TC, (c + 1) * TC) if isinstance(c, int) else bass.ds(c * TC, TC)
                for m in range(2):
                    pe.wait_ge(sg_ready, LEAD + (2 * n + m - 1 if e else 2 * n))
                    pe.wait_ge(wu_ready, LEAD + (2 * n + m - 1 if e else 2 * n))
                    for part in range(2):
                        for k in range(KT):
                            last = three_pass(pe, ring[m][:, part * 512:part * 512 + TC], expert_w(wh, e, part, k, m),
                                              expert_w(wl, e, part, k, m), x2h[:, k, at], x2l[:, k, at],
                                              k == 0, k == KT - 1)
                    last.then_inc(gu_ps, 1)

            def x2_transposed(g, b):
                for m in range(2):
                    pe.wait_ge(x2n_ready[m], g + 1)
                pe.wait_ge(x2l_ready, LEAD + g - 1)
                for m in range(2):
                    for k in range(KT):
                        last = pe.transpose((trans, proj_a)[b][:, k * TG + m * T:k * TG + (m + 1) * T],
                                            x2n[b][:, m, k * 128:(k + 1) * 128], ident[0:T, 0:T])
                last.then_inc(x2t_ps, 1)

            def route(c):
                pe.wait_ge(x2l_ready, LEAD + 2 * c + 2)
                pe.wait_ge(lgT_ready, LEAD + c)
                at = slice(c * TC, (c + 1) * TC)
                for k in range(KT):
                    last = three_pass(pe, proj_b[:, 0:TC], wrh[:, k, :], wrl[:, k, :], x2h[:, k, at], x2l[:, k, at],
                                      k == 0, k == KT - 1)
                last.then_inc(lgT_ps, 1)

            def logits_back(c):
                pe.wait_ge(lgT_ready, LEAD + c + 1)
                for m in range(4):
                    at = (4 * c + m) * NE
                    last = pe.transpose(psY[0:T, at:at + NE], lgT[:, m * T:(m + 1) * T], ident[0:NE, 0:NE])
                last.then_inc(lg_ps, 1)

            x2_transposed(0, 0)
            x2_transposed(1, 1)
            pe.wait_ge(wr_ready, 1)
            for c in range(NC):
                if c < NC - 1:
                    x2_transposed(2 * c + 2, 0)
                if c > 0:
                    logits_back(c - 1)
                if c < NC - 1:
                    x2_transposed(2 * c + 3, 1)
                route(c)
            gate_up(0, 0)
            logits_back(NC - 1)

            def down(c, e):
                n = NE * c + e
                if e == 0:
                    pe.wait_ge(oT_ready0, LEAD + c)
                    pe.wait_ge(oT_ready1, LEAD + c)
                pe.wait_ge(hh_ready, 2 * n + 2)
                pe.wait_ge(hl_ready, LEAD + 2 * n + 2)
                for m in range(2):
                    for k in range(2):
                        last = three_pass(pe, (trans, proj_a)[m][:, 0:TC], expert_w(wh, e, 2, k, m),
                                          expert_w(wl, e, 2, k, m), hh[e % 2][:, k, :], hl[e % 2][:, k, :],
                                          e == 0 and k == 0, e == NE - 1 and k == 1)
                last.then_inc(down_done, 1)

            def chunk(c, last_chunk):
                down(c, 0)
                for e in range(1, NE):
                    if e < NE - 1:
                        gate_up(c, e + 1)
                    elif not last_chunk:
                        gate_up(c + 1, 0)
                    down(c, e)
                if not last_chunk:
                    gate_up(c + 1, 1)
                pe.wait_ge(oT_ready0, LEAD + c + 1)
                pe.wait_ge(oT_ready1, LEAD + c + 1)
                pe.wait_ge(res_ready, LEAD + 2 * c)
                for m in range(4):
                    for k in range(2):
                        last = pe.transpose((proj_b, psY)[m // 2][0:T, (m % 2) * C + k * 128:(m % 2) * C + (k + 1) * 128],
                                            oT[:, k, m * T:(m + 1) * T], ident[:, :])
                last.then_inc(o_ps, 1)

            pe.wait_ge(route_done, 1)
            pe.transpose(psY[:, 256:256 + T], rt[:, 4, :], ident[0:T, 0:T]).then_inc(wT_ps, 1)
            pe.wait_ge(wT_ready, 1)
            gate_up(0, 1)
            with pe.Fori(0, NC - 1) as c:
                chunk(c, False)
            chunk(NC - 1, True)


def kernel(x, txt, L0_tok_ln1_g, L0_tok_ln1_b, L0_tok_W_proj, L0_tok_b_proj, L0_tok_ln2_g, L0_tok_ln2_b,
           L0_tok_cls_token, L0_tok_pos_emb, L0_attn_W_dq, L0_attn_W_uq, L0_attn_W_dkv, L0_attn_W_uk,
           L0_attn_W_uv, L0_attn_W_o, L0_ffn_Wg, L0_ffn_Wu, L0_ffn_Wd, L0_ffn_Wr, L0_ffn_temperature):
    import numpy as np
    import concourse.bacc as bacc
    from concourse.bass_utils import run_bass_kernel_spmd

    patches = np.asarray(x).reshape(NI, 3, 6, 16, 6, 16).transpose(0, 2, 4, 3, 5, 1).reshape(G, GP, PD)

    def tiles(w):
        w = np.asarray(w)
        return w.reshape(-1, 128, w.shape[1]).transpose(1, 0, 2).reshape(128, -1)

    dq, uq, dkv, wo = (np.asarray(w) for w in (L0_attn_W_dq, L0_attn_W_uq, L0_attn_W_dkv, L0_attn_W_o))
    copy = np.arange(128) // HS % REP
    low = -np.stack([copy >= 2, copy % 2 == 1], 1).astype(np.float32)
    place = -(np.arange(128)[:, None] % 4 == np.arange(4)).astype(np.float32) * (np.arange(128)[:, None] % 32 < 16)
    place = place.astype(np.float32)
    laid_out = {
        "patches": patches, "txt": txt,
        "by_column": np.concatenate([tiles(np.asarray(v).reshape(PD, 1)) for v in (L0_tok_ln1_g, L0_tok_ln1_b)] + [low, place], 1),
        "W_proj": L0_tok_W_proj,
        "by_row": np.concatenate([np.asarray(v) for v in (L0_tok_b_proj, L0_tok_ln2_g, L0_tok_ln2_b)]),
        "pos_emb": L0_tok_pos_emb,
        "first_token": np.concatenate([np.asarray(L0_tok_cls_token)[0], np.asarray(L0_tok_pos_emb)[0, 0:1]]).reshape(1, 2 * C),
        "attn_weights": np.concatenate([tiles(dkv.T), tiles(dq.T), uq.T, dq, tiles(L0_attn_W_uk), tiles(L0_attn_W_uv), tiles(wo.T)], 1),
        "expert_weights": np.stack([np.concatenate([tiles(np.asarray(w)[e]) for w in (L0_ffn_Wg, L0_ffn_Wu, L0_ffn_Wd)], 1)
                                    for e in range(NE)], 1),
        "Wr": L0_ffn_Wr, "temperature": L0_ffn_temperature,
    }
    nc = bacc.Bacc("TRN2", target_bir_lowering=False, num_devices=1)
    arrays, args = {}, []
    for name, a in laid_out.items():
        a = np.ascontiguousarray(a)
        arrays[f"in_{name}"] = a
        args.append(nc.dram_tensor(f"in_{name}", a.shape, mybir.dt.from_np(a.dtype), kind="ExternalInput").ap())
    out = nc.dram_tensor("out_tokens", (NI, T, C), F32, kind="ExternalOutput").ap()
    build(nc, *args, out)
    ran = run_bass_kernel_spmd(nc, [arrays], core_ids=[0])
    return ran.results[0]["out_tokens"]
```

```python
from contextlib import ExitStack

import concourse.bass as bass
from concourse import mybir

F32 = mybir.dt.float32
F32R = mybir.dt.float32r
BF16 = mybir.dt.bfloat16
I32 = mybir.dt.int32
ALU = mybir.AluOpType
ACT = mybir.ActivationFunctionType
AX = mybir.AxisListType

NI = 16
NPATCH = 36
NTXT = 77
T = 1 + NPATCH + NTXT
C = 256
KT = C // 128
PD = 768
PT = PD // 128
G = NI // 2
GP = 2 * NPATCH
TG = 2 * T
NC = NI // 4
TC = 4 * T
NH = 16
HS = C // NH
L = 128
NPAIR = NH // 2
NE = 8
EW = 6 * C
EPS = 1e-5
MASKED = -3.0e38
RSQRT_SEED = float(0x5F3759DF)
REP = 4
AW = 3 * C + 2 * NPAIR * 128
LEAD = 8
GOLDEN_CENTER = 0.36787944117144233
GOLDEN_LOWER = 0.5 - 0.28768207245178085
GOLDEN_UPPER = 0.5


def span(at, n=1):
    return slice(at, at + n) if isinstance(at, int) else bass.ds(at, n)


def settle(eng, past):
    eng.sem_inc(past, 1)


class Steps:

    def __init__(self, eng, sem, start=0):
        self.eng, self.sem, self.start, self.n = eng, sem, start, 0

    def __call__(self, instruction):
        instruction.then_inc(self.sem, 1)
        self.n += 1

    def join(self):
        self.eng.wait_ge(self.sem, self.start + self.n)

    def then(self, instruction):
        self(instruction)
        self.join()


def three_pass(pe, out, whi, wlo, xhi, xlo, first, last):
    pe.matmul(out, whi, xhi, start=first, stop=False)
    pe.matmul(out, wlo, xhi, start=False, stop=False)
    return pe.matmul(out, whi, xlo, start=False, stop=last)


def build(nc, patches, txt, by_column, W_proj, by_row, pos_emb, first_token, attn_weights, expert_weights,
          Wr, temperature, out):
    wscratch = nc.dram_tensor("routing_rows", (NI, NE, T), F32, kind="Internal").ap()

    with ExitStack() as ctx:
        def sb(where, name, shape, dt=F32):
            return where.enter_context(nc.sbuf_tensor(name, shape, dt))

        def sem(name):
            return ctx.enter_context(nc.semaphore(name))

        def psum(name, width):
            return ctx.enter_context(nc.psum_tensor(name, [128, width], F32))

        ring = [psum(f"ring{i}", 1024) for i in range(2)]
        trans = psum("trans", 512)
        proj_a = psum("proj_a", 512)
        proj_b = psum("proj_b", 512)
        psY = psum("psY", 512)

        h = sb(ctx, "h", [T, NI, C])
        wh = sb(ctx, "expert_w_hi", [128, NE * EW], F32R)
        ident = sb(ctx, "ident", [128, 128])
        ident_b = sb(ctx, "ident_b", [128, 128], BF16)
        stats = sb(ctx, "stats", [128, 4, 12])
        stats3 = sb(ctx, "stats3", [T, NI, 6])
        mv = sb(ctx, "mv", [128, NI + G, 2])
        rstd = sb(ctx, "rstd", [128, NI + G])
        offset = sb(ctx, "offset", [128, NI + G])
        nt = sb(ctx, "newton", [128, 2, NI + G])
        wr_raw = sb(ctx, "wr_raw", [128, KT, NE])
        wrh = sb(ctx, "wrh", [128, KT, 128], F32R)
        wrl = sb(ctx, "wrl", [128, KT, 128], F32R)
        temp = sb(ctx, "temp", [128, 2])

        early = ExitStack()
        praw = sb(early, "praw", [GP, G, PD])
        z = sb(early, "z", [GP, G, C])
        raw = sb(early, "raw", [128, 8 * C])
        aT = sb(early, "aT", [128, KT, C])
        early.close()
        wl = sb(ctx, "expert_w_lo", [128, NE * EW], F32R)

        upto_attention = ExitStack()
        stage = sb(upto_attention, "stage", [128, EW])
        attw_h = sb(upto_attention, "attw_h", [128, AW], F32R)
        attw_l = sb(upto_attention, "attw_l", [128, AW], F32R)
        causal = sb(upto_attention, "causal", [T, T], BF16)
        causal_t = sb(upto_attention, "causal_t", [T, T], BF16)
        column = sb(upto_attention, "column", [128, 2 * PT + 6])
        pick = sb(upto_attention, "pick", [128, 4, T], F32R)

        embedding = ExitStack()
        pn = [sb(embedding, f"pn{b}", [GP, PD]) for b in range(4)]
        zs = [sb(embedding, f"zs{b}", [128, PT, GP]) for b in range(2)]
        zT = [sb(embedding, f"zT{b}", [128, PT, GP]) for b in range(2)]
        wproj = sb(embedding, "wproj", [128, PT, C])
        cls = sb(embedding, "cls", [1, 3, C])
        pos = sb(embedding, "pos", [GP, C])
        emb = [sb(embedding, f"emb{b}", [GP, C]) for b in range(2)]
        zn = [sb(embedding, f"zn{b}", [GP, C]) for b in range(2)]
        zg = [sb(embedding, f"zg{b}", [GP, C]) for b in range(2)]
        rows = sb(embedding, "rows", [GP, 3, C])
        posb = sb(embedding, "posb", [GP, C])
        embedding.close()

        attention = ExitStack()
        xn = sb(attention, "xn", [T, 2, C])
        xh = sb(attention, "xh", [128, KT, TG], F32R)
        xl = sb(attention, "xl", [128, KT, TG], F32R)
        cdh = sb(attention, "cdh", [128, 2, TG], F32R)
        cdl = sb(attention, "cdl", [128, 2, TG], F32R)
        stacks = [sb(attention, f"stacks{b}", [128, 2, NPAIR, TG], F32R) for b in range(2)]
        probs = [sb(attention, f"probs{b}", [T, 2, 4, T]) for b in range(2)]
        vals = [sb(attention, f"vals{b}", [T, 2, NH, HS + 1]) for b in range(2)]
        mx = sb(attention, "mx", [T, 128])
        mrow = sb(attention, "mrow", [128, T], F32R)
        mdiag = sb(attention, "mdiag", [128, 4, T], F32R)
        rden = sb(attention, "rden", [T, 2, NH])
        y = sb(attention, "y", [T, 2, C])
        attention.close()
        upto_attention.close()

        oT = sb(ctx, "oT", [128, 2, TC])
        res = sb(ctx, "res", [T, 4, C])
        x2n = [sb(ctx, f"x2n{b}", [T, 2, C]) for b in range(2)]
        x2h = sb(ctx, "x2h", [128, KT, NI * T], F32R)
        x2l = sb(ctx, "x2l", [128, KT, NI * T], F32R)
        lgT = sb(ctx, "lgT", [NE, TC])
        rt = sb(ctx, "rt", [T, 10, NI * NE])
        rs = sb(ctx, "rs", [T, 4, NI])
        descend = sb(ctx, "descend", [T, NI, NE])
        wT = sb(ctx, "wT", [128, 2, T])
        wrow = [sb(ctx, f"wrow{b}", [1, TC]) for b in range(2)]
        wb = [sb(ctx, f"wb{b}", [128, TC]) for b in range(2)]
        sg = [sb(ctx, f"sg{m}", [128, TC]) for m in range(2)]
        wu = [sb(ctx, f"wu{m}", [128, TC]) for m in range(2)]
        hf = [sb(ctx, f"hf{m}", [128, TC]) for m in range(2)]
        hh = [sb(ctx, f"hh{b}", [128, 2, TC], F32R) for b in range(2)]
        hl = [sb(ctx, f"hl{b}", [128, 2, TC], F32R) for b in range(2)]

        ones_set = sem("ones_set")
        ident_ready = sem("ident_ready")
        attw_in = sem("attw_in")
        emb_w_in = sem("emb_w_in")
        cls_in = sem("cls_in")
        cls_made = sem("cls_made")
        patch_in = [sem(f"patch_in{i}") for i in range(2)]
        text_in = sem("text_in")
        cls_put = sem("cls_put")
        attw3_hi = sem("attw3_hi")
        aT_ps = sem("aT_ps")
        aT_ready = sem("aT_ready")
        kv_ps = sem("kv_ps")
        attw_hi = sem("attw_hi")
        attw_ready = sem("attw_ready")
        dve_step = sem("dve_step")
        pn_ready = sem("pn_ready")
        pnT_ps = sem("pnT_ps")
        ln1_ready = sem("ln1_ready")
        ln2_ready = sem("ln2_ready")
        descend_set = sem("descend_set")
        zs_ready = sem("zs_ready")
        zT_ready = sem("zT_ready")
        emb_ps = sem("emb_ps")
        z_ready = sem("z_ready")
        zn_ready = sem("zn_ready")
        posb_ready = sem("posb_ready")
        zg_ready = sem("zg_ready")
        emb_ready = sem("emb_ready")
        emb_put = [sem(f"emb_put{b}") for b in range(2)]
        ln_ready = sem("ln_ready")
        sp_past = sem("sp_past")
        pool_past = sem("pool_past")
        act_past = sem("act_past")
        tiles_set = sem("tiles_set")
        xn_ready = sem("xn_ready")
        xt_ps = sem("xt_ps")
        xh_ready = sem("xh_ready")
        xl_ready = sem("xl_ready")
        cd_ps = sem("cd_ps")
        cdh_ready = sem("cdh_ready")
        cdl_ready = sem("cdl_ready")
        qk_ps = sem("qk_ps")
        v_ps = sem("v_ps")
        qkh_ready = sem("qkh_ready")
        qkl_ready = sem("qkl_ready")
        v_ready = sem("v_ready")
        pick_ready = sem("pick_ready")
        s_ps = sem("s_ps")
        max_done = sem("max_done")
        m_ps = sem("m_ps")
        mh_ready = sem("mh_ready")
        ml_ready = sem("ml_ready")
        mdiag_ready = sem("mdiag_ready")
        st_ps = sem("st_ps")
        exp_done = sem("exp_done")
        pv_done = sem("pv_done")
        rden_ready = sem("rden_ready")
        y_done = sem("y_done")
        y_added = sem("y_added")
        stage_in = sem("stage_in")
        wh_ready = sem("wh_ready")
        wl_ready = sem("wl_ready")
        wr_in = sem("wr_in")
        wr_cleared = sem("wr_cleared")
        wrh_ready = sem("wrh_ready")
        wr_ready = sem("wr_ready")
        stat3_ready = sem("stat3_ready")
        ln3_ready = sem("ln3_ready")
        x2n_ready = [sem(f"x2n_ready{m}") for m in range(2)]
        x2t_ps = sem("x2t_ps")
        x2h_ready = sem("x2h_ready")
        x2l_ready = sem("x2l_ready")
        lgT_ps = sem("lgT_ps")
        lgT_ready = sem("lgT_ready")
        lg_ps = sem("lg_ps")
        lg_ready = sem("lg_ready")
        route_exp = sem("route_exp")
        dist_ready = sem("dist_ready")
        route_done = sem("route_done")
        wT_ps = sem("wT_ps")
        wT_ready = sem("wT_ready")
        wT_out = sem("wT_out")
        wrow_in = [sem(f"wrow_in{b}") for b in range(2)]
        wb_ready = sem("wb_ready")
        gu_ps = sem("gu_ps")
        sg_ready = sem("sg_ready")
        wu_ready = sem("wu_ready")
        hf_ready = sem("hf_ready")
        hh_ready = sem("hh_ready")
        hl_ready = sem("hl_ready")
        down_done = sem("down_done")
        oT_ready0 = sem("oT_ready0")
        oT_ready1 = sem("oT_ready1")
        o_ps = sem("o_ps")
        res_ready = sem("res_ready")
        out_sent = sem("out_sent")

        def dkv(w, k):
            return w[:, k * L:(k + 1) * L]

        def dq(w, k):
            return w[:, C + k * L:C + (k + 1) * L]

        def veff(w):
            return w[:, 2 * C:3 * C]

        def repeated(w, which):
            at = 3 * C + which * NPAIR * 128
            return w[:, at:at + NPAIR * 128].rearrange("p (h r d) -> p h r d", r=REP, d=HS)

        def pair_w(w, which, pair):
            at = 3 * C + (which * NPAIR + pair) * 128
            return w[:, at:at + 128]

        def heads_of(x):
            return x.rearrange("p (h d) -> p h d", d=HS).unsqueeze(2).to_broadcast([128, NH, REP, HS])

        raw_dkvT, raw_dqT, raw_uqT, raw_dq, raw_uk, raw_uv = (raw[:, j * C:(j + 1) * C] for j in range(6))
        raw_o = raw[:, 6 * C:8 * C]

        def expert_w(w, e, part, k, m):
            at = e * EW + part * KT * C + k * C + m * 128
            return w[:, at:at + 128]

        leading = [zs_ready, zg_ready, emb_ps, z_ready, emb_ready, pnT_ps, *emb_put, xt_ps, cd_ps, v_ps, st_ps,
                   pv_done, ml_ready, mdiag_ready, qkl_ready, v_ready, exp_done, y_done, m_ps, y_added, wl_ready,
                   lg_ps, lgT_ready, x2t_ps, x2l_ready, wb_ready, wu_ready, hl_ready, sg_ready, hf_ready, down_done,
                   o_ps, out_sent, oT_ready0, oT_ready1, res_ready]

        ROUTED = (slice(0, 4), slice(4, NI))
        ROUTED_ROWS = (slice(0, 4 * NE), slice(4 * NE, NI * NE))

        block = ctx.enter_context(nc.Block())

        def over_groups(eng, body):
            with eng.Fori(0, G // 2 - 1) as i:
                for b in range(2):
                    body(2 * i + b, b, True, True)
            body(G - 2, 0, True, False)
            body(G - 1, 1, False, False)

        def proj_bank(s):
            return (proj_b, proj_a)[s % 2]

        def stacked(b, s):
            return stacks[b][:, s // 4, 2 * (s % 4):2 * (s % 4) + 2, :]

        @block.sync
        def _(sp):
            for led in leading:
                sp.sem_inc(led, LEAD)
            def patches_in(i):
                sp.dma_start(praw[:, 4 * i:4 * i + 4, :],
                             patches[4 * i:4 * i + 4].rearrange("g p d -> p g d")).then_inc(patch_in[i], 16)

            patches_in(0)
            sp.dma_start(raw[:, :], attn_weights).then_inc(attw_in, 16)
            sp.dma_start(column[:, :], by_column).then_inc(emb_w_in, 16)
            sp.dma_start(wproj[:, :, :], W_proj.rearrange("(k p) n -> p k n", p=128)).then_inc(emb_w_in, 16)
            patches_in(1)
            sp.dma_start(rows[:, :, :].rearrange("p a c -> p (a c)"), by_row.partition_broadcast(GP)).then_inc(emb_w_in, 16)
            sp.dma_start(pos[0:NPATCH, :], pos_emb[0, 1:, :]).then_inc(emb_w_in, 16)
            sp.dma_start(pos[NPATCH:GP, :], pos_emb[0, 1:, :]).then_inc(emb_w_in, 16)
            sp.dma_start(cls[0:1, 0:2, :].rearrange("p a c -> p (a c)"), first_token).then_inc(cls_in, 16)
            for i in range(2):
                sp.dma_start(h[1 + NPATCH:T, 8 * i:8 * i + 8, :],
                             txt[8 * i:8 * i + 8].rearrange("b t c -> t b c")).then_inc(text_in, 16)
            sp.dma_start(wr_raw[:, :, :], Wr.rearrange("(k p) n -> p k n", p=128)).then_inc(wr_in, 16)
            sp.dma_start(temp[:, 0:1], temperature.partition_broadcast(128)).then_inc(wr_in, 16)
            sp.wait_ge(cls_made, 1)
            sp.dma_start(h[0:1, :, :], cls[0:1, 2:3, :].to_broadcast([1, NI, C])).then_inc(cls_put, 16)

            with sp.Fori(0, G // 2) as i:
                for b in range(2):
                    sp.wait_ge(emb_ready, LEAD + 2 * i + b + 1)
                    settle(sp, sp_past)
                    for m in range(2):
                        sp.dma_start(h[1:1 + NPATCH, bass.ds(4 * i + 2 * b + m, 1), :],
                                     emb[b][m * NPATCH:(m + 1) * NPATCH, :].unsqueeze(1)
                                     ).then_inc(emb_put[b], 16)

            with sp.Fori(0, NE) as e:
                sp.wait_ge(wl_ready, LEAD + e)
                settle(sp, sp_past)
                sp.dma_start(stage[:, :].unsqueeze(1), expert_weights[:, bass.ds(e, 1), :]).then_inc(stage_in, 16)


            def weights_out(r):
                rows_of = ROUTED_ROWS[r]
                sp.wait_ge(wT_ready, r + 1)
                sp.dma_start(wscratch.rearrange("i e t -> (i e) t")[rows_of, :],
                             wT[0:rows_of.stop - rows_of.start, r, :]).then_inc(wT_out, 16)
                sp.wait_ge(wT_out, 16 * (r + 1))

            def row_in(c, e):
                sp.wait_ge(wb_ready, LEAD + NE * c + e - 1)
                settle(sp, sp_past)
                at = span(c)
                sp.dma_start(wrow[e % 2][0:1, :].rearrange("p (i t) -> p i t", t=T),
                             wscratch.rearrange("(c i) e t -> e c i t", i=4)[e, at, :, :]
                             ).then_inc(wrow_in[e % 2], 16)

            def rows_and_results(c, last):
                for e in range(2, NE):
                    row_in(c, e)
                if isinstance(c, int) and c == 0:
                    weights_out(1)
                if not last:
                    row_in(c + 1, 0)
                    row_in(c + 1, 1)
                sp.wait_ge(res_ready, LEAD + 2 * c + 2)
                settle(sp, sp_past)
                at = span(c)
                sp.dma_start(out.rearrange("(c i) t n -> t c i n", i=4)[:, at, :, :],
                             res[:, :, :].unsqueeze(1)).then_inc(out_sent, 16)

            weights_out(0)
            row_in(0, 0)
            row_in(0, 1)
            rows_and_results(0, False)
            with sp.Fori(1, NC - 1) as c:
                rows_and_results(c, False)
            rows_and_results(NC - 1, True)
            sp.wait_ge(out_sent, LEAD + 16 * NC)

        @block.gpsimd
        def _(pool):
            pool.memset(wrh[:, :, :].bitcast(F32), 0.0).then_inc(wr_cleared, 1)
            pool.memset(wrl[:, :, :].bitcast(F32), 0.0).then_inc(wr_cleared, 1)
            pool.memset(ident[:, :], 1.0).then_inc(ones_set, 1)
            pool.memset(ident_b[:, :], 1.0).then_inc(ones_set, 1)
            pool.memset(causal[:, :], 0.0).then_inc(ones_set, 1)
            pool.memset(causal_t[:, :], 0.0).then_inc(ones_set, 1)
            pool.memset(pick[:, :, :].bitcast(F32), 1.0).then_inc(ones_set, 1)
            pool.wait_ge(ones_set, 5)
            for t in (ident, ident_b):
                pool.affine_select(out=t[:, :], in_=t[:, :], compare_op=ALU.is_equal, fill=0.0, base=0,
                                   pattern=[[-1, 128]], channel_multiplier=1).then_inc(ident_ready, 1)
            pool.affine_select(out=causal[:, :], in_=causal[:, :], compare_op=ALU.is_ge, fill=MASKED,
                               base=0, pattern=[[-1, T]], channel_multiplier=1).then_inc(ident_ready, 1)
            pool.affine_select(out=causal_t[:, :], in_=causal_t[:, :], compare_op=ALU.is_ge, fill=MASKED,
                               base=0, pattern=[[1, T]], channel_multiplier=-1).then_inc(ident_ready, 1)
            pool.wait_ge(ident_ready, 4)
            for at in range(0, 128, 32):
                if at:
                    pool.wait_ge(pick_ready, at // 16)
                of = pick[at:at + 32, :, :]
                pool.affine_select(out=of, in_=of, compare_op=ALU.is_ge, fill=0.0, base=0, pattern=[[-4, 4], [0, T]], channel_multiplier=1).then_inc(pick_ready, 1)
                pool.wait_ge(pick_ready, at // 16 + 1)
                pool.affine_select(out=of, in_=of, compare_op=ALU.is_ge, fill=0.0, base=3, pattern=[[4, 4], [0, T]], channel_multiplier=-1).then_inc(pick_ready, 1)
            pool.wait_ge(pick_ready, 8)
            pool.wait_ge(attw3_hi, 2)
            pool.tensor_tensor(attw_l[:, 0:2 * C], raw[:, 0:2 * C], attw_h[:, 0:2 * C].bitcast(F32),
                               ALU.subtract).then_inc(attw_ready, 1)
            pool.tensor_tensor(repeated(attw_l, 0), heads_of(raw_uqT), repeated(attw_h, 0).bitcast(F32),
                               ALU.subtract).then_inc(attw_ready, 1)
            pool.wait_ge(emb_w_in, 16 * 5)
            pool.tensor_tensor(posb[:, :], pos[:, :], rows[:, 2, :], ALU.add).then_inc(posb_ready, 1)
            pool.wait_ge(posb_ready, 1)
            with pool.Fori(0, G // 2) as i:
                for b in range(2):
                    g = 2 * i + b
                    pool.wait_ge(zn_ready, g + 1)
                    pool.wait_ge(emb_ready, LEAD + g - 1)
                    pool.tensor_tensor(zg[b][:, :], zn[b][:, :], rows[:, 1, :], ALU.mult).then_inc(zg_ready, 1)
                    pool.wait_ge(zg_ready, LEAD + g + 1)
                    pool.wait_ge(emb_put[b], LEAD + 32 * i)
                    pool.tensor_tensor(emb[b][:, :], zg[b][:, :], posb[:, :], ALU.add).then_inc(emb_ready, 1)

            def group(g, b, ahead, further):
                for m in range(2):
                    pool.wait_ge(y_done, LEAD + 2 * g + m + 1)
                    settle(pool, pool_past)
                    row = h[:, bass.ds(2 * g + m, 1), :].rearrange("p a c -> p (a c)")
                    pool.tensor_tensor(row, row, y[:, m, :], ALU.add).then_inc(y_added, 1)
                pool.wait_ge(wh_ready, g + 1)
                settle(pool, pool_past)
                pool.tensor_tensor(wl[:, bass.ds(g * EW, EW)], stage[:, :],
                                   wh[:, bass.ds(g * EW, EW)].bitcast(F32), ALU.subtract).then_inc(wl_ready, 1)

            over_groups(pool, group)

            pool.wait_ge(ln3_ready, 1)
            for e in range(NE):
                pool.memset(descend[:, :, e:e + 1], float(NE - e)).then_inc(descend_set, 1)
            with pool.Fori(0, NC) as c:
                for e in range(NE):
                    n = NE * c + e
                    pool.wait_ge(wrow_in[e % 2], 16 * (4 * c + e // 2 + 1))
                    if e >= 2:
                        pool.wait_ge(wu_ready, LEAD + 2 * n - 2)
                    else:
                        pool.wait_ge(wu_ready, LEAD + 2 * NE * c)
                    settle(pool, pool_past)
                    pool.partition_broadcast(wb[e % 2][:, :], wrow[e % 2][0:1, :]).then_inc(wb_ready, 1)
                    for m in range(2):
                        pool.wait_ge(sg_ready, LEAD + 2 * n + m + 1)
                        pool.wait_ge(wu_ready, LEAD + 2 * n + m + 1)
                        if e >= 1:
                            pool.wait_ge(hl_ready, LEAD + 2 * n + m - 1)
                        else:
                            pool.wait_ge(hl_ready, LEAD + 2 * n)
                        pool.tensor_tensor(hf[m][:, :], sg[m][:, :], wu[m][:, :], ALU.mult).then_inc(hf_ready, 1)

        @block.scalar
        def _(act):
            def norm(dst, src, at):
                w = src.shape[0]
                at = bass.ds(at, 1)
                return act.activation(dst, src[:, at, :].rearrange("p a c -> p (a c)"), ACT.Identity,
                                      scale=rstd[0:w, at], bias=offset[0:w, at])

            act.wait_ge(attw_in, 16)
            act.copy(attw_h[:, 0:2 * C], raw[:, 0:2 * C]).then_inc(attw3_hi, 1)
            act.copy(repeated(attw_h, 0), heads_of(raw_uqT)).then_inc(attw3_hi, 1)
            act.wait_ge(aT_ps, 1)
            act.mul(aT[:, :, :].rearrange("p k n -> p (k n)"), ring[0][:, 0:512], HS ** -0.5).then_inc(aT_ready, 1)
            act.wait_ge(kv_ps, 1)
            act.copy(repeated(attw_h, 1), heads_of(ring[0][:, 512:512 + C])).then_inc(attw_hi, 1)
            act.copy(veff(attw_h), ring[0][:, 512 + C:1024]).then_inc(attw_hi, 1)

            for half in range(2):
                act.wait_ge(ln1_ready, half + 1)
                for b in range(4):
                    act.wait_ge(pnT_ps, LEAD + 4 * half + b - 3)
                    norm(pn[b][:, :], praw, 4 * half + b).then_inc(pn_ready, 1)
            def embeddings_normalised(half):
                act.wait_ge(ln2_ready, half + 1)
                for g in range(4 * half, 4 * half + 4):
                    act.wait_ge(zg_ready, LEAD + g - 1)
                    act.activation(zn[g % 2][:, :], z[:, g, :], ACT.Identity, scale=rstd[0:GP, NI + g:NI + g + 1],
                                   bias=offset[0:GP, NI + g:NI + g + 1]).then_inc(zn_ready, 1)

            embeddings_normalised(0)
            act.wait_ge(wr_in, 32)
            act.wait_ge(wr_cleared, 2)
            act.copy(wrh[:, :, 0:NE], wr_raw[:, :, :]).then_inc(wrh_ready, 1)
            act.wait_ge(ln_ready, 1)
            act.wait_ge(pnT_ps, LEAD + G)
            act.wait_ge(emb_ps, LEAD + G)

            def normalised(g):
                act.wait_ge(xt_ps, LEAD + g)
                settle(act, act_past)
                for m in range(2):
                    norm(xn[:, m, :], h, 2 * g + m).then_inc(xn_ready, 1)

            def high_x(g):
                act.wait_ge(xt_ps, LEAD + g + 1)
                act.wait_ge(cd_ps, LEAD + g)
                act.copy(xh[:, :, :], trans[:, 0:2 * TG].rearrange("p (k t) -> p k t", k=KT)).then_inc(xh_ready, 1)

            def high_latents(g):
                act.wait_ge(cd_ps, LEAD + g + 1)
                act.wait_ge(v_ps, LEAD + g)
                act.copy(cdh[:, :, :], proj_a[:, 0:2 * TG].rearrange("p (k t) -> p k t", k=2)).then_inc(cdh_ready, 1)

            def high_qk(g, b, s):
                act.wait_ge(qk_ps, 8 * g + s + 1)
                if s == 0:
                    act.wait_ge(st_ps, LEAD + 4 * (g - 1))
                act.copy(stacked(b, s), proj_bank(s)[:, 0:2 * TG].rearrange("p (k t) -> p k t", k=2)).then_inc(qkh_ready, 1)

            def values_out(g, b):
                act.wait_ge(v_ps, LEAD + g + 1)
                act.wait_ge(pv_done, LEAD + 4 * (g - 1))
                act.copy(vals[b][:, :, :, 0:HS],
                         proj_b[0:T, 0:2 * C].rearrange("p (m h d) -> p m h d", m=2, h=NH)).then_inc(v_ready, 1)

            def high_maxima(g):
                act.wait_ge(m_ps, LEAD + g + 1)
                act.wait_ge(mdiag_ready, LEAD + g)
                act.copy(mrow[:, :], trans[:, 0:T]).then_inc(mh_ready, 1)

            def exponentials(g, u):
                act.wait_ge(st_ps, LEAD + 4 * g + u + 1)
                act.wait_ge(pv_done, LEAD + 4 * g + u - 1)
                act.activation(probs[u % 2][:, :, :, :].rearrange("k a j q -> k a (j q)"),
                               ring[u % 2][0:T, :].rearrange("p (a x) -> p a x", a=2)[:, :, 0:4 * T],
                               ACT.Exp).then_inc(exp_done, 1)

            def group(g, b, ahead, further):
                if ahead:
                    for s in range(1, 5):
                        high_qk(g + 1, 1 - b, s)
                high_maxima(g)
                if ahead:
                    high_qk(g + 1, 1 - b, 5)
                exponentials(g, 0)
                if ahead:
                    high_qk(g + 1, 1 - b, 6)
                exponentials(g, 1)
                if further:
                    normalised(g + 2)
                if ahead:
                    high_qk(g + 1, 1 - b, 7)
                exponentials(g, 2)
                if ahead:
                    values_out(g + 1, 1 - b)
                if further:
                    high_x(g + 2)
                exponentials(g, 3)
                if further:
                    high_latents(g + 2)
                    high_qk(g + 2, b, 0)
                act.wait_ge(stage_in, 16 * (g + 1))
                settle(act, act_past)
                act.copy(wh[:, bass.ds(g * EW, EW)], stage[:, :]).then_inc(wh_ready, 1)

            normalised(0)
            high_x(0)
            embeddings_normalised(1)
            high_latents(0)
            normalised(1)
            for s in range(8):
                high_qk(0, 0, s)
            values_out(0, 0)
            high_x(1)
            high_latents(1)
            act.wait_ge(ln_ready, 2)
            high_qk(1, 1, 0)
            over_groups(act, group)

            act.wait_ge(ln3_ready, 1)

            def x2_norm(g, b):
                act.wait_ge(x2t_ps, LEAD + g - 1)
                settle(act, act_past)
                norm(x2n[b][:, 0, :], h, 2 * g).then_inc(x2n_ready[0], 1)

            def x2_high(g, b):
                act.wait_ge(x2t_ps, LEAD + g + 1)
                settle(act, act_past)
                act.copy(x2h[:, :, bass.ds(g * TG, TG)],
                         (trans, proj_a)[b][:, 0:2 * TG].rearrange("p (k t) -> p k t", k=KT)).then_inc(x2h_ready, 1)

            def logits_out(c):
                act.wait_ge(lgT_ps, c + 1)
                act.wait_ge(lg_ps, LEAD + c)
                act.copy(lgT[:, :], proj_b[0:NE, 0:TC]).then_inc(lgT_ready, 1)

            def inhibition_exp(r):
                act.wait_ge(lg_ready, r + 1)
                at = ROUTED_ROWS[r]
                act.activation(rt[:, 1, at], rt[:, 0, at], ACT.Exp, scale=-1.0).then_inc(route_exp, 1)

            def distance_exps(r):
                act.wait_ge(dist_ready, r + 1)
                at = ROUTED_ROWS[r]
                act.activation(rt[:, 4, at], rt[:, 3, at], ACT.Exp, scale=-1.0 / 0.1).then_inc(route_exp, 1)
                act.activation(rt[:, 5, at], rt[:, 3, at], ACT.Exp, scale=-1.0 / 0.3).then_inc(route_exp, 1)

            def weights_transposed(r):
                act.wait_ge(wT_ps, r + 1)
                n = ROUTED_ROWS[r].stop - ROUTED_ROWS[r].start
                act.copy(wT[0:n, r, :], psY[0:n, 256:256 + T]).then_inc(wT_ready, 1)

            def gate(c, e):
                n = NE * c + e
                act.wait_ge(hf_ready, LEAD + 2 * n)
                for m in range(2):
                    act.wait_ge(gu_ps, 2 * n + m + 1)
                    act.activation(sg[m][:, :], ring[m][:, 0:TC], ACT.Silu).then_inc(sg_ready, 1)

            def hidden_high(c, e):
                n = NE * c + e
                act.wait_ge(down_done, LEAD + n - 1)
                for m in range(2):
                    act.wait_ge(hf_ready, LEAD + 2 * n + m + 1)
                    act.copy(hh[e % 2][:, m, :], hf[m][:, :]).then_inc(hh_ready, 1)

            def chunk(c, last):
                first = isinstance(c, int) and c == 0
                for e in range(1, NE):
                    gate(c, e)
                    hidden_high(c, e)
                    if first and e == 1:
                        inhibition_exp(1)
                    if first and e == 2:
                        distance_exps(1)
                    if first and e == 6:
                        weights_transposed(1)
                if not last:
                    gate(c + 1, 0)
                act.wait_ge(down_done, LEAD + NE * c + NE)
                act.wait_ge(o_ps, LEAD + c)
                act.copy(oT[:, 0, :], trans[:, 0:TC]).then_inc(oT_ready0, 1)
                if not last:
                    hidden_high(c + 1, 0)

            x2_norm(0, 0)
            x2_norm(1, 1)
            for g in range(4):
                x2_high(g, g % 2)
                x2_norm(g + 2, g % 2)
            logits_out(0)
            inhibition_exp(0)
            distance_exps(0)
            x2_high(4, 0)
            x2_high(5, 1)
            x2_norm(6, 0)
            act.wait_ge(ln3_ready, 2)
            x2_norm(7, 1)
            weights_transposed(0)
            gate(0, 0)
            x2_high(6, 0)
            x2_high(7, 1)
            logits_out(1)
            hidden_high(0, 0)
            for c in range(2, NC):
                logits_out(c)
            chunk(0, False)
            with act.Fori(1, NC - 1) as c:
                chunk(c, False)
            chunk(NC - 1, True)

        @block.vector
        def _(dve):
            step = Steps(dve, dve_step)

            def moments(images, src, width, parts):
                for j, at in enumerate(images):
                    for q in range(parts):
                        step(dve.bn_stats(stats[0:width, j, 6 * q:6 * q + 6], src(j, q)))
                step.join()
                for j, at in enumerate(images):
                    step(dve.bn_aggr(mv[0:width, at, :], stats[0:width, j, 0:6 * parts]))

            def rsqrt(width, first, n):
                at = slice(first, first + n)
                v, yy, t = nt[0:width, 0, at], rstd[0:width, at], nt[0:width, 1, at]
                step.join()
                step.then(dve.tensor_scalar(v, mv[0:width, at, 1:2].rearrange("p a c -> p (a c)"), EPS, None, ALU.add))
                step.then(dve.tensor_scalar(yy.bitcast(I32), v.bitcast(I32), -0.5, RSQRT_SEED, ALU.mult, ALU.add))
                for _ in range(3):
                    step.then(dve.tensor_tensor(t, yy, yy, ALU.mult))
                    step.then(dve.scalar_tensor_tensor(t, t, -0.5, v, ALU.mult, ALU.mult))
                    step.then(dve.scalar_tensor_tensor(yy, t, 1.5, yy, ALU.add, ALU.mult))
                step.then(dve.scalar_tensor_tensor(offset[0:width, at], mv[0:width, at, 0:1].rearrange("p a c -> p (a c)"),
                                                   -1.0, yy, ALU.mult, ALU.mult))

            def token_moments(first, n):
                for i in range(first, first + n, 4):
                    step.join()
                    moments(range(i, i + 4), lambda j, q: h[:, i + j, :], T, 1)

            for i in range(2):
                dve.wait_ge(patch_in[i], 16)
                if i:
                    step.join()
                moments(range(4 * i, 4 * i + 4),
                        lambda j, q: praw[:, 4 * i + j, q * (PD // 2):(q + 1) * (PD // 2)], GP, 2)
                rsqrt(GP, 4 * i, 4)
                dve.sem_inc(ln1_ready, 1)
            dve.wait_ge(emb_w_in, 16 * 5)
            def patch_affine(g, b):
                dve.wait_ge(pnT_ps, LEAD + g + 1)
                dve.wait_ge(emb_ps, LEAD + g - 1)
                dve.tensor_tensor(zs[b][:, :, :], (trans, proj_a)[b][:, 0:PT * GP].rearrange("p (k t) -> p k t", k=PT),
                                  column[:, 0:PT].unsqueeze(2).to_broadcast([128, PT, GP]), ALU.mult).then_inc(zs_ready, 1)
                dve.wait_ge(zs_ready, LEAD + g + 1)
                dve.tensor_tensor(zT[b][:, :, :], zs[b][:, :, :],
                                  column[:, PT:2 * PT].unsqueeze(2).to_broadcast([128, PT, GP]), ALU.add).then_inc(zT_ready, 1)

            def embedded(g, b):
                dve.wait_ge(emb_ps, LEAD + g + 1)
                at = span(g)
                dve.tensor_tensor(z[:, at, :].rearrange("p a c -> p (a c)"), (proj_b, psY)[b][0:GP, 0:C], rows[:, 0, :],
                                  ALU.add).then_inc(z_ready, 1)

            def attention_weights_low():
                dve.wait_ge(attw_hi, 2)
                dve.tensor_tensor(repeated(attw_l, 1), heads_of(ring[0][:, 512:512 + C]), repeated(attw_h, 1).bitcast(F32),
                                  ALU.subtract).then_inc(attw_ready, 1)
                dve.tensor_tensor(veff(attw_l), ring[0][:, 512 + C:1024], veff(attw_h).bitcast(F32),
                                  ALU.subtract).then_inc(attw_ready, 1)
                dve.wait_ge(cls_in, 16)
                dve.tensor_tensor(cls[0:1, 2, :], cls[0:1, 0, :], cls[0:1, 1, :], ALU.add).then_inc(cls_made, 1)

            def second_norm(half):
                dve.wait_ge(z_ready, LEAD + 4 * half + 4)
                step.join()
                moments(range(NI + 4 * half, NI + 4 * half + 4), lambda j, q: z[:, 4 * half + j, :], GP, 1)
                rsqrt(GP, NI + 4 * half, 4)
                dve.sem_inc(ln2_ready, 1)

            for half in range(2):
                patch_affine(4 * half, 0)
                for g in range(4 * half + 1, 4 * half + 4):
                    patch_affine(g, g % 2)
                    if g == 1:
                        attention_weights_low()
                    if g == 5:
                        second_norm(0)
                    embedded(g - 1, (g - 1) % 2)
                if half == 0:
                    embedded(3, 1)
            dve.wait_ge(text_in, 32)
            dve.wait_ge(cls_put, 16)
            dve.wait_ge(pn_ready, G)
            for b in range(2):
                dve.wait_ge(emb_put[b], LEAD + 32)
            token_moments(0, 4)
            rsqrt(T, 0, 4)
            dve.sem_inc(ln_ready, 1)
            embedded(G - 1, 1)
            second_norm(1)
            dve.wait_ge(emb_ps, LEAD + G)
            def low_x(g):
                dve.wait_ge(xh_ready, g + 1)
                dve.tensor_tensor(xl[:, :, :], trans[:, 0:2 * TG].rearrange("p (k t) -> p k t", k=KT),
                                  xh[:, :, :].bitcast(F32), ALU.subtract).then_inc(xl_ready, 1)

            def low_latents(g):
                dve.wait_ge(cdh_ready, g + 1)
                dve.tensor_tensor(cdl[:, :, :], proj_a[:, 0:2 * TG].rearrange("p (k t) -> p k t", k=2),
                                  cdh[:, :, :].bitcast(F32), ALU.subtract).then_inc(cdl_ready, 1)

            def low_qk(g, b, s):
                dve.wait_ge(qkh_ready, 8 * g + s + 1)
                at = 2 * PT + s // 4
                dve.scalar_tensor_tensor(stacked(b, s), stacked(b, s).bitcast(F32), column[:, at:at + 1],
                                         proj_bank(s)[:, 0:2 * TG].rearrange("p (k t) -> p k t", k=2),
                                         ALU.mult, ALU.add).then_inc(qkl_ready, 1)

            def maximum(g, u):
                m, half = u // 2, u % 2
                if u == 0:
                    dve.wait_ge(m_ps, LEAD + g)
                dve.wait_ge(s_ps, 4 * g + u + 1)
                dve.tensor_reduce(
                    mx[:, :].rearrange("p (a x) -> p a x", a=2)[:, :, NPAIR * m + 4 * half:NPAIR * m + 4 * half + 4],
                    ring[u % 2][0:T, :].rearrange("p (a x) -> p a x", a=2)[:, :, 0:4 * T]
                    .rearrange("p a (j k) -> p a j k", j=4), AX.X, ALU.max).then_inc(max_done, 1)

            def low_maxima(g):
                dve.wait_ge(mh_ready, g + 1)
                for at in (0, 64):
                    dve.tensor_tensor(mrow[at + 32:at + 64, :], trans[at:at + 32, 0:T],
                                      mrow[at:at + 32, :].bitcast(F32), ALU.subtract).then_inc(ml_ready, 1)
                dve.wait_ge(ml_ready, LEAD + 2 * g + 2)
                dve.wait_ge(st_ps, LEAD + 4 * g)
                dve.tensor_tensor(mdiag[:, :, :], mrow[:, :].bitcast(F32).unsqueeze(1).to_broadcast([128, 4, T]),
                                  column[:, 2 * PT + 2:2 * PT + 6].unsqueeze(2).to_broadcast([128, 4, T]),
                                  ALU.mult).then_inc(mdiag_ready, 1)

            def divide(g, m):
                dve.wait_ge(pv_done, LEAD + 4 * g + 2 * m + 2)
                heads = psY[0:T, 0:NH * (HS + 1)].rearrange("p (h d) -> p h d", h=NH)
                dve.reciprocal(rden[:, m, :], heads[:, :, HS:HS + 1].rearrange("p h d -> p (h d)")).then_inc(rden_ready, 1)
                dve.wait_ge(rden_ready, 2 * g + m + 1)
                dve.wait_ge(y_added, LEAD + 2 * g + m - 1)
                dve.tensor_tensor(y[:, m, :].rearrange("p (h d) -> p h d", h=NH), heads[:, :, 0:HS],
                                  rden[:, m, :].unsqueeze(2).to_broadcast([T, NH, HS]), ALU.mult).then_inc(y_done, 1)

            def third_moments(n):
                at = span(n)
                dve.wait_ge(y_added, LEAD + n + 1)
                dve.bn_stats(stats3[:, at, :].rearrange("p a c -> p (a c)"),
                             h[:, at, :].rearrange("p a c -> p (a c)")).then_inc(stat3_ready, 1)

            def group(g, b, ahead, further):
                for u in range(1, 4):
                    maximum(g, u)
                    if ahead:
                        low_qk(g + 1, 1 - b, u)
                low_maxima(g)
                if ahead:
                    for s in range(4, 8):
                        low_qk(g + 1, 1 - b, s)
                divide(g, 0)
                if further:
                    low_x(g + 2)
                    low_latents(g + 2)
                third_moments(2 * g)
                if ahead:
                    maximum(g + 1, 0)
                if further:
                    low_qk(g + 2, b, 0)
                if not ahead:
                    for n in range(1, NI - 2, 2):
                        third_moments(n)
                    dve.wait_ge(stat3_ready, NI - 1)
                    for n in range(NI - 2):
                        step(dve.bn_aggr(mv[0:T, n, :], stats3[:, n, :]))
                    dve.wait_ge(xn_ready, NI)
                    rsqrt(T, 0, NI - 2)
                divide(g, 1)

            low_x(0)
            low_latents(0)
            for s in range(8):
                low_qk(0, 0, s)
                if s == 1:
                    for b in range(2):
                        dve.wait_ge(emb_put[b], LEAD + 128)
                if s in (1, 3, 5):
                    token_moments(4 + 2 * (s - 1), 4)
            low_x(1)
            rsqrt(T, 4, 12)
            dve.sem_inc(ln_ready, 1)
            low_latents(1)
            dve.wait_ge(wr_cleared, 2)
            dve.wait_ge(wrh_ready, 1)
            dve.tensor_tensor(wrl[:, :, 0:NE], wr_raw[:, :, :], wrh[:, :, 0:NE].bitcast(F32), ALU.subtract).then_inc(wr_ready, 1)
            step.then(dve.reciprocal(temp[:, 1:2], temp[:, 0:1]))
            for b in range(2):
                dve.memset(vals[b][:, :, :, HS:HS + 1], 1.0).then_inc(tiles_set, 1)
            dve.memset(mx[:, :], 0.0).then_inc(tiles_set, 1)
            dve.wait_ge(tiles_set, 3)
            maximum(0, 0)
            low_qk(1, 1, 0)
            over_groups(dve, group)

            dve.wait_ge(y_added, LEAD + NI)
            dve.sem_inc(ln3_ready, 1)

            def x2_norm(g, b):
                at = bass.ds(2 * g + 1, 1)
                dve.wait_ge(x2t_ps, LEAD + g - 1)
                dve.tensor_scalar(x2n[b][:, 1, :], h[:, at, :].rearrange("p a c -> p (a c)"), rstd[0:T, at], offset[0:T, at],
                                  ALU.mult, ALU.add).then_inc(x2n_ready[1], 1)

            def x2_low(g, b):
                dve.wait_ge(x2h_ready, g + 1)
                at = bass.ds(g * TG, TG)
                dve.tensor_tensor(x2l[:, :, at], (trans, proj_a)[b][:, 0:2 * TG].rearrange("p (k t) -> p k t", k=KT),
                                  x2h[:, :, at].bitcast(F32), ALU.subtract).then_inc(x2l_ready, 1)


            def grid(r, k):
                return rt[:, k, ROUTED_ROWS[r]]

            def by_image(r, k):
                return grid(r, k).rearrange("p (i e) -> p i e", e=NE)

            def of_image(r, k):
                return rs[:, k, ROUTED[r]]

            def spread(r, k):
                n = ROUTED[r].stop - ROUTED[r].start
                return of_image(r, k).unsqueeze(2).to_broadcast([T, n, NE])

            def logits(r):
                dve.wait_ge(lg_ps, LEAD + (1, NC)[r])
                dve.tensor_scalar(grid(r, 0), psY[0:T, ROUTED_ROWS[r]], temp[0:T, 1:2], None, ALU.mult).then_inc(lg_ready, 1)

            def distances(r):
                dve.wait_ge(route_exp, 3 * r + 1)
                step.then(dve.tensor_scalar(grid(r, 1), grid(r, 1), 1.0, None, ALU.add))
                step.then(dve.reciprocal(grid(r, 2), grid(r, 1)))
                step.then(dve.tensor_scalar(grid(r, 7), grid(r, 2), -GOLDEN_CENTER, None, ALU.add))
                dve.scalar_tensor_tensor(grid(r, 3), grid(r, 7), -1.0, grid(r, 7), ALU.mult, ALU.max).then_inc(dist_ready, 1)
                step.then(dve.tensor_scalar(grid(r, 6), grid(r, 2), GOLDEN_LOWER, None, ALU.is_ge))
                step.then(dve.scalar_tensor_tensor(grid(r, 6), grid(r, 2), GOLDEN_UPPER, grid(r, 6), ALU.is_le, ALU.mult))

            def in_zone(r):
                dve.wait_ge(route_exp, 3 * r + 3)
                step.then(dve.tensor_tensor(grid(r, 4), grid(r, 4), grid(r, 6), ALU.mult))
                step.then(dve.tensor_reduce(of_image(r, 0), by_image(r, 4), AX.X, ALU.add))
                step(dve.tensor_scalar(of_image(r, 1), of_image(r, 0), 1e-8, None, ALU.is_lt))
                step(dve.tensor_scalar(of_image(r, 2), of_image(r, 0), 1e-8, None, ALU.is_ge))
                dve.wait_ge(dist_ready, r + 1)
                step.then(dve.tensor_copy(grid(r, 7), grid(r, 5)))

            def largest(r, k):
                step.then(dve.tensor_reduce(of_image(r, 3), by_image(r, 7), AX.X, ALU.max))
                step.then(dve.tensor_tensor(by_image(r, k), by_image(r, 7), spread(r, 3), ALU.is_equal))
                step.then(dve.tensor_tensor(by_image(r, k), by_image(r, k), descend[:, ROUTED[r], :], ALU.mult))
                step.then(dve.tensor_reduce(of_image(r, 3), by_image(r, k), AX.X, ALU.max))
                step.then(dve.tensor_tensor(by_image(r, k), by_image(r, k), spread(r, 3), ALU.is_equal))
                step.then(dve.scalar_tensor_tensor(grid(r, 7), grid(r, k), -4.0, grid(r, 7), ALU.mult, ALU.add))

            def normalise(r, k):
                step.then(dve.tensor_reduce(of_image(r, 3), by_image(r, k), AX.X, ALU.add))
                step.then(dve.tensor_scalar(of_image(r, 3), of_image(r, 3), 1e-8, None, ALU.max))
                step.then(dve.reciprocal(of_image(r, 3), of_image(r, 3)))
                return dve.tensor_tensor(by_image(r, k), by_image(r, k), spread(r, 3), ALU.mult)

            def combined(r):
                step.then(dve.tensor_tensor(grid(r, 8), grid(r, 8), grid(r, 9), ALU.add))
                step.then(dve.tensor_tensor(grid(r, 5), grid(r, 5), grid(r, 8), ALU.mult))
                step.then(normalise(r, 5))
                step.then(dve.tensor_tensor(by_image(r, 5), by_image(r, 5), spread(r, 1), ALU.mult))
                step.then(dve.tensor_tensor(by_image(r, 4), by_image(r, 4), spread(r, 2), ALU.mult))
                step.then(dve.tensor_tensor(grid(r, 4), grid(r, 4), grid(r, 5), ALU.add))
                normalise(r, 4).then_inc(route_done, 1)

            x2_norm(0, 0)
            x2_norm(1, 1)
            for g in range(4):
                x2_low(g, g % 2)
                x2_norm(g + 2, g % 2)
                if g == 1:
                    third_moments(NI - 1)
                    dve.wait_ge(stat3_ready, NI)
                    for n in (NI - 2, NI - 1):
                        step(dve.bn_aggr(mv[0:T, n, :], stats3[:, n, :]))
                    rsqrt(T, NI - 2, 2)
                    dve.sem_inc(ln3_ready, 1)
            dve.wait_ge(descend_set, NE)
            logits(0)
            distances(0)
            in_zone(0)
            largest(0, 8)
            largest(0, 9)
            combined(0)
            x2_low(4, 0)
            x2_norm(6, 0)
            x2_low(5, 1)
            x2_norm(7, 1)
            x2_low(6, 0)
            x2_low(7, 1)

            def weighted_up(c, e):
                n = NE * c + e
                dve.wait_ge(wb_ready, LEAD + n + 1)
                for m in range(2):
                    dve.wait_ge(gu_ps, 2 * n + m + 1)
                    dve.wait_ge(hf_ready, LEAD + 2 * n + m - 1)
                    dve.tensor_tensor(wu[m][:, :], ring[m][:, 512:512 + TC], wb[e % 2][:, :], ALU.mult).then_inc(wu_ready, 1)

            def hidden_low(c, e):
                n = NE * c + e
                dve.wait_ge(down_done, LEAD + n - 1)
                for m in range(2):
                    dve.wait_ge(hh_ready, 2 * n + m + 1)
                    dve.tensor_tensor(hl[e % 2][:, m, :], hf[m][:, :], hh[e % 2][:, m, :].bitcast(F32),
                                      ALU.subtract).then_inc(hl_ready, 1)

            def chunk(c, last):
                first = isinstance(c, int) and c == 0
                for e in range(1, NE):
                    weighted_up(c, e)
                    hidden_low(c, e)
                    if first and e == 1:
                        logits(1)
                    if first and e == 2:
                        distances(1)
                    if first and e == 3:
                        in_zone(1)
                        largest(1, 8)
                    if first and e == 4:
                        largest(1, 9)
                    if first and e == 5:
                        combined(1)
                if not last:
                    weighted_up(c + 1, 0)
                dve.wait_ge(down_done, LEAD + NE * c + NE)
                dve.wait_ge(o_ps, LEAD + c)
                dve.tensor_copy(oT[:, 1, :], proj_a[:, 0:TC]).then_inc(oT_ready1, 1)
                if not last:
                    hidden_low(c + 1, 0)
                dve.wait_ge(o_ps, LEAD + c + 1)
                dve.wait_ge(out_sent, LEAD + 16 * c)
                for half, ps in enumerate((proj_b, psY)):
                    dve.tensor_tensor(res[:, 2 * half:2 * half + 2, :],
                                      h[:, span(4 * c + 2 * half, 2), :],
                                      ps[0:T, :].rearrange("p (i n) -> p i n", i=2), ALU.add).then_inc(res_ready, 1)

            weighted_up(0, 0)
            hidden_low(0, 0)
            chunk(0, False)
            with dve.Fori(1, NC - 1) as c:
                chunk(c, False)
            chunk(NC - 1, True)

        @block.tensor
        def _(pe):
            pe.wait_ge(attw_in, 16)
            for m in range(KT):
                last = pe.matmul(ring[0][:, m * C:(m + 1) * C], raw_uqT[:, m * 128:(m + 1) * 128],
                                 raw_dq, start=True, stop=True)
            last.then_inc(aT_ps, 1)
            pe.wait_ge(aT_ready, 1)
            for at, w, x in ((512, raw_uk, aT[:, :, :].rearrange("p k n -> p (k n)")), (512 + C, raw_uv, raw_o)):
                for k in range(KT):
                    last = pe.matmul(ring[0][:, at:at + C], w[:, k * L:(k + 1) * L], x[:, k * C:(k + 1) * C], start=(k == 0), stop=(k == KT - 1))
            last.then_inc(kv_ps, 1)

            pe.wait_ge(ident_ready, 4)
            pe.wait_ge(emb_w_in, 16 * 5)

            def patch_transposes(g, k):
                pe.wait_ge(pn_ready, g + 1)
                pe.wait_ge(zs_ready, LEAD + g - 1)
                for n in range(PT):
                    last = pe.transpose((trans, proj_a)[k % 2][:, n * GP:(n + 1) * GP], pn[k][:, n * 128:(n + 1) * 128],
                                        ident[0:GP, 0:GP])
                last.then_inc(pnT_ps, 1)

            def embed(g, k):
                pe.wait_ge(zT_ready, g + 1)
                pe.wait_ge(z_ready, LEAD + g - 1)
                for n in range(PT):
                    last = pe.matmul((proj_b, psY)[k % 2][0:GP, 0:C], zT[k % 2][:, n, :], wproj[:, n, :],
                                     start=(n == 0), stop=(n == PT - 1))
                last.then_inc(emb_ps, 1)

            with pe.Fori(0, 2) as i:
                patch_transposes(4 * i, 0)
                for k in range(1, 4):
                    patch_transposes(4 * i + k, k)
                    embed(4 * i + k - 1, k - 1)
                embed(4 * i + 3, 3)

            pe.wait_ge(attw_ready, 4)
            pe.wait_ge(z_ready, LEAD + G)
            pe.wait_ge(pick_ready, 8)

            def tokens_transposed(g):
                pe.wait_ge(xn_ready, 2 * g + 2)
                pe.wait_ge(ml_ready, LEAD + 2 * (g - 1))
                for m in range(2):
                    for k in range(KT):
                        last = pe.transpose(trans[:, k * TG + m * T:k * TG + (m + 1) * T],
                                            xn[:, m, k * 128:(k + 1) * 128], ident[0:T, 0:T])
                last.then_inc(xt_ps, 1)

            def latents(g, j):
                if j == 0:
                    pe.wait_ge(xh_ready, g + 1)
                    pe.wait_ge(xl_ready, g + 1)
                    pe.wait_ge(qkl_ready, LEAD + 8 * g)
                w = (dkv, dq)[j]
                for k in range(KT):
                    last = three_pass(pe, proj_a[:, j * TG:(j + 1) * TG], w(attw_h, k), w(attw_l, k),
                                      xh[:, k, :], xl[:, k, :], k == 0, k == KT - 1)
                if j == 1:
                    last.then_inc(cd_ps, 1)

            def project_qk(g, s):
                if s == 0:
                    pe.wait_ge(cdh_ready, g + 1)
                    pe.wait_ge(cdl_ready, g + 1)
                    pe.wait_ge(v_ready, LEAD + g)
                elif s >= 2:
                    pe.wait_ge(qkl_ready, LEAD + 8 * g + s - 1)
                which = s // 4
                for k in range(2):
                    w = (attw_h, attw_l)
                    last = three_pass(pe, proj_bank(s)[:, k * TG:(k + 1) * TG],
                                      *(pair_w(x, which, 2 * (s % 4) + k) for x in w),
                                      cdh[:, 1 - which, :], cdl[:, 1 - which, :], True, True)
                last.then_inc(qk_ps, 1)

            def project_v(g):
                pe.wait_ge(qkl_ready, LEAD + 8 * g + 7)
                for m in range(2):
                    ch, cl = cdh[:, 0, m * T:(m + 1) * T], cdl[:, 0, m * T:(m + 1) * T]
                    o = proj_b[0:T, m * C:(m + 1) * C]
                    pe.matmul(o, ch, veff(attw_h), start=True, stop=False)
                    pe.matmul(o, ch, veff(attw_l), start=False, stop=False)
                    last = pe.matmul(o, cl, veff(attw_h), start=False, stop=True)
                last.then_inc(v_ps, 1)

            def score(g, b, u, q_first):
                m, half = u // 2, u % 2
                for par in range(2):
                    pe.matmul(ring[u % 2][0:T, par * 512:par * 512 + 4 * T], ident_b[0:T, 0:T],
                              (causal if q_first else causal_t)[:, :].unsqueeze(1).to_broadcast([T, 4, T]),
                              start=True, stop=False, skip_group_check=True)
                for j in range(4):
                    for par in range(2):
                        pair = 4 * half + j
                        q, k = (stacks[b][64 * par:64 * par + 64, s, pair, m * T:(m + 1) * T] for s in range(2))
                        o = ring[u % 2][0:T, par * 512 + j * T:par * 512 + (j + 1) * T]
                        w, x = (q, k) if q_first else (k, q)
                        last = pe.matmul(o, w, x, start=False, stop=(q_first and j == 3), skip_group_check=True)
                if not q_first:
                    if u == 0:
                        pe.wait_ge(mdiag_ready, LEAD + g + 1)
                    for par in range(2):
                        last = pe.matmul(ring[u % 2][0:T, par * 512:par * 512 + 4 * T], pick[64 * par:64 * par + 64, u, :],
                                         mdiag[64 * par:64 * par + 64, :, :].rearrange("p j t -> p (j t)"),
                                         start=False, stop=True, skip_group_check=True)
                return last

            def scores(g, b, u):
                if u == 0:
                    pe.wait_ge(qkl_ready, LEAD + 8 * g + 8)
                if u < 2:
                    pe.wait_ge(exp_done, LEAD + 4 * g + u - 1)
                else:
                    pe.wait_ge(max_done, 4 * g + u - 1)
                score(g, b, u, True).then_inc(s_ps, 1)

            def maxima_transposed(g, ahead):
                pe.wait_ge(max_done, 4 * g + 4)
                if ahead:
                    pe.wait_ge(xl_ready, g + 2)
                pe.transpose(trans[:, 0:T], mx[:, :], ident[0:T, 0:T]).then_inc(m_ps, 1)

            def transposed_scores(g, b, u):
                if u >= 2:
                    pe.wait_ge(exp_done, LEAD + 4 * g + u - 1)
                score(g, b, u, False).then_inc(st_ps, 1)

            def weighted(g, b, u, part):
                m, half = u // 2, u % 2
                if part == 0:
                    pe.wait_ge(tiles_set, 3)
                    pe.wait_ge(exp_done, LEAD + 4 * g + u + 1)
                    if u == 0:
                        pe.wait_ge(v_ready, LEAD + g + 1)
                    if half == 0:
                        pe.wait_ge(y_done, LEAD + 2 * g + m)
                for j in range(2 * part, 2 * part + 2):
                    for par in range(2):
                        head = 2 * (4 * half + j) + par
                        last = pe.matmul(psY[0:T, head * (HS + 1):(head + 1) * (HS + 1)], probs[u % 2][:, par, j, :],
                                         vals[b][:, m, head, :], start=True, stop=True)
                if part == 1:
                    last.then_inc(pv_done, 1)

            def group(g, b, ahead, further):
                for u in range(1, 4):
                    scores(g, b, u)
                    if ahead:
                        project_qk(g + 1, u)
                if ahead:
                    project_qk(g + 1, 4)
                maxima_transposed(g, ahead)
                if ahead:
                    project_qk(g + 1, 5)
                transposed_scores(g, b, 0)
                if ahead:
                    project_qk(g + 1, 6)
                transposed_scores(g, b, 1)
                weighted(g, b, 0, 0)
                if ahead:
                    project_qk(g + 1, 7)
                weighted(g, b, 0, 1)
                transposed_scores(g, b, 2)
                weighted(g, b, 1, 0)
                if ahead:
                    project_v(g + 1)
                weighted(g, b, 1, 1)
                if further:
                    tokens_transposed(g + 2)
                transposed_scores(g, b, 3)
                weighted(g, b, 2, 0)
                if further:
                    latents(g + 2, 0)
                weighted(g, b, 2, 1)
                if further:
                    latents(g + 2, 1)
                if ahead:
                    scores(g + 1, 1 - b, 0)
                weighted(g, b, 3, 0)
                if further:
                    project_qk(g + 2, 0)
                weighted(g, b, 3, 1)

            tokens_transposed(0)
            latents(0, 0)
            latents(0, 1)
            for s in range(8):
                project_qk(0, s)
            project_v(0)
            tokens_transposed(1)
            latents(1, 0)
            latents(1, 1)
            scores(0, 0, 0)
            project_qk(1, 0)
            over_groups(pe, group)

            def gate_up(c, e):
                n = NE * c + e
                at = span(c * TC, TC)
                for m in range(2):
                    pe.wait_ge(sg_ready, LEAD + (2 * n + m - 1 if e else 2 * n))
                    pe.wait_ge(wu_ready, LEAD + (2 * n + m - 1 if e else 2 * n))
                    for part in range(2):
                        for k in range(KT):
                            last = three_pass(pe, ring[m][:, part * 512:part * 512 + TC], expert_w(wh, e, part, k, m),
                                              expert_w(wl, e, part, k, m), x2h[:, k, at], x2l[:, k, at],
                                              k == 0, k == KT - 1)
                    last.then_inc(gu_ps, 1)

            def x2_transposed(g, b):
                for m in range(2):
                    pe.wait_ge(x2n_ready[m], g + 1)
                pe.wait_ge(x2l_ready, LEAD + g - 1)
                for m in range(2):
                    for k in range(KT):
                        last = pe.transpose((trans, proj_a)[b][:, k * TG + m * T:k * TG + (m + 1) * T],
                                            x2n[b][:, m, k * 128:(k + 1) * 128], ident[0:T, 0:T])
                last.then_inc(x2t_ps, 1)

            def route(c):
                pe.wait_ge(x2l_ready, LEAD + 2 * c + 2)
                pe.wait_ge(lgT_ready, LEAD + c)
                at = slice(c * TC, (c + 1) * TC)
                for k in range(KT):
                    last = three_pass(pe, proj_b[:, 0:TC], wrh[:, k, :], wrl[:, k, :], x2h[:, k, at], x2l[:, k, at],
                                      k == 0, k == KT - 1)
                last.then_inc(lgT_ps, 1)

            def logits_back(c):
                pe.wait_ge(lgT_ready, LEAD + c + 1)
                for m in range(4):
                    at = (4 * c + m) * NE
                    last = pe.transpose(psY[0:T, at:at + NE], lgT[:, m * T:(m + 1) * T], ident[0:NE, 0:NE])
                last.then_inc(lg_ps, 1)

            def weights_back(r):
                at = ROUTED_ROWS[r]
                pe.wait_ge(route_done, r + 1)
                pe.transpose(psY[0:at.stop - at.start, 256:256 + T], rt[:, 4, at], ident[0:T, 0:T]).then_inc(wT_ps, 1)

            for g in range(4):
                x2_transposed(g, g % 2)
            pe.wait_ge(wr_ready, 1)
            route(0)
            x2_transposed(4, 0)
            logits_back(0)
            x2_transposed(5, 1)
            pe.wait_ge(wh_ready, NE)
            pe.wait_ge(wl_ready, LEAD + NE)
            gate_up(0, 0)
            weights_back(0)
            x2_transposed(6, 0)
            x2_transposed(7, 1)
            route(1)

            def down(c, e):
                n = NE * c + e
                if e == 0:
                    pe.wait_ge(oT_ready0, LEAD + c)
                    pe.wait_ge(oT_ready1, LEAD + c)
                pe.wait_ge(hh_ready, 2 * n + 2)
                pe.wait_ge(hl_ready, LEAD + 2 * n + 2)
                for m in range(2):
                    for k in range(2):
                        last = three_pass(pe, (trans, proj_a)[m][:, 0:TC], expert_w(wh, e, 2, k, m),
                                          expert_w(wl, e, 2, k, m), hh[e % 2][:, k, :], hl[e % 2][:, k, :],
                                          e == 0 and k == 0, e == NE - 1 and k == 1)
                last.then_inc(down_done, 1)

            def chunk(c, last_chunk):
                down(c, 0)
                for e in range(1, NE):
                    if isinstance(c, int) and c == 0 and e == 6:
                        weights_back(1)
                    if e < NE - 1:
                        gate_up(c, e + 1)
                    elif not last_chunk:
                        gate_up(c + 1, 0)
                    down(c, e)
                if not last_chunk:
                    gate_up(c + 1, 1)
                pe.wait_ge(oT_ready0, LEAD + c + 1)
                pe.wait_ge(oT_ready1, LEAD + c + 1)
                pe.wait_ge(res_ready, LEAD + 2 * c)
                for m in range(4):
                    for k in range(2):
                        last = pe.transpose((proj_b, psY)[m // 2][0:T, (m % 2) * C + k * 128:(m % 2) * C + (k + 1) * 128],
                                            oT[:, k, m * T:(m + 1) * T], ident[:, :])
                last.then_inc(o_ps, 1)

            gate_up(0, 1)
            logits_back(1)
            for c in range(2, NC):
                route(c)
                logits_back(c)
            chunk(0, False)
            with pe.Fori(1, NC - 1) as c:
                chunk(c, False)
            chunk(NC - 1, True)


def kernel(x, txt, L0_tok_ln1_g, L0_tok_ln1_b, L0_tok_W_proj, L0_tok_b_proj, L0_tok_ln2_g, L0_tok_ln2_b,
           L0_tok_cls_token, L0_tok_pos_emb, L0_attn_W_dq, L0_attn_W_uq, L0_attn_W_dkv, L0_attn_W_uk,
           L0_attn_W_uv, L0_attn_W_o, L0_ffn_Wg, L0_ffn_Wu, L0_ffn_Wd, L0_ffn_Wr, L0_ffn_temperature):
    import numpy as np
    import concourse.bacc as bacc
    from concourse.bass_utils import run_bass_kernel_spmd

    patches = np.asarray(x).reshape(NI, 3, 6, 16, 6, 16).transpose(0, 2, 4, 3, 5, 1).reshape(G, GP, PD)

    def tiles(w):
        w = np.asarray(w)
        return w.reshape(-1, 128, w.shape[1]).transpose(1, 0, 2).reshape(128, -1)

    dq, uq, dkv, wo = (np.asarray(w) for w in (L0_attn_W_dq, L0_attn_W_uq, L0_attn_W_dkv, L0_attn_W_o))
    copy = np.arange(128) // HS % REP
    low = -np.stack([copy >= 2, copy % 2 == 1], 1).astype(np.float32)
    place = -(np.arange(128)[:, None] % 4 == np.arange(4)).astype(np.float32) * (np.arange(128)[:, None] % 32 < 16)
    place = place.astype(np.float32)
    laid_out = {
        "patches": patches, "txt": txt,
        "by_column": np.concatenate([tiles(np.asarray(v).reshape(PD, 1)) for v in (L0_tok_ln1_g, L0_tok_ln1_b)] + [low, place], 1),
        "W_proj": L0_tok_W_proj,
        "by_row": np.concatenate([np.asarray(v) for v in (L0_tok_b_proj, L0_tok_ln2_g, L0_tok_ln2_b)]),
        "pos_emb": L0_tok_pos_emb,
        "first_token": np.concatenate([np.asarray(L0_tok_cls_token)[0], np.asarray(L0_tok_pos_emb)[0, 0:1]]).reshape(1, 2 * C),
        "attn_weights": np.concatenate([tiles(dkv.T), tiles(dq.T), uq.T, dq, tiles(L0_attn_W_uk), tiles(L0_attn_W_uv), tiles(wo.T)], 1),
        "expert_weights": np.stack([np.concatenate([tiles(np.asarray(w)[e]) for w in (L0_ffn_Wg, L0_ffn_Wu, L0_ffn_Wd)], 1)
                                    for e in range(NE)], 1),
        "Wr": L0_ffn_Wr, "temperature": L0_ffn_temperature,
    }
    nc = bacc.Bacc("TRN2", target_bir_lowering=False, num_devices=1)
    arrays, args = {}, []
    for name, a in laid_out.items():
        a = np.ascontiguousarray(a)
        arrays[f"in_{name}"] = a
        args.append(nc.dram_tensor(f"in_{name}", a.shape, mybir.dt.from_np(a.dtype), kind="ExternalInput").ap())
    out = nc.dram_tensor("out_tokens", (NI, T, C), F32, kind="ExternalOutput").ap()
    build(nc, *args, out)
    ran = run_bass_kernel_spmd(nc, [arrays], core_ids=[0])
    return ran.results[0]["out_tokens"]
```
